# Optimizing a Trainium2 kernel written in Bass

```python
import numpy as np
import jax
import jax.numpy as jnp

def _softmax(x, axis=-1):
    return jax.nn.softmax(x, axis=axis)

def _gelu(x):
    return jax.nn.gelu(x, approximate=True)

def _silu(x):
    return jax.nn.silu(x)

def _sigmoid(x):
    return jax.nn.sigmoid(x)

def _layernorm(x, axis=-1, eps=1e-05):
    m = jnp.mean(x, axis=axis, keepdims=True)
    v = jnp.var(x, axis=axis, keepdims=True)
    return (x - m) / jnp.sqrt(v + eps)

def _scatter_add(tgt, idx, src, axis=0):
    return tgt.at[idx].add(src)

def _segment_sum(src, seg, n):
    return jax.ops.segment_sum(src, seg, n)
kernel_name = 'mk_adj_ffn_d1_adj_r2_4353d7'

def setup_inputs(seed: int=0):
    np.random.seed(seed)
    _w = jnp.asarray

    def _rec_inputs():
        import jax
        import jax.numpy as jnp
        _gk = jax.random.key(seed)
        x = -0.0001538 + 1 * jax.random.normal(jax.random.fold_in(_gk, 1), (128, 64, 384), jnp.float32)
        _a = jax.random.bernoulli(jax.random.fold_in(_gk, 2), 0.125, (128, 64, 64))
        _a = jnp.logical_or(_a, jnp.swapaxes(_a, -1, -2))
        _a = jnp.logical_or(_a, jnp.eye(64, dtype=bool))
        _af = _a.astype(jnp.float32)
        _af = _af * jax.random.uniform(jax.random.fold_in(_gk, 3), (128, 64, 64), jnp.float32, 0.05, 0.999992)
        adj = _af
        return (x, adj)
    x, adj = _rec_inputs()

    def _L0_gnn_setup():
        import jax, jax.numpy as jnp
        import numpy as np
        B, N, D, H = (8, 512, 384, 12)
        HD = D // H

        def _split_heads(x):
            b, n, _ = x.shape
            return x.reshape(b, n, H, HD).transpose(0, 2, 1, 3)
        key = jax.random.key(seed)
        ks = jax.random.split(key, 10)
        input_graph = jax.random.normal(ks[0], (B, N, D), dtype=jnp.float32)
        u = jax.random.uniform(ks[1], (B, N, N), dtype=jnp.float32)
        keep = jax.random.uniform(ks[2], (B, N, N)) < 0.15
        adj = jnp.where(keep, u, 0.0)
        s = 1.0 / np.sqrt(D)
        Wq = jax.random.normal(ks[3], (D, D), dtype=jnp.float32) * s
        bq = jnp.zeros((D,), dtype=jnp.float32)
        Wk = jax.random.normal(ks[4], (D, D), dtype=jnp.float32) * s
        bk = jnp.zeros((D,), dtype=jnp.float32)
        Wv = jax.random.normal(ks[5], (D, D), dtype=jnp.float32) * s
        bv = jnp.zeros((D,), dtype=jnp.float32)
        beta = jnp.asarray(0.1, dtype=jnp.float32)
        return {'input_graph': input_graph, 'adj': adj, 'Wq': Wq, 'bq': bq, 'Wk': Wk, 'bk': bk, 'Wv': Wv, 'bv': bv, 'beta': beta}
    _L0_gnn_all = _L0_gnn_setup()
    _L0_gnn_in = {k: v for k, v in _L0_gnn_all.items() if k in ('Wq', 'bq', 'Wk', 'bk', 'Wv', 'bv', 'beta')}
    del _L0_gnn_all

    def _L0_ffn_setup():
        import jax, jax.numpy as jnp
        import numpy as np
        B, L, D, H, F = (4, 1024, 384, 12, 1536)
        ROUTE_FRAC = 0.15
        LN_EPS = 1e-05

        def _ln(x, g, b):
            m = jnp.mean(x, axis=-1, keepdims=True)
            v = jnp.mean((x - m) ** 2, axis=-1, keepdims=True)
            return (x - m) * jax.lax.rsqrt(v + LN_EPS) * g + b
        key = jax.random.key(seed)
        ks = jax.random.split(key, 20)
        s = 0.02
        return {'hidden_states': jax.random.normal(ks[0], (B, L, D), dtype=jnp.float32), 'g1': jnp.ones((D,), jnp.float32), 'b1': jnp.zeros((D,), jnp.float32), 'g2': jnp.ones((D,), jnp.float32), 'b2': jnp.zeros((D,), jnp.float32), 'Wr': jax.random.normal(ks[1], (D,), jnp.float32) * s, 'br': jnp.zeros((), jnp.float32), 'Wq': jax.random.normal(ks[2], (D, D), jnp.float32) * s, 'bq': jnp.zeros((D,), jnp.float32), 'Wk': jax.random.normal(ks[3], (D, D), jnp.float32) * s, 'bk': jnp.zeros((D,), jnp.float32), 'Wv': jax.random.normal(ks[4], (D, D), jnp.float32) * s, 'bv': jnp.zeros((D,), jnp.float32), 'Wo': jax.random.normal(ks[5], (D, D), jnp.float32) * s, 'bo': jnp.zeros((D,), jnp.float32), 'Wm': jax.random.normal(ks[6], (D, D), jnp.float32) * s, 'bm': jnp.zeros((D,), jnp.float32), 'W1': jax.random.normal(ks[7], (D, F), jnp.float32) * s, 'bf1': jnp.zeros((F,), jnp.float32), 'W2': jax.random.normal(ks[8], (F, D), jnp.float32) * s, 'bf2': jnp.zeros((D,), jnp.float32)}
    _L0_ffn_all = _L0_ffn_setup()
    _L0_ffn_in = {k: v for k, v in _L0_ffn_all.items() if k in ('g1', 'b1', 'g2', 'b2', 'Wr', 'br', 'Wq', 'bq', 'Wk', 'bk', 'Wv', 'bv', 'Wo', 'bo', 'Wm', 'bm', 'W1', 'bf1', 'W2', 'bf2')}
    del _L0_ffn_all
    return {'x': x, 'adj': adj, 'L0_gnn_Wq': _L0_gnn_in['Wq'], 'L0_gnn_bq': _L0_gnn_in['bq'], 'L0_gnn_Wk': _L0_gnn_in['Wk'], 'L0_gnn_bk': _L0_gnn_in['bk'], 'L0_gnn_Wv': _L0_gnn_in['Wv'], 'L0_gnn_bv': _L0_gnn_in['bv'], 'L0_gnn_beta': _L0_gnn_in['beta'], 'L0_ffn_g1': _L0_ffn_in['g1'], 'L0_ffn_b1': _L0_ffn_in['b1'], 'L0_ffn_g2': _L0_ffn_in['g2'], 'L0_ffn_b2': _L0_ffn_in['b2'], 'L0_ffn_Wr': _L0_ffn_in['Wr'], 'L0_ffn_br': _L0_ffn_in['br'], 'L0_ffn_Wq': _L0_ffn_in['Wq'], 'L0_ffn_bq': _L0_ffn_in['bq'], 'L0_ffn_Wk': _L0_ffn_in['Wk'], 'L0_ffn_bk': _L0_ffn_in['bk'], 'L0_ffn_Wv': _L0_ffn_in['Wv'], 'L0_ffn_bv': _L0_ffn_in['bv'], 'L0_ffn_Wo': _L0_ffn_in['Wo'], 'L0_ffn_bo': _L0_ffn_in['bo'], 'L0_ffn_Wm': _L0_ffn_in['Wm'], 'L0_ffn_bm': _L0_ffn_in['bm'], 'L0_ffn_W1': _L0_ffn_in['W1'], 'L0_ffn_bf1': _L0_ffn_in['bf1'], 'L0_ffn_W2': _L0_ffn_in['W2'], 'L0_ffn_bf2': _L0_ffn_in['bf2']}

def reference(x, adj, L0_gnn_Wq, L0_gnn_bq, L0_gnn_Wk, L0_gnn_bk, L0_gnn_Wv, L0_gnn_bv, L0_gnn_beta, L0_ffn_g1, L0_ffn_b1, L0_ffn_g2, L0_ffn_b2, L0_ffn_Wr, L0_ffn_br, L0_ffn_Wq, L0_ffn_bq, L0_ffn_Wk, L0_ffn_bk, L0_ffn_Wv, L0_ffn_bv, L0_ffn_Wo, L0_ffn_bo, L0_ffn_Wm, L0_ffn_bm, L0_ffn_W1, L0_ffn_bf1, L0_ffn_W2, L0_ffn_bf2):
    import jax
    import jax.numpy as jnp

    def _L0_gnn_ref(input_graph, adj, Wq, bq, Wk, bk, Wv, bv, beta):
        import jax, jax.numpy as jnp
        import numpy as np
        B, N, D, H = (8, 512, 384, 12)
        HD = D // H

        def _split_heads(x):
            b, n, _ = x.shape
            return x.reshape(b, n, H, HD).transpose(0, 2, 1, 3)
        q = _split_heads(input_graph @ Wq + bq)
        k = _split_heads(input_graph @ Wk + bk)
        v = _split_heads(input_graph @ Wv + bv)
        scores = jnp.einsum('bhqd,bhkd->bhqk', q, k) / jnp.sqrt(jnp.asarray(HD, input_graph.dtype))
        adj_e = adj[:, None, :, :]
        scores = scores + beta * adj_e
        scores = jnp.where(adj_e > 0, scores, jnp.asarray(-9000000000000000.0, scores.dtype))
        probs = jax.nn.softmax(scores, axis=-1)
        out = jnp.einsum('bhqk,bhkd->bhqd', probs, v)
        return out.transpose(0, 2, 1, 3).reshape(input_graph.shape[0], input_graph.shape[1], D)

    def _L0_ffn_ref(hidden_states, g1, b1, g2, b2, Wr, br, Wq, bq, Wk, bk, Wv, bv, Wo, bo, Wm, bm, W1, bf1, W2, bf2):
        import jax, jax.numpy as jnp
        import numpy as np
        B, L, D, H, F = (4, 1024, 384, 12, 1536)
        ROUTE_FRAC = 0.15
        LN_EPS = 1e-05

        def _ln(x, g, b):
            m = jnp.mean(x, axis=-1, keepdims=True)
            v = jnp.mean((x - m) ** 2, axis=-1, keepdims=True)
            return (x - m) * jax.lax.rsqrt(v + LN_EPS) * g + b
        b, l, d = hidden_states.shape
        dh = d // H
        normed = _ln(hidden_states, g1, b1)
        scores = jax.nn.sigmoid(jnp.einsum('bld,d->bl', normed, Wr) + br)
        k = max(1, int(round(ROUTE_FRAC * l)))
        _, idx = jax.lax.top_k(-scores, k)
        attn_mask = jnp.zeros((b, l), bool).at[jnp.arange(b)[:, None], idx].set(True)
        q = (normed @ Wq + bq).reshape(b, l, H, dh)
        kk = (normed @ Wk + bk).reshape(b, l, H, dh)
        v = (normed @ Wv + bv).reshape(b, l, H, dh)
        logits = jnp.einsum('blhd,bmhd->bhlm', q, kk) / jnp.sqrt(jnp.float32(dh))
        probs = jax.nn.softmax(logits, axis=-1)
        ctx = jnp.einsum('bhlm,bmhd->blhd', probs, v).reshape(b, l, d)
        attn_out = ctx @ Wo + bo
        w = scores / (jnp.sum(scores, axis=1, keepdims=True) + 1e-06)
        pooled = jnp.einsum('bl,bld->bd', w, normed)
        mix_out = (normed + scores[..., None] * pooled[:, None, :]) @ Wm + bm
        merged = jnp.where(attn_mask[..., None], attn_out, mix_out)
        h = hidden_states + merged
        n2 = _ln(h, g2, b2)
        ffn = jax.nn.gelu(n2 @ W1 + bf1, approximate=False) @ W2 + bf2
        return h + ffn
    x = x + _L0_gnn_ref(_layernorm(x, axis=-1), adj, L0_gnn_Wq, L0_gnn_bq, L0_gnn_Wk, L0_gnn_bk, L0_gnn_Wv, L0_gnn_bv, L0_gnn_beta)
    x = x + _L0_ffn_ref(_layernorm(x, axis=-1), L0_ffn_g1, L0_ffn_b1, L0_ffn_g2, L0_ffn_b2, L0_ffn_Wr, L0_ffn_br, L0_ffn_Wq, L0_ffn_bq, L0_ffn_Wk, L0_ffn_bk, L0_ffn_Wv, L0_ffn_bv, L0_ffn_Wo, L0_ffn_bo, L0_ffn_Wm, L0_ffn_bm, L0_ffn_W1, L0_ffn_bf1, L0_ffn_W2, L0_ffn_bf2)
    return x

_drawn_inputs = setup_inputs


def setup_inputs(seed=0):
    import zlib

    import numpy as np

    out = dict(_drawn_inputs(seed))
    spreads = {'L0_gnn_bq': (0.0, 0.1),
     'L0_gnn_bk': (0.0, 2.0),
     'L0_gnn_bv': (0.0, 0.1),
     'L0_ffn_g1': (1.0, 0.2),
     'L0_ffn_b1': (0.0, 0.292),
     'L0_ffn_g2': (1.0, 0.6),
     'L0_ffn_b2': (0.0, 0.8),
     'L0_ffn_bq': (0.0, 0.8),
     'L0_ffn_bk': (0.0, 2.0),
     'L0_ffn_bv': (0.0, 0.8),
     'L0_ffn_bo': (0.0, 0.407),
     'L0_ffn_bm': (0.0, 0.309),
     'L0_ffn_bf1': (0.0, 0.379),
     'L0_ffn_bf2': (0.0, 0.281)}
    factors = {'L0_ffn_Wq': 8.0, 'L0_ffn_Wk': 8.0, 'L0_ffn_Wv': 8.0, 'L0_ffn_Wo': 5.699}
    for name, (base, spread) in spreads.items():
        noise = np.random.default_rng([zlib.crc32(name.encode()), seed]).standard_normal(out[name].shape)
        drawn = base * np.exp(spread * noise) if base else spread * noise
        out[name] = jnp.asarray(drawn.astype(out[name].dtype))
    for name, factor in factors.items():
        out[name] = (out[name] * factor).astype(out[name].dtype)
    return out
```

```python
from contextlib import ExitStack

import concourse.bass as bass
from concourse import mybir

ALU = mybir.AluOpType
ACT = mybir.ActivationFunctionType
F32 = mybir.dt.float32
F16 = mybir.dt.float16
AX_X = mybir.AxisListType.X
RMAX = bass.bass_isa.ReduceOp.max

P = 128
GRAPHS, NODES, D = 128, 64, 384
HEADS, HD = 12, 32
F = 1536
KC = D // P
FC = F // P
PER_TILE = P // NODES
TILES = 4
TOK = TILES * P
GPS = TILES * PER_TILE
STEPS = GRAPHS // GPS
PICK = max(1, int(round(0.15 * NODES)))
EPS = 1e-5
MASKED = -9000000000000000.0
Z_SCALE = 1024.0
Z_MAX = float(D) ** 0.5 * 1.01
TOP = 32768.0
W_TOP = 2048.0
TINY = 1e-20
RSQRT_HD = float(HD) ** -0.5
VW = HD + 1


class Step:

    def __init__(self, m, b, u=2):
        self.m, self.b, self.u = m, b, u
        self.par = b % u
        self.i = b if isinstance(m, int) else u * m + b
        self.turn = b // u if isinstance(m, int) else m + b // u

    def plus(self, n):
        return Step(self.m, self.b + n, self.u)


def reach(eng, sem, value):
    if not (isinstance(value, int) and value <= 0):
        eng.wait_ge(sem, value)


def carry(eng):
    eng.nop(nofuse=True)


class Links:

    def __init__(self, eng, sem):
        self.eng, self.sem, self.base, self.n = eng, sem, 0, 0

    def start(self, base):
        self.base, self.n = base, 0

    def link(self, ins):
        self.n += 1
        ins.then_inc(self.sem, 1)
        self.eng.wait_ge(self.sem, self.base + self.n)


def run_steps(eng, body, first, loop_first, loops, last, u=2):
    for b in range(first, loop_first):
        body(Step(0, b, u))
    with eng.Fori(0, loops) as m:
        for n in range(u):
            body(Step(m, loop_first + n, u))
    for b in range(loop_first + u * loops, last + 1):
        body(Step(0, b, u))


class Pool:

    def __init__(self, nc, ctx, tag):
        self.nc, self.ctx, self.tag = nc, ctx, tag

    def sb(self, name, shape, dt):
        return self.ctx.enter_context(self.nc.sbuf_tensor(f"{self.tag}_{name}", shape, dt))

    def ps(self, name, shape, dt=F32):
        return self.ctx.enter_context(self.nc.psum_tensor(f"{self.tag}_{name}", shape, dt))

    def sem(self, name):
        return self.ctx.enter_context(self.nc.semaphore(f"{self.tag}_{name}"))


def gnn_phase(nc, x, adj, wq, bq, wk, bk, wv, bv, beta, x1):
    with ExitStack() as ctx:
        a = Pool(nc, ctx, "gnn")
        x_v = x.rearrange("(i t g) q d -> i (g q) t d", t=TILES, g=PER_TILE)
        x1_v = x1.rearrange("(i t g) q d -> i (g q) t d", t=TILES, g=PER_TILE)
        adj_v = adj.rearrange("(i g) q k -> i q g k", g=GPS)

        NW = 3
        wst = a.sb("w_staging", [P, NW, KC, D], F32)
        bst = a.sb("b_staging", [1, 2, D], F32)
        wh = a.sb("w_high", [P, NW, KC, D], F16)
        wl = a.sb("w_low", [P, NW, KC, D], F16)
        bias_rows = a.sb("bias_rows", [P, 2, D], F16)
        scale_rows = a.sb("scale_rows", [P, TOK], F16)
        tops = a.sb("tops", [P, 2, NW], F32)
        topa = a.sb("tops_all", [P, 2, NW], F32)
        wmax = a.sb("w_max", [P, NW], F32)
        wrec = a.sb("w_rec", [P, NW], F32)
        wscale = a.sb("w_scale", [P, NW], F32)
        bound = a.sb("bound", [P, NW], F32)
        brec = a.sb("bound_rec", [P, NW], F32)
        cscale = a.sb("out_scale", [P, NW], F32)
        evac = a.sb("evac_scale", [P, NW], F32)
        sscale = a.sb("score_scale", [P, 1], F32)
        ident = a.sb("ident", [P, P], F32)
        bvrow = a.sb("bv_row", [P, D], F32)
        betac = a.sb("beta_col", [P, 1], F32)
        nhalf = a.sb("minus_half", [P, TILES], F32)
        onec = a.sb("one_col", [P, 1], F32)

        xin = a.sb("x_in", [P, 2, TILES, D], F32)
        xres = a.sb("x_plus_bv", [P, 2, TILES, D], F32)
        z = a.sb("z", [P, TILES, D], F32)
        stat = a.sb("stat", [P, TILES, 6], F32)
        mv = a.sb("mean_var", [P, TILES, 2], F32)
        vs = a.sb("var_scaled", [P, TILES], F32)
        rstd = a.sb("rstd", [P, TILES], F32)
        nmean = a.sb("minus_mean", [P, TILES], F32)
        nmr = a.sb("minus_mean_rstd", [P, TILES], F32)
        zh = a.sb("zT_high", [P, KC, TOK], F16)
        zl = a.sb("zT_low", [P, KC, TOK], F16)
        qh = a.sb("q_high", [P, 2, KC, 2, GPS, 2, NODES], F16)
        ql = a.sb("q_low", [P, 2, KC, 2, GPS, 2, NODES], F16)
        kh = a.sb("k_high", [P, 2, KC, TOK], F16)
        kl = a.sb("k_low", [P, 2, KC, TOK], F16)
        vh = a.sb("v_high", [P, 2, TILES, HEADS, VW], F16)
        vl = a.sb("v_low", [P, 2, TILES, HEADS, VW], F16)
        adjb = a.sb("adj_in", [P, GPS * NODES], F32)
        edge = a.sb("beta_adj", [P, GPS * NODES], F32)
        neg = a.sb("mask_neg", [P, GPS * NODES], F32)
        mask = a.sb("mask_add", [P, 2, GPS * NODES], F32)
        NJ = HEADS // 2
        sc = a.sb("scores", [P, 2, NJ, P], F32)
        mx = a.sb("row_max", [P, 2, HEADS], F32)
        pth = a.sb("pT_high", [P, 2, NJ, P], F16)
        ptl = a.sb("pT_low", [P, 2, NJ, P], F16)
        rs = a.sb("row_rec", [P, 2, HEADS], F32)
        on = a.sb("out_norm", [P, 2, D], F32)
        x1b = a.sb("x1_out", [P, 2, TILES, D], F32)

        zT_ps = a.ps("zT_ps", [P, TOK])
        pr_ps = [a.ps(f"proj_ps{n}", [P, TOK]) for n in range(2)]
        s_ps = a.ps("score_ps", [P, 2 * 512])
        p_ps = a.ps("pT_ps", [P, 2 * 512])
        o_ps = a.ps("pv_ps", [P, 512])
        s3 = s_ps[:, 0:NJ * P].rearrange("p (j c) -> p j c", j=NJ)
        p3 = p_ps[:, 0:NJ * P].rearrange("p (j c) -> p j c", j=NJ)
        o3 = o_ps[:, 0:HEADS * VW].rearrange("p (h c) -> p h c", h=HEADS)

        sem = a.sem
        w_in, b_in, row_in = sem("w_in"), sem("b_in"), sem("row_in")
        const_set, ident_set = sem("const_set"), sem("ident_set")
        zeroed, tops_done, topall_done = sem("zeroed"), sem("tops_done"), sem("topall_done")
        chain, scales_done = sem("chain"), sem("scales_done")
        wh_done, wl_done = sem("wh_done"), sem("wl_done")
        x_in = [sem("x_in0"), sem("x_in1")]
        adj_in = sem("adj_in")
        neg_done, mask_done = sem("neg_done"), sem("mask_done")
        bn_done, stats_done = sem("bn_done"), sem("stats_done")
        pool_chain, rstd_done, xres_done = sem("pool_chain"), sem("rstd_done"), sem("xres_done")
        z_done, zT_done, zTh_done, zTl_done = sem("z_done"), sem("zT_done"), sem("zTh_done"), sem("zTl_done")
        proj_done, projh_done, projl_done = sem("proj_done"), sem("projh_done"), sem("projl_done")
        s_done, s_evac, mx_done, sub_done, exp_done = (
            sem("s_done"), sem("s_evac"), sem("mx_done"), sem("sub_done"), sem("exp_done"))
        pT_done, pTh_done, pTl_done = sem("pT_done"), sem("pTh_done"), sem("pTl_done")
        pv_done, rs_done, o_done, x1_done = sem("pv_done"), sem("rs_done"), sem("o_done"), sem("x1_done")
        x1_out = [sem("x1_out0"), sem("x1_out1")]
        NP = 2 * KC + TILES

        FIRST, LOOP, PAIRS, LAST = -1, 2, (STEPS - 4) // 2, STEPS
        assert LOOP + 2 * PAIRS <= STEPS - 2

        block = ctx.enter_context(nc.Block())

        @block.sync
        def _(sp):
            for n, w in enumerate((wq, wk, wv)):
                sp.dma_start(wst[:, n], w.rearrange("(k p) n -> p k n", p=P)).then_inc(w_in, 16)
            for n, b in enumerate((bq, bk)):
                sp.dma_start(bst[:, n, :], b.rearrange("(a d) -> a d", a=1)).then_inc(b_in, 16)
            for n in range(2):
                sp.dma_start(xin[:, n], x_v[n]).then_inc(x_in[n], 16)
            for n in range(2):
                sp.dma_start(adjb[n * NODES:(n + 1) * NODES, :].rearrange("q (g k) -> q g k", g=GPS),
                             adj_v[0]).then_inc(adj_in, 16)
            sp.dma_start(bvrow[:], bv.rearrange("(a d) -> a d", a=1).to_broadcast([P, D])).then_inc(row_in, 16)
            sp.dma_start(betac[:], beta.rearrange("(a b) -> a b", a=1).to_broadcast([P, 1])).then_inc(row_in, 16)

            def body(s):
                ahead, prev = s.plus(2), s.plus(-1)
                if 0 <= s.b and ahead.b < STEPS:
                    sp.wait_ge(z_done, TILES * (s.i + 1))
                    sp.wait_ge(xres_done, s.i + 1)
                    sp.dma_start(xin[:, s.par], x_v[ahead.i]).then_inc(x_in[s.par], 16)
                if ahead.b < STEPS:
                    reach(sp, mask_done, s.i + 2)
                    for n in range(2):
                        sp.dma_start(adjb[n * NODES:(n + 1) * NODES, :].rearrange("q (g k) -> q g k", g=GPS),
                                     adj_v[ahead.i]).then_inc(adj_in, 16)
                if prev.b >= 0:
                    sp.wait_ge(x1_done, TILES * (prev.i + 1))
                    sp.dma_start(x1_v[prev.i], x1b[:, prev.par]).then_inc(x1_out[prev.par], 16)

            run_steps(sp, body, FIRST, LOOP, PAIRS, LAST)
            for n in range(2):
                sp.wait_ge(x1_out[n], 16 * (STEPS // 2))

        @block.gpsimd
        def _(pool):
            g = nc.gpsimd
            g.memset(ident[:], 0.0).then_inc(zeroed, 1)
            g.memset(tops[:], 0.0).then_inc(const_set, 1)
            g.memset(scale_rows[:], Z_SCALE).then_inc(const_set, 1)
            g.memset(bias_rows[:], 0.0).then_inc(const_set, 1)
            g.memset(nhalf[:], -0.5).then_inc(const_set, 1)
            g.memset(onec[:], 1.0).then_inc(const_set, 1)
            pool.wait_ge(zeroed, 1)
            g.affine_select(out=ident[:], in_=ident[:], compare_op=ALU.not_equal, fill=1.0, base=0,
                            pattern=[[-1, P]], channel_multiplier=1).then_inc(ident_set, 1)
            pool.wait_ge(tops_done, 2)
            g.partition_all_reduce(topa[:].rearrange("p a n -> p (a n)"), tops[:].rearrange("p a n -> p (a n)"),
                                   P, RMAX).then_inc(topall_done, 1)
            for n in range(2):
                for t in (qh, ql):
                    g.memset(t[:, n], 0.0).then_inc(zeroed, 1)
            pool.wait_ge(const_set, 5)
            pool.wait_ge(row_in, 32)

            links = [0]

            def rstd_of():
                carry(pool)
                g.tensor_scalar(nmean[:], mv[:, :, 0], -1.0, None, ALU.mult)
                g.tensor_scalar(vs[:], mv[:, :, 1], EPS, Z_SCALE ** -2, ALU.add, ALU.mult).then_inc(pool_chain, 1)

            def ln(s):
                reach(pool, stats_done, s.i + 1)
                rstd_of()
                pool.wait_ge(pool_chain, 2 * s.i + 1)
                reach(pool, z_done, TILES * s.i)
                g.tensor_tensor(rstd[:], vs[:], nhalf[:], ALU.pow).then_inc(pool_chain, 1)
                pool.wait_ge(pool_chain, 2 * s.i + 2)
                g.tensor_tensor(nmr[:], nmean[:], rstd[:], ALU.mult).then_inc(rstd_done, 1)

            def make_mask(s):
                pool.wait_ge(adj_in, 32 * (s.i + 1))
                reach(pool, mask_done, s.i)
                carry(pool)
                g.tensor_scalar(edge[:], adjb[:], betac[:, 0:1], None, ALU.mult)
                g.tensor_scalar(neg[:], adjb[:], 0.0, MASKED, ALU.is_le, ALU.mult).then_inc(neg_done, 1)
                pool.wait_ge(neg_done, s.i + 1)
                reach(pool, s_evac, TILES * (s.i - 1))
                g.tensor_tensor(mask[:, s.par], edge[:], neg[:], ALU.add).then_inc(mask_done, 1)

            def subtract(s, t):
                pool.wait_ge(mx_done, TILES * s.i + t + 1)
                sv = sc[:, t % 2].rearrange("p j (g k) -> p (j g) k", g=PER_TILE)
                g.tensor_tensor(sv, sv,
                                mx[:, t % 2, :].unsqueeze(2).to_broadcast([P, HEADS, NODES]), ALU.subtract).then_inc(sub_done, 1)

            def residual(s, t):
                pool.wait_ge(o_done, TILES * s.i + t + 1)
                if t == 0:
                    reach(pool, x1_out[s.par], 16 * s.turn)
                    pool.wait_ge(xres_done, s.i + 1)
                g.tensor_tensor(x1b[:, s.par, t, :], on[:, t % 2, :],
                                xres[:, s.par, t, :], ALU.add).then_inc(x1_done, 1)

            def add_bv(s):
                reach(pool, x1_done, TILES * (s.i - 1))
                g.tensor_tensor(xres[:, s.par], xin[:, s.par], bvrow[:].unsqueeze(1).to_broadcast([P, TILES, D]),
                                ALU.add).then_inc(xres_done, 1)

            def body(s):
                prev, nx, ah = s.plus(-1), s.plus(1), s.plus(2)
                main, tail = 0 <= s.b < STEPS, prev.b >= 0
                if s.b < 0:
                    ln(nx)
                    make_mask(nx)
                    add_bv(nx)
                if main:
                    subtract(s, 0)
                if tail:
                    residual(prev, 2)
                if main:
                    subtract(s, 1)
                if tail:
                    residual(prev, 3)
                if nx.b >= 1 and nx.b < STEPS:
                    make_mask(nx)
                if ah.b < STEPS:
                    ln(ah)
                if main:
                    subtract(s, 2)
                    residual(s, 0)
                    subtract(s, 3)
                    residual(s, 1)
                if nx.b >= 1 and nx.b < STEPS:
                    add_bv(nx)

            run_steps(pool, body, FIRST, LOOP, PAIRS, LAST)

        @block.scalar
        def _(act):
            s_ = nc.scalar
            for n in range(NW):
                act.wait_ge(scales_done, 1)
                s_.activation(wh[:, n].rearrange("p k n -> p (k n)"), wst[:, n].rearrange("p k n -> p (k n)"),
                              ACT.Copy, scale=wscale[:, n:n + 1]).then_inc(wh_done, 1)
            act.wait_ge(zeroed, 5)

            def normalise(s, t):
                if t == 0:
                    act.wait_ge(rstd_done, s.i + 1)
                    reach(act, zT_done, KC * s.i)
                s_.activation(z[:, t, :], xin[:, s.par, t, :], ACT.Identity, bias=nmr[:, t:t + 1],
                              scale=rstd[:, t:t + 1]).then_inc(z_done, 1)

            def zT_high(s, k):
                act.wait_ge(zT_done, KC * s.i + k + 1)
                s_.copy(zh[:, k, :], zT_ps[:]).then_inc(zTh_done, 1)

            def proj_high(s, n):
                act.wait_ge(proj_done, NP * s.i + n + 1)
                ps = pr_ps[n % 2]
                if n >= 2 * KC:
                    t = n - 2 * KC
                    s_.activation(vh[:, s.par, t, :, 0:HD], ps[:, 0:D].rearrange("p (h d) -> p h d", h=HEADS),
                                  ACT.Copy, scale=evac[:, 2:3]).then_inc(projh_done, 4)
                elif n % 2:
                    s_.activation(kh[:, s.par, n // 2, :], ps[:], ACT.Copy, scale=evac[:, 1:2]).then_inc(projh_done, 4)
                else:
                    for h in range(4):
                        r = slice(HD * h, HD * h + HD)
                        s_.activation(qh[r, s.par, n // 2, h // 2, :, h % 2, :],
                                      ps[r, :].rearrange("p (g q) -> p g q", g=GPS),
                                      ACT.Copy, scale=evac[r, 0:1]).then_inc(projh_done, 1)

            def exp(s, t):
                act.wait_ge(sub_done, TILES * s.i + t + 1)
                s_.activation(sc[:, t % 2], sc[:, t % 2], ACT.Exp).then_inc(exp_done, 1)

            def pT_high(s, t):
                act.wait_ge(pT_done, TILES * s.i + t + 1)
                s_.copy(pth[:, t % 2], p3).then_inc(pTh_done, 1)

            def body(s):
                prev, nx, ah = s.plus(-1), s.plus(1), s.plus(2)
                main, proj, norm, tail = 0 <= s.b < STEPS, nx.b < STEPS, ah.b < STEPS, prev.b >= 0
                if s.b < 0:
                    for t in range(TILES):
                        normalise(nx, t)
                if proj:
                    zT_high(nx, 0)
                if tail:
                    pT_high(prev, 3)
                if proj:
                    zT_high(nx, 1)
                    zT_high(nx, 2)
                if main:
                    exp(s, 0)
                if proj:
                    proj_high(nx, 0)
                if main:
                    exp(s, 1)
                if proj:
                    proj_high(nx, 1)
                if main:
                    pT_high(s, 0)
                if proj:
                    proj_high(nx, 2)
                    proj_high(nx, 3)
                if main:
                    pT_high(s, 1)
                    exp(s, 2)
                if norm:
                    normalise(ah, 0)
                if proj:
                    proj_high(nx, 4)
                if norm:
                    normalise(ah, 1)
                    normalise(ah, 2)
                    normalise(ah, 3)
                if proj:
                    proj_high(nx, 5)
                if main:
                    exp(s, 3)
                if proj:
                    proj_high(nx, 6)
                    proj_high(nx, 7)
                if main:
                    pT_high(s, 2)
                if proj:
                    proj_high(nx, 8)
                    proj_high(nx, 9)

            run_steps(act, body, FIRST, LOOP, PAIRS, LAST)

        @block.vector
        def _(dve):
            v = nc.vector
            dve.wait_ge(const_set, 1)
            dve.wait_ge(w_in, 16 * NW)
            v.tensor_reduce(tops[:, 0, :], wst[:].rearrange("p w k n -> p w (k n)"), AX_X, ALU.max, apply_absolute_value=True)\
                .then_inc(tops_done, 1)
            dve.wait_ge(b_in, 32)
            v.tensor_reduce(tops[0:1, 1, 0:2], bst[:], AX_X, ALU.max, apply_absolute_value=True).then_inc(tops_done, 1)
            links = [0]

            def link(ins):
                links[0] += 1
                ins.then_inc(chain, 1)
                dve.wait_ge(chain, links[0])

            dve.wait_ge(topall_done, 1)
            link(v.tensor_tensor(wmax[:], topa[:, 0, :], topa[:, 1, :], ALU.max))
            link(v.tensor_scalar(wmax[:], wmax[:], TINY, None, ALU.max))
            link(v.reciprocal(wrec[:], wmax[:]))
            v.tensor_scalar(wscale[:], wrec[:], W_TOP, None, ALU.mult).then_inc(scales_done, 1)
            link(v.scalar_tensor_tensor(out=bound[:], in0=topa[:, 0, :], scalar=Z_MAX * D, in1=topa[:, 1, :],
                                        op0=ALU.mult, op1=ALU.add))
            link(v.tensor_scalar(bound[:], bound[:], TINY, None, ALU.max))
            link(v.reciprocal(brec[:], bound[:]))
            link(v.tensor_scalar(cscale[:], brec[:], TOP, None, ALU.mult))
            link(v.scalar_tensor_tensor(out=evac[:], in0=cscale[:], scalar=1.0 / (Z_SCALE * W_TOP), in1=wmax[:],
                                        op0=ALU.mult, op1=ALU.mult))
            link(v.scalar_tensor_tensor(out=sscale[:], in0=bound[:, 0:1], scalar=RSQRT_HD / (TOP * TOP),
                                        in1=bound[:, 1:2], op0=ALU.mult, op1=ALU.mult))
            ones = vh[:, :, :, :, HD].rearrange("p a t h -> p (a t) h")
            onesl = vl[:, :, :, :, HD].rearrange("p a t h -> p (a t) h")
            cvb = cscale[:, 2:3].unsqueeze(2).to_broadcast([P, 2 * TILES, HEADS])
            link(v.tensor_copy(ones, cvb))
            link(v.tensor_tensor(onesl, cvb, ones, ALU.subtract))
            dve.wait_ge(const_set, 3)
            for n in range(2):
                link(v.tensor_scalar(bias_rows[0:1, n, :], bst[:, n, :], wscale[0:1, n:n + 1], None, ALU.mult))
                link(v.scalar_tensor_tensor(out=bias_rows[32:33, n, :], in0=bst[:, n, :],
                                            scalar=wscale[0:1, n:n + 1], in1=bias_rows[0:1, n, :],
                                            op0=ALU.mult, op1=ALU.subtract))
            for n in range(NW):
                dve.wait_ge(wh_done, n + 1)
                v.scalar_tensor_tensor(out=wl[:, n].rearrange("p k n -> p (k n)"),
                                       in0=wst[:, n].rearrange("p k n -> p (k n)"), scalar=wscale[:, n:n + 1],
                                       in1=wh[:, n].rearrange("p k n -> p (k n)"),
                                       op0=ALU.mult, op1=ALU.subtract).then_inc(wl_done, 1)
            dve.wait_ge(const_set, 5)
            dve.wait_ge(zeroed, 5)

            def stats(s):
                dve.wait_ge(x_in[s.par], 16 * (s.turn + 1))
                for t in range(TILES):
                    last = v.bn_stats(stat[:, t, :], xin[:, s.par, t, :])
                last.then_inc(bn_done, 1)
                dve.wait_ge(bn_done, s.i + 1)
                reach(dve, rstd_done, s.i)
                carry(dve)
                for t in range(TILES):
                    last = v.bn_aggr(mv[:, t, :], stat[:, t, :])
                last.then_inc(stats_done, 1)

            def zT_low(s, k):
                dve.wait_ge(zTh_done, KC * s.i + k + 1)
                v.tensor_tensor(zl[:, k, :], zT_ps[:], zh[:, k, :], ALU.subtract).then_inc(zTl_done, 1)

            def proj_low(s, n):
                count = 4 * (NP * s.i + n)
                if n % 2 or n >= 2 * KC:
                    dve.wait_ge(projh_done, count + 4)
                ps = pr_ps[n % 2]
                if n >= 2 * KC:
                    t = n - 2 * KC
                    v.scalar_tensor_tensor(out=vl[:, s.par, t, :, 0:HD],
                                           in0=ps[:, 0:D].rearrange("p (h d) -> p h d", h=HEADS),
                                           scalar=evac[:, 2:3], in1=vh[:, s.par, t, :, 0:HD],
                                           op0=ALU.mult, op1=ALU.subtract).then_inc(projl_done, 1)
                elif n % 2:
                    v.scalar_tensor_tensor(out=kl[:, s.par, n // 2, :], in0=ps[:], scalar=evac[:, 1:2],
                                           in1=kh[:, s.par, n // 2, :],
                                           op0=ALU.mult, op1=ALU.subtract).then_inc(projl_done, 1)
                else:
                    for h in range(4):
                        dve.wait_ge(projh_done, count + h + 1)
                        r = slice(HD * h, HD * h + HD)
                        at = (r, s.par, n // 2, h // 2, slice(None), h % 2, slice(None))
                        last = v.scalar_tensor_tensor(out=ql[at], in0=ps[r, :].rearrange("p (g q) -> p g q", g=GPS),
                                                      scalar=evac[r, 0:1], in1=qh[at],
                                                      op0=ALU.mult, op1=ALU.subtract)
                    last.then_inc(projl_done, 1)

            def mask_scores(s, t):
                dve.wait_ge(s_done, TILES * s.i + t + 1)
                if t == 0:
                    dve.wait_ge(mask_done, s.i + 1)
                reach(dve, pT_done, TILES * s.i + t - 1)
                m = mask[:, s.par, P * t:P * t + P].unsqueeze(1).to_broadcast([P, NJ, P])
                v.scalar_tensor_tensor(out=sc[:, t % 2], in0=s3, scalar=sscale[:, 0:1], in1=m,
                                       op0=ALU.mult, op1=ALU.add).then_inc(s_evac, 1)
                dve.wait_ge(s_evac, TILES * s.i + t + 1)
                reach(dve, sub_done, TILES * s.i + t - 1)
                v.tensor_reduce(mx[:, t % 2, :], sc[:, t % 2].rearrange("p j (g k) -> p (j g) k", g=PER_TILE),
                                AX_X, ALU.max).then_inc(mx_done, 1)

            def pT_low(s, t):
                dve.wait_ge(pTh_done, TILES * s.i + t + 1)
                v.tensor_tensor(ptl[:, t % 2], p3, pth[:, t % 2], ALU.subtract).then_inc(pTl_done, 1)

            def divide(s, t):
                dve.wait_ge(pv_done, TILES * s.i + t + 1)
                v.reciprocal(rs[:, t % 2, :], o3[:, :, HD]).then_inc(rs_done, 1)
                dve.wait_ge(rs_done, TILES * s.i + t + 1)
                reach(dve, x1_done, TILES * s.i + t - 1)
                v.tensor_tensor(on[:, t % 2, :].rearrange("p (h d) -> p h d", h=HEADS), o3[:, :, 0:HD],
                                rs[:, t % 2, :].unsqueeze(2).to_broadcast([P, HEADS, HD]),
                                ALU.mult).then_inc(o_done, 1)

            def body(s):
                prev, nx, ah = s.plus(-1), s.plus(1), s.plus(2)
                main, proj, norm, tail = 0 <= s.b < STEPS, nx.b < STEPS, ah.b < STEPS, prev.b >= 0
                if s.b < 0:
                    stats(nx)
                if proj:
                    zT_low(nx, 0)
                if main:
                    mask_scores(s, 0)
                if proj:
                    zT_low(nx, 1)
                if tail:
                    pT_low(prev, 3)
                if proj:
                    zT_low(nx, 2)
                if tail:
                    divide(prev, 2)
                if main:
                    mask_scores(s, 1)
                if proj:
                    proj_low(nx, 0)
                if tail:
                    divide(prev, 3)
                if proj:
                    proj_low(nx, 1)
                if main:
                    pT_low(s, 0)
                if norm:
                    stats(ah)
                if proj:
                    proj_low(nx, 2)
                if main:
                    mask_scores(s, 2)
                if proj:
                    proj_low(nx, 3)
                if main:
                    divide(s, 0)
                    pT_low(s, 1)
                if proj:
                    proj_low(nx, 4)
                if main:
                    mask_scores(s, 3)
                    divide(s, 1)
                if proj:
                    proj_low(nx, 5)
                    proj_low(nx, 6)
                    proj_low(nx, 7)
                if main:
                    pT_low(s, 2)
                if proj:
                    proj_low(nx, 8)
                    proj_low(nx, 9)

            run_steps(dve, body, FIRST, LOOP, PAIRS, LAST)

        @block.tensor
        def _(pe):
            mm = nc.tensor.matmul
            pe.wait_ge(ident_set, 1)
            pe.wait_ge(wl_done, NW)

            def three(out, sh, sl, mh, ml, first, last):
                mm(out, sh, mh, start=first, stop=False)
                mm(out, sl, mh, start=False, stop=False)
                return mm(out, sh, ml, start=False, stop=last)

            def zT(s, k):
                if k == 0:
                    pe.wait_ge(z_done, TILES * (s.i + 1))
                reach(pe, zTl_done, KC * s.i + k)
                for t in range(TILES):
                    last = nc.tensor.transpose(zT_ps[:, P * t:P * t + P], z[:, t, P * k:P * k + P], ident[:])
                last.then_inc(zT_done, 1)

            def proj(s, n):
                reach(pe, projl_done, NP * s.i + n - 1)
                ps = pr_ps[n % 2]
                if n < 2 * KC:
                    w, c = n % 2, slice(P * (n // 2), P * (n // 2) + P)
                    mm(ps[:], bias_rows[:, w, c], scale_rows[:], start=True, stop=False)
                    for k in range(KC):
                        if n == 0:
                            pe.wait_ge(zTl_done, KC * s.i + k + 1)
                        last = three(ps[:], wh[:, w, k, c], wl[:, w, k, c], zh[:, k, :], zl[:, k, :],
                                     False, k == KC - 1)
                else:
                    c = slice(P * (n - 2 * KC), P * (n - 2 * KC) + P)
                    for k in range(KC):
                        last = three(ps[:, 0:D], zh[:, k, c], zl[:, k, c], wh[:, 2, k, :], wl[:, 2, k, :],
                                     k == 0, k == KC - 1)
                last.then_inc(proj_done, 1)

            def scores(s, t):
                if t == 0:
                    pe.wait_ge(projl_done, NP * s.i + 2 * KC)
                reach(pe, s_evac, TILES * s.i + t)
                for j in range(NJ):
                    for g in range(PER_TILE):
                        gg = PER_TILE * t + g
                        at = (slice(None), s.par, j // 2, j % 2, gg)
                        st_h = qh[at].rearrange("p h q -> p (h q)")
                        st_l = ql[at].rearrange("p h q -> p (h q)")
                        c = slice(NODES * gg, NODES * gg + NODES)
                        last = three(s3[:, j, NODES * g:NODES * g + NODES], st_h, st_l,
                                     kh[:, s.par, j // 2, c], kl[:, s.par, j // 2, c], True, True)
                last.then_inc(s_done, 1)

            def pT(s, t):
                pe.wait_ge(exp_done, TILES * s.i + t + 1)
                reach(pe, pTl_done, TILES * s.i + t)
                for j in range(NJ):
                    last = nc.tensor.transpose(p3[:, j, :], sc[:, t % 2, j, :], ident[:])
                last.then_inc(pT_done, 1)

            def pv(s, t):
                pe.wait_ge(pTl_done, TILES * s.i + t + 1)
                pe.wait_ge(projl_done, NP * s.i + 2 * KC + t + 1)
                reach(pe, o_done, TILES * s.i + t)
                carry(pe)
                for h in range(HEADS):
                    for g in range(PER_TILE):
                        r = slice(NODES * g, NODES * g + NODES)
                        c = slice(NODES * (h % 2), NODES * (h % 2) + NODES)
                        last = three(o3[r, h, :], pth[r, t % 2, h // 2, c], ptl[r, t % 2, h // 2, c],
                                     vh[r, s.par, t, h, :], vl[r, s.par, t, h, :], True, True)
                last.then_inc(pv_done, 1)

            def body(s):
                prev, nx = s.plus(-1), s.plus(1)
                main, more, tail = 0 <= s.b < STEPS, nx.b < STEPS, prev.b >= 0
                if more:
                    zT(nx, 0)
                if main:
                    scores(s, 0)
                if tail:
                    pT(prev, 3)
                if more:
                    zT(nx, 1)
                if tail:
                    pv(prev, 2)
                if more:
                    zT(nx, 2)
                if main:
                    scores(s, 1)
                if more:
                    proj(nx, 0)
                if tail:
                    pv(prev, 3)
                if more:
                    proj(nx, 1)
                if main:
                    pT(s, 0)
                if more:
                    proj(nx, 2)
                if main:
                    scores(s, 2)
                if more:
                    proj(nx, 3)
                if main:
                    pv(s, 0)
                    pT(s, 1)
                if more:
                    proj(nx, 4)
                if main:
                    scores(s, 3)
                    pv(s, 1)
                if more:
                    proj(nx, 5)
                    proj(nx, 6)
                    proj(nx, 7)
                if main:
                    pT(s, 2)
                if more:
                    proj(nx, 8)
                    proj(nx, 9)

            run_steps(pe, body, FIRST, LOOP, PAIRS, LAST)


def mlp_phase(nc, h, x1, g2, b2, w1, bf1, w2, bf2, ident_in, out):
    with ExitStack() as ctx:
        a = Pool(nc, ctx, "mlp")
        view = lambda t: t.rearrange("(i t g) q d -> i (g q) t d", t=TILES, g=PER_TILE)
        h_v, x1_v, out_v = view(h), view(x1), view(out)
        row = lambda t: t.rearrange("(a d) -> a d", a=1)
        RING = 4
        LAG = 2
        BANKS = 3

        w1s = a.sb("w1_staging", [P, KC, F], F32)
        w2s = a.sb("w2_staging", [P, FC, D], F32)
        w1h, w1l = a.sb("w1_high", [P, KC, F], F16), a.sb("w1_low", [P, KC, F], F16)
        w2h, w2l = a.sb("w2_high", [P, FC, D], F16), a.sb("w2_low", [P, FC, D], F16)
        ident = a.sb("ident", [P, P], F32)
        tops, topa = a.sb("tops", [P, 5], F32), a.sb("tops_all", [P, 5], F32)
        gcol, bcol, fcol = a.sb("g2_col", [P, KC], F32), a.sb("b2_col", [P, KC], F32), a.sb("bf1_col", [P, FC], F32)
        rec5 = a.sb("rec", [P, 5], F32)
        wsc = a.sb("w_scale", [P, 2], F32)
        gsc = a.sb("g_scaled", [P, KC], F32)
        bsc = a.sb("b_scale", [P, 1], F32)
        bh, bl = a.sb("b2_high", [P, KC], F16), a.sb("b2_low", [P, KC], F16)
        ub = a.sb("u_bound", [P, 2], F32)
        ca = a.sb("act_scale", [P, 1], F32)
        us = a.sb("u_scale", [P, 1], F32)
        bs = a.sb("bias_scale", [P, 1], F32)
        os_ = a.sb("out_scale", [P, 1], F32)
        ubias = a.sb("u_bias", [P, FC], F32)
        frow = a.sb("bf2_row", [P, D], F32)
        nhalf = a.sb("minus_half", [P, TILES], F32)
        onec = a.sb("one_col", [P, 1], F32)

        hin = a.sb("h_in", [P, 2, TILES, D], F32)
        xin = a.sb("x1_in", [P, 2, TILES, D], F32)
        base = a.sb("base", [P, TILES, D], F32)
        z = a.sb("z", [P, TILES, D], F32)
        stat = a.sb("stat", [P, TILES, 6], F32)
        mv = a.sb("mean_var", [P, TILES, 2], F32)
        vs, rstd, nmean, nmr = (a.sb(n, [P, TILES], F32) for n in ("var_eps", "rstd", "minus_mean", "minus_mean_rstd"))
        zh, zl = a.sb("zT_high", [P, 2, KC, TOK], F16), a.sb("zT_low", [P, 2, KC, TOK], F16)
        act32 = a.sb("act", [P, 2, TOK], F32)
        ah, al = a.sb("act_high", [P, RING, TOK], F16), a.sb("act_low", [P, RING, TOK], F16)
        outb = a.sb("out", [P, 2, TILES, D], F32)

        u_ps = [a.ps(f"u_ps{n}", [P, TOK]) for n in range(BANKS)]
        y_ps = [a.ps(f"y_ps{n}", [P, 512]) for n in range(TILES)]
        zT_ps = a.ps("zT_ps", [P, TOK])

        sem = a.sem
        w_in, col_in, row_in = sem("w_in"), sem("col_in"), sem("row_in")
        const_set, tops_done, topall_done = sem("const_set"), sem("tops_done"), sem("topall_done")
        chain, scales_done, bsplit_done = sem("chain"), sem("scales_done"), sem("bsplit_done")
        wh_done, wl_done, bias_done, ubias_done = sem("wh_done"), sem("wl_done"), sem("bias_done"), sem("ubias_done")
        h_in, x_in = [sem("h_in0"), sem("h_in1")], [sem("x_in0"), sem("x_in1")]
        bn_done, stats_done, pool_chain, rstd_done = (
            sem("bn_done"), sem("stats_done"), sem("pool_chain"), sem("rstd_done"))
        z_done, zT_done, zTh_done, zTl_done = sem("z_done"), sem("zT_done"), sem("zTh_done"), sem("zTl_done")
        sum_done, base_done = sem("sum_done"), sem("base_done")
        u_done, gelu_done, ah_done, al_done = sem("u_done"), sem("gelu_done"), sem("ah_done"), sem("al_done")
        y_part, out_done = sem("y_part"), sem("out_done")
        out_st = [sem("out_st0"), sem("out_st1")]

        FIRST, LOOP, LOOPS, LAST = -1, 1, (STEPS - 3) // 2, STEPS
        block = ctx.enter_context(nc.Block())

        @block.sync
        def _(sp):
            for k in range(KC):
                sp.dma_start(w1s[:, k, :], w1[P * k:P * k + P, :]).then_inc(w_in, 16)
            sp.dma_start(w2s[:], w2.rearrange("(k p) n -> p k n", p=P)).then_inc(w_in, 16)
            sp.dma_start(gcol[:], g2.rearrange("(k p) -> p k", p=P), allow_slow_non_contiguous=True).then_inc(col_in, 16)
            sp.dma_start(bcol[:], b2.rearrange("(k p) -> p k", p=P), allow_slow_non_contiguous=True).then_inc(col_in, 16)
            sp.dma_start(fcol[:], bf1.rearrange("(k p) -> p k", p=P), allow_slow_non_contiguous=True).then_inc(col_in, 16)
            sp.dma_start(ident[:], ident_in).then_inc(row_in, 16)
            sp.dma_start(frow[:], row(bf2).to_broadcast([P, D])).then_inc(row_in, 16)
            for n in range(2):
                sp.dma_start(hin[:, n], h_v[n]).then_inc(h_in[n], 16)
                sp.dma_start(xin[:, n], x1_v[n]).then_inc(x_in[n], 16)

            def body(s):
                if s.b >= 0 and s.b + 2 < STEPS:
                    sp.wait_ge(base_done, s.i + 1)
                    sp.dma_start(hin[:, s.par], h_v[s.i + 2]).then_inc(h_in[s.par], 16)
                    sp.dma_start(xin[:, s.par], x1_v[s.i + 2]).then_inc(x_in[s.par], 16)
                if s.b >= 1:
                    before = s.plus(-1)
                    sp.wait_ge(out_done, TILES * s.i)
                    sp.dma_start(out_v[before.i], outb[:, before.par]).then_inc(out_st[before.par], 16)

            run_steps(sp, body, FIRST, LOOP, LOOPS, LAST)
            for n in range(2):
                sp.wait_ge(out_st[n], 16 * (STEPS // 2))

        @block.gpsimd
        def _(pool):
            g = nc.gpsimd
            g.memset(nhalf[:], -0.5).then_inc(const_set, 1)
            g.memset(onec[:], 1.0).then_inc(const_set, 1)
            pool.wait_ge(tops_done, 5)
            g.partition_all_reduce(topa[:], tops[:], P, RMAX).then_inc(topall_done, 1)
            pool.wait_ge(const_set, 2)
            pool.wait_ge(row_in, 32)

            def ln(s):
                reach(pool, stats_done, s.i + 1)
                carry(pool)
                g.tensor_scalar(nmean[:], mv[:, :, 0], -1.0, None, ALU.mult)
                g.tensor_scalar(vs[:], mv[:, :, 1], EPS, 1.0, ALU.add, ALU.mult).then_inc(pool_chain, 1)
                pool.wait_ge(pool_chain, 2 * s.i + 1)
                reach(pool, z_done, TILES * s.i)
                g.tensor_tensor(rstd[:], vs[:], nhalf[:], ALU.pow).then_inc(pool_chain, 1)
                pool.wait_ge(pool_chain, 2 * s.i + 2)
                g.tensor_tensor(nmr[:], nmean[:], rstd[:], ALU.mult).then_inc(rstd_done, 1)

            def sums(s):
                pool.wait_ge(x_in[s.par], 16 * (s.turn + 1))
                pool.wait_ge(h_in[s.par], 16 * (s.turn + 1))
                reach(pool, out_done, TILES * s.i)
                pool.wait_ge(z_done, TILES * (s.i + 1))
                g.tensor_tensor(base[:], xin[:, s.par],
                                hin[:, s.par], ALU.add).then_inc(sum_done, 1)
                pool.wait_ge(sum_done, s.i + 1)
                g.tensor_tensor(base[:], base[:],
                                frow[:].unsqueeze(1).to_broadcast([P, TILES, D]), ALU.add).then_inc(base_done, 1)

            def body(s):
                if s.b + 1 < STEPS:
                    ln(s.plus(1))
                if 0 <= s.b < STEPS:
                    sums(s)

            run_steps(pool, body, FIRST, LOOP, LOOPS, LAST)

        @block.scalar
        def _(act):
            s_ = nc.scalar
            act.wait_ge(scales_done, 1)
            for k in range(KC):
                s_.activation(w1h[:, k, :], w1s[:, k, :], ACT.Copy, scale=wsc[:, 0:1]).then_inc(wh_done, 1)
            for k in range(3):
                c = slice(4 * k, 4 * k + 4)
                s_.activation(w2h[:, c, :], w2s[:, c, :], ACT.Copy, scale=wsc[:, 1:2]).then_inc(wh_done, 1)
            act.wait_ge(ubias_done, 1)

            def normalise(s, t):
                if t == 0:
                    act.wait_ge(rstd_done, s.i + 1)
                    reach(act, zT_done, KC * s.i)
                s_.activation(z[:, t, :], hin[:, s.par, t, :], ACT.Identity, bias=nmr[:, t:t + 1],
                              scale=rstd[:, t:t + 1]).then_inc(z_done, 1)

            def zT_high(s, k):
                act.wait_ge(zT_done, KC * s.i + k + 1)
                s_.activation(zh[:, s.par, k, :], zT_ps[:], ACT.Copy, scale=gsc[:, k:k + 1]).then_inc(zTh_done, 1)

            def gelu(s, c):
                act.wait_ge(u_done, FC * s.i + c + 1)
                reach(act, al_done, FC * s.i + c - 1)
                s_.activation(act32[:, c % 2, :], u_ps[c % BANKS][:], ACT.Gelu, bias=ubias[:, c:c + 1],
                              scale=us[:, 0:1]).then_inc(gelu_done, 1)

            def body(s):
                nx = s.plus(1)
                main, norm = 0 <= s.b < STEPS, nx.b < STEPS
                for c in range(FC):
                    if main:
                        gelu(s, c)
                    if norm and 2 <= c < 2 + TILES:
                        normalise(nx, c - 2)
                    if norm and c in (7, 9, 11):
                        zT_high(nx, (c - 7) // 2)

            run_steps(act, body, FIRST, LOOP, LOOPS, LAST)

        @block.vector
        def _(dve):
            v = nc.vector
            dve.wait_ge(w_in, 16 * (KC + 1))
            v.tensor_reduce(tops[:, 0:1], w1s[:].rearrange("p k n -> p (k n)"), AX_X, ALU.max, apply_absolute_value=True).then_inc(tops_done, 1)
            v.tensor_reduce(tops[:, 1:2], w2s[:].rearrange("p k n -> p (k n)"), AX_X, ALU.max, apply_absolute_value=True).then_inc(tops_done, 1)
            dve.wait_ge(col_in, 48)
            for n, c in enumerate((gcol, bcol, fcol)):
                v.tensor_reduce(tops[:, 2 + n:3 + n], c[:], AX_X, ALU.max, apply_absolute_value=True).then_inc(tops_done, 1)
            links = [0]

            def link(ins):
                links[0] += 1
                ins.then_inc(chain, 1)
                dve.wait_ge(chain, links[0])

            dve.wait_ge(topall_done, 1)
            col = lambda n: topa[:, n:n + 1]
            link(v.tensor_scalar(topa[:], topa[:], TINY, None, ALU.max))
            link(v.reciprocal(rec5[:], topa[:]))
            v.tensor_scalar(wsc[:], rec5[:, 0:2], W_TOP, None, ALU.mult).then_inc(scales_done, 1)
            link(v.tensor_scalar(gsc[:], gcol[:], rec5[:, 2:3], TOP / Z_MAX, ALU.mult, ALU.mult))
            link(v.tensor_scalar(bsc[:], rec5[:, 3:4], TOP, None, ALU.mult))
            link(v.tensor_scalar(bh[:], bcol[:], bsc[:, 0:1], None, ALU.mult))
            v.scalar_tensor_tensor(out=bl[:], in0=bcol[:], scalar=bsc[:, 0:1], in1=bh[:],
                                   op0=ALU.mult, op1=ALU.subtract).then_inc(bsplit_done, 1)
            link(v.tensor_scalar(us[:], col(0), col(2), Z_MAX / (TOP * W_TOP), ALU.mult, ALU.mult))
            link(v.tensor_scalar(bs[:], col(0), col(3), 1.0 / (TOP * W_TOP), ALU.mult, ALU.mult))
            link(v.scalar_tensor_tensor(out=ub[:, 0:1], in0=col(2), scalar=Z_MAX, in1=col(3),
                                        op0=ALU.mult, op1=ALU.add))
            link(v.tensor_scalar(ub[:, 0:1], ub[:, 0:1], col(0), float(D), ALU.mult, ALU.mult))
            link(v.tensor_tensor(ub[:, 0:1], ub[:, 0:1], col(4), ALU.add))
            link(v.reciprocal(ub[:, 1:2], ub[:, 0:1]))
            link(v.tensor_scalar(ca[:], ub[:, 1:2], TOP, None, ALU.mult))
            link(v.tensor_scalar(os_[:], ub[:, 0:1], col(1), 1.0 / (TOP * W_TOP), ALU.mult, ALU.mult))
            for k in range(KC):
                dve.wait_ge(wh_done, k + 1)
                v.scalar_tensor_tensor(out=w1l[:, k, :], in0=w1s[:, k, :], scalar=wsc[:, 0:1], in1=w1h[:, k, :],
                                       op0=ALU.mult, op1=ALU.subtract).then_inc(wl_done, 1)
            for k in range(3):
                dve.wait_ge(wh_done, KC + k + 1)
                c = slice(4 * k, 4 * k + 4)
                v.scalar_tensor_tensor(out=w2l[:, c, :], in0=w2s[:, c, :], scalar=wsc[:, 1:2], in1=w2h[:, c, :],
                                       op0=ALU.mult, op1=ALU.subtract).then_inc(wl_done, 1)
            dve.wait_ge(bias_done, 1)
            v.scalar_tensor_tensor(out=ubias[:], in0=zT_ps[:, 0:FC], scalar=bs[:, 0:1], in1=fcol[:],
                                   op0=ALU.mult, op1=ALU.add).then_inc(ubias_done, 1)

            def stats(s):
                dve.wait_ge(h_in[s.par], 16 * (s.turn + 1))
                for t in range(TILES):
                    last = v.bn_stats(stat[:, t, :], hin[:, s.par, t, :])
                last.then_inc(bn_done, 1)
                reach(dve, rstd_done, s.i)
                dve.wait_ge(bn_done, s.i + 1)
                carry(dve)
                for t in range(TILES):
                    last = v.bn_aggr(mv[:, t, :], stat[:, t, :])
                last.then_inc(stats_done, 1)

            def zT_low(s, k):
                dve.wait_ge(zTh_done, KC * s.i + k + 1)
                v.scalar_tensor_tensor(out=zl[:, s.par, k, :], in0=zT_ps[:], scalar=gsc[:, k:k + 1],
                                       in1=zh[:, s.par, k, :], op0=ALU.mult, op1=ALU.subtract).then_inc(zTl_done, 1)

            def split(s, c):
                dve.wait_ge(gelu_done, FC * s.i + c + 1)
                reach(dve, y_part, TILES * (FC * s.i + c + 1 - RING))
                v.tensor_scalar(ah[:, c % RING, :], act32[:, c % 2, :], ca[:, 0:1], None, ALU.mult).then_inc(ah_done, 1)
                dve.wait_ge(ah_done, FC * s.i + c + 1)
                v.scalar_tensor_tensor(out=al[:, c % RING, :], in0=act32[:, c % 2, :], scalar=ca[:, 0:1],
                                       in1=ah[:, c % RING, :], op0=ALU.mult, op1=ALU.subtract).then_inc(al_done, 1)

            def finish(s, t):
                dve.wait_ge(y_part, TILES * (FC * s.i + FC - 1) + t + 1)
                if t == 0:
                    dve.wait_ge(base_done, s.i + 1)
                    reach(dve, out_st[s.par], 16 * s.turn)
                v.scalar_tensor_tensor(out=outb[:, s.par, t, :], in0=y_ps[t][:, 0:D], scalar=os_[:, 0:1],
                                       in1=base[:, t, :], op0=ALU.mult, op1=ALU.add).then_inc(out_done, 1)

            def body(s):
                nx = s.plus(1)
                main, norm = 0 <= s.b < STEPS, nx.b < STEPS
                if s.b < 0:
                    stats(nx)
                for c in range(FC):
                    if main:
                        split(s, c)
                    if c == 1 and s.b >= 1:
                        for t in range(TILES):
                            finish(s.plus(-1), t)
                    if c == 1 and main and norm:
                        stats(nx)
                    if norm and c in (7, 9, 11):
                        zT_low(nx, (c - 7) // 2)

            run_steps(dve, body, FIRST, LOOP, LOOPS, LAST)

        @block.tensor
        def _(pe):
            mm = nc.tensor.matmul
            pe.wait_ge(bsplit_done, 1)
            pe.wait_ge(wl_done, KC)
            for c in range(FC):
                f = slice(P * c, P * c + P)
                for k in range(KC):
                    mm(zT_ps[:, c:c + 1], w1h[:, k, f], bh[:, k:k + 1], start=k == 0, stop=False)
                    mm(zT_ps[:, c:c + 1], w1l[:, k, f], bh[:, k:k + 1], start=False, stop=False)
                    last = mm(zT_ps[:, c:c + 1], w1h[:, k, f], bl[:, k:k + 1], start=False, stop=k == KC - 1)
            last.then_inc(bias_done, 1)
            pe.wait_ge(wl_done, KC + 3)
            pe.wait_ge(row_in, 32)
            pe.wait_ge(ubias_done, 1)

            def zT(s, k):
                if k == 0:
                    pe.wait_ge(z_done, TILES * (s.i + 1))
                reach(pe, zTl_done, KC * s.i + k)
                for t in range(TILES):
                    last = nc.tensor.transpose(zT_ps[:, P * t:P * t + P], z[:, t, P * k:P * k + P], ident[:])
                last.then_inc(zT_done, 1)

            def first(s, c):
                if c == 0:
                    pe.wait_ge(zTl_done, KC * (s.i + 1))
                reach(pe, gelu_done, FC * s.i + c + 1 - BANKS)
                ps, f = u_ps[c % BANKS], slice(P * c, P * c + P)
                for k in range(KC):
                    mm(ps[:], w1h[:, k, f], zh[:, s.par, k, :], start=k == 0, stop=False)
                    mm(ps[:], w1h[:, k, f], zl[:, s.par, k, :], start=False, stop=False)
                    last = mm(ps[:], w1l[:, k, f], zh[:, s.par, k, :], start=False, stop=k == KC - 1)
                last.then_inc(u_done, 1)

            def second(s, c):
                pe.wait_ge(al_done, FC * s.i + c + 1)
                for t in range(TILES):
                    if c == 0:
                        reach(pe, out_done, TILES * (s.i - 1) + t + 1)
                    y, tk = y_ps[t][:, 0:D], slice(P * t, P * t + P)
                    mm(y, ah[:, c % RING, tk], w2h[:, c, :], start=c == 0, stop=False)
                    mm(y, ah[:, c % RING, tk], w2l[:, c, :], start=False, stop=False)
                    last = mm(y, al[:, c % RING, tk], w2h[:, c, :], start=False, stop=c == FC - 1)
                    last.then_inc(y_part, 1)

            def body(s):
                nx, before = s.plus(1), s.plus(-1)
                main, norm = 0 <= s.b < STEPS, nx.b < STEPS
                for c in range(FC):
                    if main:
                        first(s, c)
                    if norm and c in (6, 8, 10):
                        zT(nx, (c - 6) // 2)
                    if c >= LAG and main:
                        second(s, c - LAG)
                    elif c < LAG and s.b >= 1:
                        second(before, FC - LAG + c)

            run_steps(pe, body, FIRST, LOOP, LOOPS, LAST)


C_ID, C_ONE, C_SAME, C_LESS, C_IOTA, C_GRAPH, C_ATT, C_BIAS, C_ALL = 0, 128, 256, 384, 512, 532, 534, 535, 536
SLOT = 32
SPARE = PER_TILE * PICK
LOGIT_TOP = 16.635532
LOGIT_LOW = -88.7228


def constants():
    import numpy as np

    c = np.zeros((P, C_ALL), np.float32)
    p, q = np.arange(P)[:, None], np.arange(P)[None, :]
    c[:, C_ID:C_ID + P] = p == q
    c[:, C_ONE:C_ONE + P] = 1
    c[:, C_SAME:C_SAME + P] = p // NODES == q // NODES
    c[:, C_LESS:C_LESS + P] = (p // NODES == q // NODES) & (q < p)
    r = np.arange(SPARE)[None, :]
    c[:, C_IOTA:C_IOTA + SPARE] = np.where(r // PICK == p // NODES, r % PICK, -1)
    c[:, C_GRAPH:C_GRAPH + PER_TILE] = p // NODES == np.arange(PER_TILE)[None, :]
    c[:, C_ATT] = np.arange(P) % SLOT < SPARE
    c[:, C_BIAS] = np.arange(P) % SLOT == SPARE + PER_TILE
    return c


def mix_phase(nc, x1, g1, b1, wr, br, wq, bq, wk, bk, wv, bv, wo, bo, wm, bm, const_in, h):
    with ExitStack() as ctx:
        a = Pool(nc, ctx, "mix")
        view = lambda t: t.rearrange("(i t g) q d -> i (g q) t d", t=TILES, g=PER_TILE)
        x1_v, h_v = view(x1), view(h)
        row = lambda t: t.rearrange("(a d) -> a d", a=1)
        NW = 5
        Q, K, V, O, M = range(NW)
        U = 3
        G4 = GPS

        wst = a.sb("w_staging", [P, NW, KC, D], F32)
        wh, wl = a.sb("w_high", [P, NW, KC, D], F16), a.sb("w_low", [P, NW, KC, D], F16)
        cst = a.sb("constants", [P, C_ALL], F32)
        id16 = a.sb("ident16", [P, P], F16)
        bst = a.sb("b_staging", [1, NW, D], F32)
        bias_rows, scale_rows = a.sb("bias_rows", [P, 2, D], F16), a.sb("scale_rows", [P, TOK], F16)
        tops, topa = a.sb("tops", [P, 2 * NW + 2], F32), a.sb("tops_all", [P, 2 * NW + 2], F32)
        nb, nr = a.sb("n_bound", [P, 1], F32), a.sb("n_rec", [P, 1], F32)
        nscale = a.sb("n_scale", [P, 1], F32)
        wmax, wrec, wscale = (a.sb(n, [P, NW], F32) for n in ("w_max", "w_rec", "w_scale"))
        brow = a.sb("b_row_scale", [P, 2], F32)
        bound, brec, cscale, evac = (a.sb(n, [P, 3], F32) for n in ("bound", "bound_rec", "out_scale", "evac_scale"))
        sscale = a.sb("score_scale", [P, 1], F32)
        tb = a.sb("t_bound", [P, 3], F32)
        tr = a.sb("t_rec", [P, 1], F32)
        ct = a.sb("t_scale", [P, 1], F32)
        tdown = a.sb("t_down", [P, 1], F32)
        d1 = a.sb("mix_down", [P, 1], F32)
        es = a.sb("e_scale", [P, 3], F32)
        sel2 = a.sb("bias_scale", [P, 2], F32)
        biasm = a.sb("e_bias", [P, D], F32)
        grow, b1row, wrow = (a.sb(n, [P, D], F32) for n in ("g1_row", "b1_row", "wr_row"))
        borow, bmrow = a.sb("bo_row", [P, D], F32), a.sb("bm_row", [P, D], F32)
        bvcol, brcol = a.sb("bv_col", [P, KC], F32), a.sb("br_col", [P, 1], F32)
        nhalf, onec = a.sb("minus_half", [P, TILES], F32), a.sb("one_col", [P, 1], F32)

        xin = a.sb("x1_in", [P, TILES, D], F32)
        h0 = wst[:].rearrange("p w k n -> p (w k n)")[:, 0:U * TILES * D]\
            .rearrange("p (u t d) -> p u t d", u=U, t=TILES)
        n32 = a.sb("normed", [P, TILES, D], F32)
        nh, nl = a.sb("n_high", [P, U, TILES, D], F16), a.sb("n_low", [P, U, TILES, D], F16)
        nT = a.sb("nT", [P, U, KC, 2, TOK], F16)
        kh, kl = a.sb("k_high", [P, U, KC, TOK], F16), a.sb("k_low", [P, U, KC, TOK], F16)
        vh, vl = a.sb("v_high", [P, U, TILES, D], F16), a.sb("v_low", [P, U, TILES, D], F16)
        stat = a.sb("stat", [P, TILES, 6], F32)
        mv = a.sb("mean_var", [P, TILES, 2], F32)
        vs, rstd, nmean, nmr = (a.sb(n, [P, TILES], F32) for n in ("var_eps", "rstd", "minus_mean", "minus_mean_rstd"))
        dots = a.sb("dots", [P, D], F32)
        lg = a.sb("logit", [P, TILES], F32)
        lgb = a.sb("logit_br", [P, TILES], F32)
        lgc = a.sb("logit_clamped", [P, U, TILES], F32)
        ex = a.sb("exp_logit", [P, TILES], F32)
        sg = a.sb("score", [P, U, TILES], F32)
        diag = a.sb("logit_diag", [P, TILES, P], F32)
        cmp_ = a.sb("compared", [P, TILES, 2, P], F32)
        rank, keep, sk = (a.sb(n, [P, TILES], F32) for n in ("rank", "keep", "kept_score"))
        acol = a.sb("mix_scale", [P, U, TILES], F32)
        den, rden, wc = a.sb("pool_den", [P, TILES], F32), a.sb("pool_den_rec", [P, TILES], F32), a.sb("pool_weight", [P, TILES], F32)
        wg, sgk = a.sb("weight_by_graph", [P, TILES, 2], F32), a.sb("kept_by_graph", [P, TILES, 2], F32)
        gh, gl = a.sb("gather_high", [P, TILES, SLOT], F16), a.sb("gather_low", [P, TILES, SLOT], F16)
        ch, cl = a.sb("scatter_high", [P, TILES * (P + SLOT)], F16), a.sb("scatter_low", [P, TILES * (P + SLOT)], F16)
        cT = a.sb("scatterT", [P, 2, TOK], F16)
        nsh, nsl = a.sb("picked_high", [P, KC, P], F16), a.sb("picked_low", [P, KC, P], F16)
        plh, pll = a.sb("pooled_high", [P, KC, TILES, SLOT], F16), a.sb("pooled_low", [P, KC, TILES, SLOT], F16)
        qh, ql = a.sb("q_high", [P, KC, G4, P], F16), a.sb("q_low", [P, KC, G4, P], F16)
        sx = a.sb("scores", [P, G4, NODES], F32)
        smx, ssm, srec = (a.sb(n, [P, G4], F32) for n in ("row_max", "row_sum", "row_rec"))
        pth, ptl = a.sb("pT_high", [P, TILES, P], F16), a.sb("pT_low", [P, TILES, P], F16)
        c32 = a.sb("ctx", [P, KC, TILES, SLOT], F32)
        cxh, cxl = a.sb("ctx_high", [P, KC, P], F16), a.sb("ctx_low", [P, KC, P], F16)
        e32 = a.sb("rows", [P, D], F32)
        eh, el = a.sb("rows_high", [P, D], F16), a.sb("rows_low", [P, D], F16)
        tT = a.sb("scattered", [P, 2, D], F32)
        mg = a.sb("merged", [P, 2, D], F32)
        hb = a.sb("h_out", [P, TILES, D], F32)

        A = a.ps("turn_ps", [P, 2, TOK], F16)
        ring = [a.ps(f"proj_ps{n}", [P, TOK]) for n in range(2)]
        XY = a.ps("chain_ps", [P, 2, TOK])
        X, Y = XY[:, 0, :], XY[:, 1, :]
        T = a.ps("scatter_ps", [P, TOK])
        MX = [a.ps(f"mix_ps{n}", [P, TOK]) for n in range(2)]

        ident = cst[:, C_ID:C_ID + P]
        ones = cst[:, C_ONE:C_ONE + P]
        same, less = cst[:, C_SAME:C_SAME + P], cst[:, C_LESS:C_LESS + P]
        iota = cst[:, C_IOTA:C_IOTA + SPARE]
        graph = cst[:, C_GRAPH:C_GRAPH + PER_TILE]
        slots = lambda t: t[:, 0:TILES * (P + SLOT)].rearrange("p (t c) -> p t c", c=P + SLOT)
        ch4, cl4 = slots(ch), slots(cl)

        sem = a.sem
        w_in, b_in, row_in, col_in, cst_in = (sem(n) for n in ("w_in", "b_in", "row_in", "col_in", "cst_in"))
        const_set, zeroed = sem("const_set"), sem("zeroed")
        tops_done, topall_done, chain, scales_done, rows_done = (
            sem(n) for n in ("tops_done", "topall_done", "chain", "scales_done", "rows_done"))
        wh_done, wl_done = sem("wh_done"), sem("wl_done")
        x_in = sem("x_in")
        h_st = sem("h_st")
        bn_done, stats_done, pool_chain, rstd_done = (
            sem(n) for n in ("bn_done", "stats_done", "pool_chain", "rstd_done"))
        h0_done, z_done, zg_done, n_done, nh_done, nl_done = (
            sem(n) for n in ("h0_done", "z_done", "zg_done", "n_done", "nh_done", "nl_done"))
        dot_done, score_chain, lgb_done, sexp_done, diag_done = (
            sem(n) for n in ("dot_done", "score_chain", "lgb_done", "sexp_done", "diag_done"))
        nT_done, nTe_done = sem("nT_done"), sem("nTe_done")
        kv_done, kvh_done, kvl_done = sem("kv_done"), sem("kvh_done"), sem("kvl_done")
        r_done, cmp_done, rank_chain, rank_done = (
            sem(n) for n in ("r_done", "cmp_done", "rank_chain", "rank_done"))
        cT_done, cTe_done = sem("cT_done"), sem("cTe_done")
        ns_done, nsh_done, nsl_done = sem("ns_done"), sem("nsh_done"), sem("nsl_done")
        q_done, qh_done, ql_done = sem("q_done"), sem("qh_done"), sem("ql_done")
        s_done, smx_done, ssub_done, exp_done, ssum_done, srec_done, p_done = (
            sem(n) for n in ("s_done", "smx_done", "ssub_done", "exp_done", "ssum_done", "srec_done", "p_done"))
        pt_done, pth_done, ptl_done = sem("pt_done"), sem("pth_done"), sem("ptl_done")
        pv_done, ctx_done, cxh_done, cx_done = sem("pv_done"), sem("ctx_done"), sem("cxh_done"), sem("cx_done")
        e_done, e32_done, eh_done, el_done = sem("e_done"), sem("e32_done"), sem("eh_done"), sem("el_done")
        m_done, t_done, te_done, mg_done, h_done = (
            sem(n) for n in ("m_done", "t_done", "te_done", "mg_done", "h_done"))
        NKV = KC + TILES

        FIRST, LOOP, LOOPS, LAST = -3, 2, (STEPS - 5) // U, STEPS
        tail_, main_, proj_, norm_, far_ = (lambda s: s.b >= 1, lambda s: 0 <= s.b < STEPS,
                                            lambda s: 0 <= s.b + 1 < STEPS, lambda s: 0 <= s.b + 2 < STEPS,
                                            lambda s: s.b + 3 < STEPS)
        flags = lambda s: (tail_(s), main_(s), proj_(s), norm_(s), far_(s))

        block = ctx.enter_context(nc.Block())

        @block.sync
        def _(sp):
            sp.dma_start(cst[:], const_in).then_inc(cst_in, 16)
            for n, w in enumerate((wq, wk, wv, wo, wm)):
                sp.dma_start(wst[:, n], w.rearrange("(k p) n -> p k n", p=P)).then_inc(w_in, 16)
            for n, b in enumerate((bq, bk, bv, bo, bm)):
                sp.dma_start(bst[:, n, :], row(b)).then_inc(b_in, 16)
            for t, r in ((grow, g1), (b1row, b1), (wrow, wr), (borow, bo), (bmrow, bm)):
                sp.dma_start(t[:], row(r).to_broadcast([P, D])).then_inc(row_in, 16)
            sp.dma_start(bvcol[:], bv.rearrange("(k p) -> p k", p=P), allow_slow_non_contiguous=True)\
                .then_inc(col_in, 16)
            sp.dma_start(brcol[:], row(br).to_broadcast([P, 1])).then_inc(col_in, 16)
            sp.dma_start(xin[:], x1_v[0]).then_inc(x_in, 16)

            def body(s):
                if s.b >= 1:
                    sp.wait_ge(h_done, TILES * s.i)
                    sp.dma_start(h_v[s.plus(-1).i], hb[:]).then_inc(h_st, 16)
                if -2 <= s.b and s.b + 3 < STEPS:
                    sp.wait_ge(h0_done, TILES * (s.i + 3))
                    sp.dma_start(xin[:], x1_v[s.i + 3]).then_inc(x_in, 16)

            run_steps(sp, body, FIRST, LOOP, LOOPS, LAST, U)
            sp.wait_ge(h_st, 16 * STEPS)

        @block.gpsimd
        def _(pool):
            g = nc.gpsimd
            g.memset(tops[:], 0.0).then_inc(const_set, 1)
            g.memset(nhalf[:], -0.5).then_inc(const_set, 1)
            g.memset(onec[:], 1.0).then_inc(const_set, 1)
            g.memset(scale_rows[:], TOP).then_inc(const_set, 1)
            for t in (bias_rows, gh, gl, ch, cl, plh, pll, c32, qh, ql):
                g.memset(t[:], 0.0).then_inc(zeroed, 1)
            pool.wait_ge(tops_done, 3)
            g.partition_all_reduce(topa[:], tops[:], P, RMAX).then_inc(topall_done, 1)
            pool.wait_ge(const_set, 4)
            pool.wait_ge(rows_done, 1)

            def rstd_of(s, nth):
                n = 2 * s.i + nth
                reach(pool, stats_done, n + 1)
                carry(pool)
                g.tensor_scalar(nmean[:], mv[:, :, 0], -1.0, None, ALU.mult)
                g.tensor_scalar(vs[:], mv[:, :, 1], EPS, 1.0, ALU.add, ALU.mult).then_inc(pool_chain, 1)
                pool.wait_ge(pool_chain, 2 * n + 1)
                if nth:
                    pool.wait_ge(h0_done, TILES * (s.i + 1))
                else:
                    reach(pool, z_done, TILES * s.i)
                g.tensor_tensor(rstd[:], vs[:], nhalf[:], ALU.pow).then_inc(pool_chain, 1)
                pool.wait_ge(pool_chain, 2 * n + 2)
                g.tensor_tensor(nmr[:], nmean[:], rstd[:], ALU.mult).then_inc(rstd_done, 1)

            def affine(s):
                for t in range(TILES):
                    pool.wait_ge(z_done, TILES * s.i + t + 1)
                    g.tensor_tensor(n32[:, t, :], n32[:, t, :],
                                    grow[:], ALU.mult).then_inc(zg_done, 1)
                for t in range(TILES):
                    pool.wait_ge(zg_done, TILES * s.i + t + 1)
                    g.tensor_tensor(n32[:, t, :], n32[:, t, :],
                                    b1row[:], ALU.add).then_inc(n_done, 1)

            def low(s):
                for t in range(TILES):
                    pool.wait_ge(nh_done, TILES * s.i + t + 1)
                    g.tensor_tensor(nl[:, s.par, t, :], n32[:, t, :],
                                    nh[:, s.par, t, :], ALU.subtract)\
                        .then_inc(nl_done, 1)

            def residual(s, t):
                pool.wait_ge(mg_done, TILES * s.i + t + 1)
                if t == 0:
                    reach(pool, h_st, 16 * s.i)
                g.tensor_tensor(hb[:, t, :], mg[:, t % 2, :], h0[:, s.par, t, :], ALU.add).then_inc(h_done, 1)

            def body(s):
                tail, main, proj, norm, far = flags(s)
                prev, ah = s.plus(-1), s.plus(2)
                if tail:
                    for t in range(TILES):
                        residual(prev, t)
                if norm:
                    rstd_of(ah, 1)
                    affine(ah)
                    low(ah)
                if far:
                    rstd_of(s.plus(3), 0)

            run_steps(pool, body, FIRST, LOOP, LOOPS, LAST, U)

        @block.scalar
        def _(act):
            s_ = nc.scalar
            act.wait_ge(scales_done, 1)
            for n in range(NW):
                s_.activation(wh[:, n].rearrange("p k n -> p (k n)"), wst[:, n].rearrange("p k n -> p (k n)"),
                              ACT.Copy, scale=wscale[:, n:n + 1]).then_inc(wh_done, 1)
            act.wait_ge(zeroed, 10)
            act.wait_ge(rows_done, 1)
            act.wait_ge(wl_done, NW)

            def first_norm(s, t):
                if t == 0:
                    act.wait_ge(rstd_done, 2 * s.i + 1)
                    reach(act, h_done, TILES * (s.i - 2))
                s_.activation(h0[:, s.par, t, :], xin[:, t, :], ACT.Identity, bias=nmr[:, t:t + 1],
                              scale=rstd[:, t:t + 1]).then_inc(h0_done, 1)

            def second_norm(s, t):
                if t == 0:
                    act.wait_ge(rstd_done, 2 * s.i + 2)
                    reach(act, nl_done, TILES * s.i)
                    reach(act, dot_done, TILES * s.i)
                s_.activation(n32[:, t, :], h0[:, s.par, t, :], ACT.Identity, bias=nmr[:, t:t + 1],
                              scale=rstd[:, t:t + 1]).then_inc(z_done, 1)

            def n_high(s, t):
                act.wait_ge(n_done, TILES * s.i + t + 1)
                s_.copy(nh[:, s.par, t, :], n32[:, t, :]).then_inc(nh_done, 1)

            def score_exp(s):
                act.wait_ge(lgb_done, s.i + 1)
                s_.activation(ex[:], lgb[:], ACT.Exp, scale=-1.0).then_inc(sexp_done, 1)

            def nT_out(s, k):
                act.wait_ge(nT_done, KC * s.i + k + 1)
                s_.copy(nT[:, s.par, k], A[:]).then_inc(nTe_done, 1)

            def kv_high(s, n):
                act.wait_ge(kv_done, NKV * s.i + n + 1)
                ps = ring[n % 2]
                if n < KC:
                    s_.activation(kh[:, s.par, n, :], ps[:], ACT.Copy, scale=evac[:, K:K + 1]).then_inc(kvh_done, 1)
                else:
                    s_.activation(vh[:, s.par, n - KC, :], ps[:, 0:D], ACT.Copy, scale=evac[:, V:V + 1])\
                        .then_inc(kvh_done, 1)

            def picked_high(s):
                act.wait_ge(ns_done, s.i + 1)
                s_.copy(nsh[:].rearrange("p k c -> p (k c)"), X[:, 0:KC * P]).then_inc(nsh_done, 1)

            def scatter_out(s):
                act.wait_ge(cT_done, s.i + 1)
                s_.copy(cT[:], A[:]).then_inc(cTe_done, 1)

            def q_high(s):
                act.wait_ge(q_done, s.i + 1)
                for c in range(KC):
                    for n in range(4):
                        r, hd = slice(HD * n, HD * n + HD), PICK * (4 * c + n)
                        src = Y[r, P * c:P * c + P].rearrange("p (t c) -> p t c", c=SLOT)[:, :, 0:SPARE]\
                            .rearrange("p t (g c) -> p t g c", g=PER_TILE)
                        dst = qh[r, c, :, hd:hd + PICK].rearrange("p (t g) c -> p t g c", g=PER_TILE)
                        last = s_.activation(dst, src, ACT.Copy, scale=evac[r, Q:Q + 1])
                last.then_inc(qh_done, 1)

            def exp(s):
                act.wait_ge(ssub_done, s.i + 1)
                s_.activation(sx[:], sx[:], ACT.Exp, scale=sscale[:, 0:1]).then_inc(exp_done, 1)

            def pT_high(s):
                act.wait_ge(pt_done, s.i + 1)
                s_.copy(pth[:].rearrange("p t c -> p (t c)"), X).then_inc(pth_done, 1)

            def scattered(s, t):
                act.wait_ge(t_done, TILES * s.i + t + 1)
                reach(act, mg_done, TILES * s.i + t - 1)
                s_.activation(tT[:, t % 2, :], T[:, 0:D], ACT.Copy, scale=tdown[:, 0:1]).then_inc(te_done, 1)

            def body(s):
                tail, main, proj, norm, far = flags(s)
                prev, nx, ah = s.plus(-1), s.plus(1), s.plus(2)
                if proj:
                    nT_out(nx, 0)
                if tail:
                    scattered(prev, 0)
                if main:
                    picked_high(s)
                if proj:
                    nT_out(nx, 1)
                if tail:
                    scattered(prev, 1)
                if proj:
                    nT_out(nx, 2)
                if main:
                    q_high(s)
                if proj:
                    score_exp(nx)
                if tail:
                    scattered(prev, 2)
                if proj:
                    kv_high(nx, 0)
                if tail:
                    scattered(prev, 3)
                if proj:
                    kv_high(nx, 1)
                if norm:
                    for t in range(TILES):
                        first_norm(ah, t)
                if main:
                    scatter_out(s)
                    exp(s)
                if proj:
                    kv_high(nx, 2)
                    kv_high(nx, 3)
                    kv_high(nx, 4)
                if main:
                    pT_high(s)
                if norm:
                    second_norm(ah, 0)
                    second_norm(ah, 1)
                    second_norm(ah, 2)
                    second_norm(ah, 3)
                if proj:
                    kv_high(nx, 5)
                    kv_high(nx, 6)
                if norm:
                    for t in range(TILES):
                        n_high(ah, t)

            run_steps(act, body, FIRST, LOOP, LOOPS, LAST, U)

        @block.vector
        def _(dve):
            v = nc.vector
            dve.wait_ge(const_set, 1)
            dve.wait_ge(w_in, 16 * NW)
            v.tensor_reduce(tops[:, 0:NW], wst[:].rearrange("p w k n -> p w (k n)"), AX_X, ALU.max, apply_absolute_value=True)\
                .then_inc(tops_done, 1)
            dve.wait_ge(b_in, 16 * NW)
            v.tensor_reduce(tops[0:1, NW:2 * NW], bst[:], AX_X, ALU.max, apply_absolute_value=True).then_inc(tops_done, 1)
            dve.wait_ge(row_in, 80)
            v.tensor_reduce(tops[:, 2 * NW:2 * NW + 1], grow[:], AX_X, ALU.max, apply_absolute_value=True)
            v.tensor_reduce(tops[:, 2 * NW + 1:2 * NW + 2], b1row[:], AX_X, ALU.max, apply_absolute_value=True).then_inc(tops_done, 1)
            once = Links(dve, chain)
            link = once.link
            dve.wait_ge(topall_done, 1)
            tw, tbias = topa[:, 0:NW], topa[:, NW:2 * NW]
            link(v.scalar_tensor_tensor(out=nb[:], in0=topa[:, 10:11], scalar=Z_MAX, in1=topa[:, 11:12],
                                        op0=ALU.mult, op1=ALU.add))
            link(v.tensor_scalar(nb[:], nb[:], TINY, None, ALU.max))
            link(v.reciprocal(nr[:], nb[:]))
            link(v.tensor_scalar(nscale[:], nr[:], TOP, None, ALU.mult))
            link(v.tensor_copy(wmax[:], tw))
            link(v.scalar_tensor_tensor(out=wmax[:, 0:2], in0=tbias[:, 0:2], scalar=nr[:, 0:1], in1=tw[:, 0:2],
                                        op0=ALU.mult, op1=ALU.max))
            link(v.tensor_scalar(wmax[:], wmax[:], TINY, None, ALU.max))
            link(v.reciprocal(wrec[:], wmax[:]))
            v.tensor_scalar(wscale[:], wrec[:], W_TOP, None, ALU.mult).then_inc(scales_done, 1)
            link(v.tensor_scalar(brow[:], wrec[:, 0:2], nr[:, 0:1], W_TOP, ALU.mult, ALU.mult))
            link(v.tensor_scalar(bound[:], tw[:, 0:3], nb[:, 0:1], float(D), ALU.mult, ALU.mult))
            link(v.tensor_tensor(bound[:], bound[:], tbias[:, 0:3], ALU.add))
            link(v.tensor_scalar(bound[:], bound[:], TINY, None, ALU.max))
            link(v.reciprocal(brec[:], bound[:]))
            link(v.tensor_scalar(cscale[:], brec[:], TOP, None, ALU.mult))
            link(v.tensor_scalar(evac[:], brec[:], nb[:, 0:1], 1.0 / W_TOP, ALU.mult, ALU.mult))
            link(v.tensor_tensor(evac[:], evac[:], wmax[:, 0:3], ALU.mult))
            link(v.scalar_tensor_tensor(out=sscale[:], in0=bound[:, Q:Q + 1], scalar=RSQRT_HD / (TOP * TOP),
                                        in1=bound[:, K:K + 1], op0=ALU.mult, op1=ALU.mult))
            link(v.tensor_scalar(tb[:, 0:1], tw[:, O:O + 1], bound[:, V:V + 1], float(D), ALU.mult, ALU.mult))
            link(v.tensor_scalar(tb[:, 1:2], tw[:, M:M + 1], nb[:, 0:1], float(D), ALU.mult, ALU.mult))
            link(v.tensor_tensor(tb[:, 2:3], tbias[:, O:O + 1], tbias[:, M:M + 1], ALU.add))
            link(v.tensor_tensor(tb[:, 2:3], tb[:, 2:3], tb[:, 0:1], ALU.add))
            link(v.tensor_tensor(tb[:, 2:3], tb[:, 2:3], tb[:, 1:2], ALU.add))
            link(v.tensor_scalar(tb[:, 2:3], tb[:, 2:3], TINY, None, ALU.max))
            link(v.reciprocal(tr[:], tb[:, 2:3]))
            link(v.tensor_scalar(ct[:], tr[:], TOP, None, ALU.mult))
            link(v.tensor_scalar(tdown[:], tb[:, 2:3], 1.0 / TOP, None, ALU.mult))
            link(v.tensor_scalar(d1[:], nb[:], wmax[:, M:M + 1], 1.0 / (TOP * W_TOP), ALU.mult, ALU.mult))
            link(v.tensor_scalar(es[:, 0:1], bound[:, V:V + 1], wmax[:, O:O + 1], 1.0 / (TOP * W_TOP),
                                 ALU.mult, ALU.mult))
            dve.wait_ge(cst_in, 16)
            link(v.tensor_tensor(es[:, 0:1], es[:, 0:1], d1[:], ALU.subtract))
            link(v.scalar_tensor_tensor(out=es[:, 1:2], in0=es[:, 0:1], scalar=cst[:, C_ATT:C_ATT + 1], in1=d1[:],
                                        op0=ALU.mult, op1=ALU.add))
            link(v.tensor_tensor(es[:, 2:3], es[:, 1:2], ct[:], ALU.mult))
            link(v.tensor_scalar(sel2[:], cst[:, C_ATT:C_ATT + 2], ct[:, 0:1], None, ALU.mult))
            link(v.tensor_scalar(biasm[:], borow[:], sel2[:, 0:1], None, ALU.mult))
            link(v.scalar_tensor_tensor(out=biasm[:], in0=bmrow[:], scalar=sel2[:, 1:2], in1=biasm[:],
                                        op0=ALU.mult, op1=ALU.add))
            link(v.tensor_scalar(grow[:], grow[:], nscale[:, 0:1], None, ALU.mult))
            link(v.tensor_scalar(b1row[:], b1row[:], nscale[:, 0:1], None, ALU.mult))
            link(v.tensor_scalar(wrow[:], wrow[:], nb[:, 0:1], 1.0 / TOP, ALU.mult, ALU.mult))
            dve.wait_ge(col_in, 32)
            link(v.tensor_scalar(bvcol[:], bvcol[:], cscale[:, V:V + 1], None, ALU.mult))
            dve.wait_ge(zeroed, 10)
            link(v.tensor_copy(id16[:], ident))
            for n in range(2):
                link(v.tensor_scalar(bias_rows[0:1, n, :], bst[:, n, :], brow[0:1, n:n + 1], None, ALU.mult))
                link(v.scalar_tensor_tensor(out=bias_rows[32:33, n, :], in0=bst[:, n, :], scalar=brow[0:1, n:n + 1],
                                            in1=bias_rows[0:1, n, :], op0=ALU.mult, op1=ALU.subtract))
            v.tensor_copy(ssm[:], cst[:, 0:G4]).then_inc(rows_done, 1)
            for n in range(NW):
                dve.wait_ge(wh_done, n + 1)
                v.scalar_tensor_tensor(out=wl[:, n].rearrange("p k n -> p (k n)"),
                                       in0=wst[:, n].rearrange("p k n -> p (k n)"), scalar=wscale[:, n:n + 1],
                                       in1=wh[:, n].rearrange("p k n -> p (k n)"),
                                       op0=ALU.mult, op1=ALU.subtract).then_inc(wl_done, 1)
            dve.wait_ge(const_set, 4)

            def stats(s, nth):
                n = 2 * s.i + nth
                if nth:
                    dve.wait_ge(h0_done, TILES * (s.i + 1))
                else:
                    dve.wait_ge(x_in, 16 * (s.i + 1))
                reach(dve, stats_done, n)
                for t in range(TILES):
                    last = v.bn_stats(stat[:, t, :], h0[:, s.par, t, :] if nth else xin[:, t, :])
                last.then_inc(bn_done, 1)
                reach(dve, rstd_done, n)
                dve.wait_ge(bn_done, n + 1)
                carry(dve)
                for t in range(TILES):
                    last = v.bn_aggr(mv[:, t, :], stat[:, t, :])
                last.then_inc(stats_done, 1)

            def dot(s):
                for t in range(TILES):
                    dve.wait_ge(n_done, TILES * s.i + t + 1)
                    reach(dve, dot_done, TILES * s.i + t)
                    v.tensor_tensor_reduce(out=dots[:], in0=n32[:, t, :], in1=wrow[:], scale=1.0, scalar=0.0,
                                           op0=ALU.mult, op1=ALU.add, accum_out=lg[:, t:t + 1]).then_inc(dot_done, 1)
                dve.wait_ge(dot_done, TILES * (s.i + 1))
                v.tensor_scalar(lgb[:], lg[:], brcol[:, 0:1], None, ALU.add).then_inc(lgb_done, 1)
                dve.wait_ge(lgb_done, s.i + 1)
                links = Links(dve, score_chain)
                links.start(3 * s.i)
                links.link(v.tensor_scalar(lgc[:, s.par, :], lgb[:], LOGIT_TOP, LOGIT_LOW, ALU.min, ALU.max))
                reach(dve, r_done, s.i)
                v.tensor_tensor(diag[:], ident.unsqueeze(1).to_broadcast([P, TILES, P]),
                                lgc[:, s.par, :].unsqueeze(2).to_broadcast([P, TILES, P]), ALU.mult)\
                    .then_inc(diag_done, 1)
                dve.wait_ge(sexp_done, s.i + 1)
                links.link(v.tensor_scalar(ex[:], ex[:], 1.0, None, ALU.add))
                links.link(v.reciprocal(sg[:, s.par, :], ex[:]))

            def kv_low(s, n):
                dve.wait_ge(kvh_done, NKV * s.i + n + 1)
                ps = ring[n % 2]
                if n < KC:
                    v.scalar_tensor_tensor(out=kl[:, s.par, n, :], in0=ps[:], scalar=evac[:, K:K + 1],
                                           in1=kh[:, s.par, n, :], op0=ALU.mult, op1=ALU.subtract)\
                        .then_inc(kvl_done, 1)
                else:
                    v.scalar_tensor_tensor(out=vl[:, s.par, n - KC, :], in0=ps[:, 0:D], scalar=evac[:, V:V + 1],
                                           in1=vh[:, s.par, n - KC, :], op0=ALU.mult, op1=ALU.subtract)\
                        .then_inc(kvl_done, 1)

            def picked_low(s):
                dve.wait_ge(nsh_done, s.i + 1)
                v.tensor_tensor(nsl[:].rearrange("p k c -> p (k c)"), X[:, 0:KC * P],
                                nsh[:].rearrange("p k c -> p (k c)"), ALU.subtract).then_inc(nsl_done, 1)
                dve.wait_ge(nsl_done, 2 * s.i + 1)
                for to, of in ((plh, nsh), (pll, nsl)):
                    last = v.tensor_copy(to[:, :, :, SPARE:SPARE + PER_TILE],
                                         of[:].rearrange("p k (t c) -> p k t c", c=SLOT)[:, :, :, SPARE:SPARE + PER_TILE])
                last.then_inc(nsl_done, 1)

            def q_low(s):
                dve.wait_ge(qh_done, s.i + 1)
                for c in range(KC):
                    for n in range(4):
                        r, hd = slice(HD * n, HD * n + HD), PICK * (4 * c + n)
                        src = Y[r, P * c:P * c + P].rearrange("p (t c) -> p t c", c=SLOT)[:, :, 0:SPARE]\
                            .rearrange("p t (g c) -> p t g c", g=PER_TILE)
                        at = lambda t: t[r, c, :, hd:hd + PICK].rearrange("p (t g) c -> p t g c", g=PER_TILE)
                        last = v.scalar_tensor_tensor(out=at(ql), in0=src, scalar=evac[r, Q:Q + 1], in1=at(qh),
                                                      op0=ALU.mult, op1=ALU.subtract)
                last.then_inc(ql_done, 1)

            def score_max(s):
                dve.wait_ge(s_done, s.i + 1)
                x3 = X.rearrange("p (g k) -> p g k", g=G4)
                v.tensor_reduce(smx[:], x3, AX_X, ALU.max).then_inc(smx_done, 1)
                dve.wait_ge(smx_done, s.i + 1)
                reach(dve, pt_done, s.i)
                v.tensor_tensor(sx[:], x3, smx[:].unsqueeze(2).to_broadcast([P, G4, NODES]), ALU.subtract)\
                    .then_inc(ssub_done, 1)

            def score_norm(s):
                dve.wait_ge(exp_done, s.i + 1)
                v.tensor_reduce(ssm[:], sx[:], AX_X, ALU.add).then_inc(ssum_done, 1)
                dve.wait_ge(ssum_done, s.i + 1)
                v.reciprocal(srec[:], ssm[:]).then_inc(srec_done, 1)
                dve.wait_ge(srec_done, s.i + 1)
                v.tensor_tensor(sx[:], sx[:], srec[:].unsqueeze(2).to_broadcast([P, G4, NODES]), ALU.mult)\
                    .then_inc(p_done, 1)

            def compare(s):
                dve.wait_ge(r_done, s.i + 1)
                for t in range(TILES):
                    rt = Y[:, P * t:P * t + P]
                    v.scalar_tensor_tensor(out=cmp_[:, t, 0, :], in0=rt, scalar=lgc[:, s.par, t:t + 1], in1=same,
                                           op0=ALU.is_lt, op1=ALU.mult)
                    last = v.scalar_tensor_tensor(out=cmp_[:, t, 1, :], in0=rt, scalar=lgc[:, s.par, t:t + 1],
                                                  in1=less, op0=ALU.is_equal, op1=ALU.mult)
                last.then_inc(cmp_done, 1)

            def lists(s):
                dve.wait_ge(cmp_done, s.i + 1)
                links = Links(dve, rank_chain)
                links.start(5 * s.i)
                ln = links.link
                v.tensor_scalar(den[:], T[:, 0:TILES], 1e-6, None, ALU.add)
                ln(v.tensor_reduce(rank[:], cmp_[:].rearrange("p t a c -> p t (a c)"), AX_X, ALU.add))
                reach(dve, ns_done, s.i)
                reach(dve, cT_done, s.i)
                v.tensor_tensor(gh[:, :, 0:SPARE], iota.unsqueeze(1).to_broadcast([P, TILES, SPARE]),
                                rank[:].unsqueeze(2).to_broadcast([P, TILES, SPARE]), ALU.is_equal)
                v.reciprocal(rden[:], den[:])
                ln(v.tensor_scalar(keep[:], rank[:], float(PICK), None, ALU.is_ge))
                v.tensor_copy(ch4[:, :, 0:SPARE], gh[:, :, 0:SPARE])
                v.tensor_copy(ch4[:, :, SPARE + 2:SPARE + 3], keep[:].unsqueeze(2))
                v.tensor_scalar(acol[:, s.par, :], keep[:], d1[:, 0:1], None, ALU.mult)
                v.tensor_tensor(sk[:], sg[:, s.par, :], keep[:], ALU.mult)
                ln(v.tensor_tensor(wc[:], sg[:, s.par, :], rden[:], ALU.mult))
                g2_ = graph.unsqueeze(1).to_broadcast([P, TILES, PER_TILE])
                two = lambda c: c.unsqueeze(2).to_broadcast([P, TILES, PER_TILE])
                v.tensor_tensor(wg[:], two(wc[:]), g2_, ALU.mult)
                ln(v.tensor_tensor(sgk[:], two(sk[:]), g2_, ALU.mult))
                v.tensor_copy(gh[:, :, SPARE:SPARE + 2], wg[:])
                ln(v.tensor_copy(ch4[:, :, SPARE:SPARE + 2], sgk[:]))
                v.tensor_tensor(gl[:, :, SPARE:SPARE + 2], wg[:], gh[:, :, SPARE:SPARE + 2], ALU.subtract)
                v.tensor_tensor(cl4[:, :, SPARE:SPARE + 2], sgk[:], ch4[:, :, SPARE:SPARE + 2], ALU.subtract)\
                    .then_inc(rank_done, 1)

            def pT_low(s):
                dve.wait_ge(pth_done, s.i + 1)
                v.tensor_tensor(ptl[:].rearrange("p t c -> p (t c)"), X, pth[:].rearrange("p t c -> p (t c)"),
                                ALU.subtract).then_inc(ptl_done, 1)

            def context(s):
                dve.wait_ge(pv_done, s.i + 1)
                W4 = 4 * PICK
                for n in range(4):
                    r = slice(HD * n, HD * n + HD)
                    own = slice(PICK * n, PICK * n + PICK)
                    blocks = XY[r, :, 0:TILES * KC * W4].rearrange("p y (t c w) -> p t c y w", t=TILES, c=KC)
                    for c in range(KC):
                        dst = c32[r, c, :, 0:SPARE].rearrange("p t (g w) -> p t g w", g=PER_TILE)
                        last = v.tensor_scalar(dst, blocks[:, :, c, :, own], bvcol[r, c:c + 1], None, ALU.add)
                last.then_inc(ctx_done, 1)
                dve.wait_ge(ctx_done, s.i + 1)
                f = c32[:].rearrange("p k t c -> p (k t c)")
                v.tensor_copy(cxh[:].rearrange("p k c -> p (k c)"), f).then_inc(cxh_done, 1)
                dve.wait_ge(cxh_done, s.i + 1)
                v.tensor_tensor(cxl[:].rearrange("p k c -> p (k c)"), f, cxh[:].rearrange("p k c -> p (k c)"),
                                ALU.subtract).then_inc(cx_done, 1)

            def rows(s):
                dve.wait_ge(e_done, s.i + 1)
                v.scalar_tensor_tensor(out=e32[:], in0=X[:, 0:D], scalar=es[:, 2:3], in1=biasm[:],
                                       op0=ALU.mult, op1=ALU.add).then_inc(e32_done, 1)
                dve.wait_ge(e32_done, s.i + 1)
                v.tensor_copy(eh[:], e32[:]).then_inc(eh_done, 1)
                dve.wait_ge(eh_done, s.i + 1)
                v.tensor_tensor(el[:], e32[:], eh[:], ALU.subtract).then_inc(el_done, 1)

            def merge(s, t):
                dve.wait_ge(m_done, TILES * s.i + t + 1)
                dve.wait_ge(te_done, TILES * s.i + t + 1)
                reach(dve, h_done, TILES * s.i + t - 1)
                v.scalar_tensor_tensor(out=mg[:, t % 2, :], in0=MX[t % 2][:, 0:D], scalar=acol[:, s.par, t:t + 1],
                                       in1=tT[:, t % 2, :], op0=ALU.mult, op1=ALU.add).then_inc(mg_done, 1)

            def body(s):
                tail, main, proj, norm, far = flags(s)
                prev, nx, ah = s.plus(-1), s.plus(1), s.plus(2)
                if tail:
                    merge(prev, 0)
                if main:
                    picked_low(s)
                if tail:
                    merge(prev, 1)
                if proj:
                    dot(nx)
                if tail:
                    merge(prev, 2)
                if main:
                    q_low(s)
                if proj:
                    kv_low(nx, 0)
                if tail:
                    merge(prev, 3)
                if proj:
                    kv_low(nx, 1)
                    compare(nx)
                if main:
                    score_max(s)
                if norm:
                    stats(ah, 1)
                if main:
                    score_norm(s)
                if proj:
                    kv_low(nx, 2)
                    kv_low(nx, 3)
                    kv_low(nx, 4)
                if main:
                    pT_low(s)
                if proj:
                    kv_low(nx, 5)
                if main:
                    context(s)
                if proj:
                    kv_low(nx, 6)
                    lists(nx)
                if main:
                    rows(s)
                if far:
                    stats(s.plus(3), 0)

            run_steps(dve, body, FIRST, LOOP, LOOPS, LAST, U)

        @block.tensor
        def _(pe):
            mm = nc.tensor.matmul
            pe.wait_ge(wl_done, NW)
            pe.wait_ge(rows_done, 1)

            def three(out, sh, sl, mh, ml, first, last):
                mm(out, sh, mh, start=first, stop=False)
                mm(out, sl, mh, start=False, stop=False)
                return mm(out, sh, ml, start=False, stop=last)

            def picked(s):
                pe.wait_ge(rank_done, s.i + 1)
                reach(pe, e32_done, s.i)
                for t in range(TILES):
                    for k in range(KC):
                        f = slice(P * k, P * k + P)
                        out = X[:, P * k + SLOT * t:P * k + SLOT * t + SLOT]
                        last = three(out, nh[:, s.par, t, f], nl[:, s.par, t, f], gh[:, t, :], gl[:, t, :], True, True)
                last.then_inc(ns_done, 1)

            def turn_scatter(s):
                reach(pe, nTe_done, KC * (s.i + 2 if s.b + 1 < STEPS else s.i + 1))
                for n, c in enumerate((ch, cl)):
                    for t in range(TILES):
                        last = nc.tensor.transpose(A[:, n, P * t:P * t + P], c[:, P * t:P * t + P], id16[:])
                last.then_inc(cT_done, 1)

            def nT_of(s, k):
                if k == 0:
                    pe.wait_ge(nl_done, TILES * (s.i + 1))
                    reach(pe, cTe_done, s.i - 1)
                reach(pe, nTe_done, KC * s.i + k)
                for n, c in enumerate((nh, nl)):
                    for t in range(TILES):
                        last = nc.tensor.transpose(A[:, n, P * t:P * t + P], c[:, s.par, t, P * k:P * k + P], id16[:])
                last.then_inc(nT_done, 1)

            def kv(s, n):
                reach(pe, kvl_done, NKV * s.i + max(n - 1, 0))
                ps = ring[n % 2]
                if n < KC:
                    c = slice(P * n, P * n + P)
                    mm(ps[:], bias_rows[:, K, c], scale_rows[:], start=True, stop=False)
                    for k in range(KC):
                        if n == 0:
                            pe.wait_ge(nTe_done, KC * s.i + k + 1)
                        last = three(ps[:], wh[:, K, k, c], wl[:, K, k, c], nT[:, s.par, k, 0, :],
                                     nT[:, s.par, k, 1, :], False, k == KC - 1)
                else:
                    c = slice(P * (n - KC), P * (n - KC) + P)
                    for k in range(KC):
                        last = three(ps[:, 0:D], nT[:, s.par, k, 0, c], nT[:, s.par, k, 1, c], wh[:, V, k, :],
                                     wl[:, V, k, :], k == 0, k == KC - 1)
                last.then_inc(kv_done, 1)

            def queries(s):
                pe.wait_ge(nsl_done, 2 * s.i + 1)
                reach(pe, ctx_done, s.i)
                for n in range(KC):
                    c = slice(P * n, P * n + P)
                    mm(Y[:, c], bias_rows[:, Q, c], scale_rows[:, 0:P], start=True, stop=False)
                    for k in range(KC):
                        last = three(Y[:, c], wh[:, Q, k, c], wl[:, Q, k, c], nsh[:, k, :], nsl[:, k, :],
                                     False, k == KC - 1)
                last.then_inc(q_done, 1)

            def scores(s):
                pe.wait_ge(ql_done, s.i + 1)
                pe.wait_ge(nsl_done, 2 * s.i + 2)
                pe.wait_ge(kvl_done, NKV * (s.i + 1))
                for g in range(G4):
                    c = slice(NODES * g, NODES * g + NODES)
                    for k in range(KC):
                        last = three(X[:, c], qh[:, k, g, :], ql[:, k, g, :], kh[:, s.par, k, c], kl[:, s.par, k, c],
                                     k == 0, k == KC - 1)
                last.then_inc(s_done, 1)

            def spread(s):
                pe.wait_ge(diag_done, s.i + 1)
                pe.wait_ge(score_chain, 3 * (s.i + 1))
                reach(pe, ql_done, s.i)
                reach(pe, te_done, TILES * (s.i - 1))
                mm(T[:, 0:TILES], same, sg[:, s.par, :], start=True, stop=True)
                mm(Y, ones, diag[:].rearrange("p t c -> p (t c)"), start=True, stop=True).then_inc(r_done, 1)

            def turn_p(s):
                pe.wait_ge(p_done, s.i + 1)
                f = sx[:].rearrange("p g k -> p (g k)")
                for t in range(TILES):
                    last = nc.tensor.transpose(X[:, P * t:P * t + P], f[:, P * t:P * t + P], ident)
                last.then_inc(pt_done, 1)

            def attend(s):
                pe.wait_ge(ptl_done, s.i + 1)
                if s.b + 1 < STEPS:
                    pe.wait_ge(cmp_done, s.i + 2)
                W4 = 4 * PICK
                for g in range(G4):
                    t, r = g // PER_TILE, slice(NODES * (g % PER_TILE), NODES * (g % PER_TILE) + NODES)
                    for c in range(KC):
                        at = W4 * (KC * t + c)
                        out = XY[:, g % PER_TILE, at:at + W4]
                        f = slice(P * c, P * c + P)
                        q = slice(W4 * c, W4 * c + W4)
                        last = three(out, vh[r, s.par, t, f], vl[r, s.par, t, f], pth[r, t, q], ptl[r, t, q], True, True)
                last.then_inc(pv_done, 1)

            def make_rows(s):
                pe.wait_ge(cx_done, s.i + 1)
                pl = lambda t, k: t[:, k].rearrange("p t c -> p (t c)")
                for k in range(KC):
                    three(X[:, 0:D], cxh[:, k, :], cxl[:, k, :], wh[:, O, k, :], wl[:, O, k, :], k == 0, False)
                for k in range(KC):
                    last = three(X[:, 0:D], pl(plh, k), pl(pll, k), wh[:, M, k, :], wl[:, M, k, :],
                                 False, k == KC - 1)
                last.then_inc(e_done, 1)

            def mix(s, t):
                reach(pe, mg_done, TILES * s.i + t - 1)
                c = slice(P * t, P * t + P)
                for k in range(KC):
                    last = three(MX[t % 2][:, 0:D], nT[:, s.par, k, 0, c], nT[:, s.par, k, 1, c], wh[:, M, k, :],
                                 wl[:, M, k, :], k == 0, k == KC - 1)
                last.then_inc(m_done, 1)

            def scatter(s, t):
                if t == 0:
                    pe.wait_ge(el_done, s.i + 1)
                    pe.wait_ge(cTe_done, s.i + 1)
                    if s.b + 1 < STEPS:
                        pe.wait_ge(rank_done, s.i + 2)
                reach(pe, te_done, TILES * s.i + t)
                c = slice(P * t, P * t + P)
                three(T[:, 0:D], cT[:, 0, c], cT[:, 1, c], eh[:], el[:], True, True).then_inc(t_done, 1)

            def body(s):
                tail, main, proj, norm, far = flags(s)
                prev, nx = s.plus(-1), s.plus(1)
                if proj:
                    nT_of(nx, 0)
                if tail:
                    scatter(prev, 0)
                if main:
                    picked(s)
                if proj:
                    nT_of(nx, 1)
                if tail:
                    mix(prev, 2)
                    scatter(prev, 1)
                if proj:
                    nT_of(nx, 2)
                if main:
                    queries(s)
                if tail:
                    mix(prev, 3)
                    scatter(prev, 2)
                if proj:
                    kv(nx, 0)
                if tail:
                    scatter(prev, 3)
                if proj:
                    kv(nx, 1)
                if main:
                    turn_scatter(s)
                if proj:
                    spread(nx)
                if main:
                    scores(s)
                if proj:
                    kv(nx, 2)
                    kv(nx, 3)
                    kv(nx, 4)
                if main:
                    turn_p(s)
                if proj:
                    kv(nx, 5)
                if main:
                    attend(s)
                if proj:
                    kv(nx, 6)
                if main:
                    mix(s, 0)
                    make_rows(s)
                    mix(s, 1)

            run_steps(pe, body, FIRST, LOOP, LOOPS, LAST, U)


def build(nc, x, adj, gnn, attention, mlp, const_in, out):
    x1 = nc.dram_tensor("x1_dram", (GRAPHS, NODES, D), F32, kind="Internal").ap()
    h = nc.dram_tensor("h_dram", (GRAPHS, NODES, D), F32, kind="Internal").ap()
    gnn_phase(nc, x, adj, *gnn, x1)
    mix_phase(nc, x1, *attention, const_in, h)
    mlp_phase(nc, h, x1, *mlp, const_in[:, C_ID:C_ID + P], out)


GNN_INS = ["Wq", "bq", "Wk", "bk", "Wv", "bv", "beta"]
ATTENTION_INS = ["g1", "b1", "Wr", "br", "Wq", "bq", "Wk", "bk", "Wv", "bv", "Wo", "bo", "Wm", "bm"]
MLP_INS = ["g2", "b2", "W1", "bf1", "W2", "bf2"]


def kernel(**inputs):
    import numpy as np
    import concourse.bacc as bacc
    from concourse.bass_utils import run_bass_kernel_spmd

    nc = bacc.Bacc("TRN2", target_bir_lowering=False, num_devices=1)
    arrays = {}

    def take(name, array):
        array = np.ascontiguousarray(np.atleast_1d(array))
        arrays[f"in_{name}_dram"] = array
        return nc.dram_tensor(f"in_{name}_dram", array.shape, mybir.dt.from_np(array.dtype),
                              kind="ExternalInput").ap()

    x, adj = take("x", inputs["x"]), take("adj", inputs["adj"])
    gnn = [take(f"L0_gnn_{n}", inputs[f"L0_gnn_{n}"]) for n in GNN_INS]
    attention, mlp = ([take(f"L0_ffn_{n}", inputs[f"L0_ffn_{n}"]) for n in names] for names in (ATTENTION_INS, MLP_INS))
    const_in = take("constants", constants())
    out = nc.dram_tensor("out_0_dram", (GRAPHS, NODES, D), F32, kind="ExternalOutput").ap()
    build(nc, x, adj, gnn, attention, mlp, const_in, out)
    result = run_bass_kernel_spmd(nc, [arrays], core_ids=[0])
    return result.results[0]["out_0_dram"]
```

```python
from contextlib import ExitStack

import concourse.bass as bass
from concourse import mybir

ALU = mybir.AluOpType
ACT = mybir.ActivationFunctionType
F32 = mybir.dt.float32
F16 = mybir.dt.float16
AX_X = mybir.AxisListType.X
RMAX = bass.bass_isa.ReduceOp.max

P = 128
GRAPHS, NODES, D = 128, 64, 384
HEADS, HD = 12, 32
F = 1536
KC = D // P
FC = F // P
PER_TILE = P // NODES
TILES = 4
TOK = TILES * P
GPS = TILES * PER_TILE
STEPS = GRAPHS // GPS
PICK = max(1, int(round(0.15 * NODES)))
EPS = 1e-5
MASKED = -9000000000000000.0
Z_SCALE = 1024.0
Z_MAX = float(D) ** 0.5 * 1.01
TOP = 32768.0
W_TOP = 2048.0
TINY = 1e-20
RSQRT_HD = float(HD) ** -0.5
VW = HD + 1


class Step:

    def __init__(self, m, b, u=2):
        self.m, self.b, self.u = m, b, u
        self.par = b % u
        self.i = b if isinstance(m, int) else u * m + b
        self.turn = b // u if isinstance(m, int) else m + b // u

    def plus(self, n):
        return Step(self.m, self.b + n, self.u)


def reach(eng, sem, value):
    if not (isinstance(value, int) and value <= 0):
        eng.wait_ge(sem, value)


def carry(eng):
    eng.nop(nofuse=True)


class Links:

    def __init__(self, eng, sem):
        self.eng, self.sem, self.base, self.n = eng, sem, 0, 0

    def start(self, base):
        self.base, self.n = base, 0

    def link(self, ins):
        self.n += 1
        ins.then_inc(self.sem, 1)
        self.eng.wait_ge(self.sem, self.base + self.n)


def run_steps(eng, body, first, loop_first, loops, last, u=2):
    for b in range(first, loop_first):
        body(Step(0, b, u))
    with eng.Fori(0, loops) as m:
        for n in range(u):
            body(Step(m, loop_first + n, u))
    for b in range(loop_first + u * loops, last + 1):
        body(Step(0, b, u))


class Memory:

    def __init__(self, nc, ctx, tag):
        self.nc, self.ctx, self.tag = nc, ctx, tag

    def sb(self, name, shape, dt):
        return self.ctx.enter_context(self.nc.sbuf_tensor(f"{self.tag}_{name}", shape, dt))

    def ps(self, name, shape, dt=F32):
        return self.ctx.enter_context(self.nc.psum_tensor(f"{self.tag}_{name}", shape, dt))

    def sem(self, name):
        return self.ctx.enter_context(self.nc.semaphore(f"{self.tag}_{name}"))


def gnn_phase(nc, x, adj, wq, bq, wk, bk, wv, bv, beta, x1):
    with ExitStack() as ctx:
        a = Memory(nc, ctx, "gnn")
        x_v = x.rearrange("(i t g) q d -> i (g q) t d", t=TILES, g=PER_TILE)
        x1_v = x1.rearrange("(i t g) q d -> i (g q) t d", t=TILES, g=PER_TILE)
        adj_v = adj.rearrange("(i g) q k -> i q g k", g=GPS)

        NW = 3
        wst = a.sb("w_staging", [P, NW, KC, D], F32)
        bst = a.sb("b_staging", [1, 2, D], F32)
        wh = a.sb("w_high", [P, NW, KC, D], F16)
        wl = a.sb("w_low", [P, NW, KC, D], F16)
        bias_rows = a.sb("bias_rows", [P, 2, D], F16)
        scale_rows = a.sb("scale_rows", [P, TOK], F16)
        tops = a.sb("tops", [P, 2, NW], F32)
        topa = a.sb("tops_all", [P, 2, NW], F32)
        wmax = a.sb("w_max", [P, NW], F32)
        wrec = a.sb("w_rec", [P, NW], F32)
        wscale = a.sb("w_scale", [P, NW], F32)
        bound = a.sb("bound", [P, NW], F32)
        brec = a.sb("bound_rec", [P, NW], F32)
        cscale = a.sb("out_scale", [P, NW], F32)
        evac = a.sb("evac_scale", [P, NW], F32)
        sscale = a.sb("score_scale", [P, 1], F32)
        ident = a.sb("ident", [P, P], F32)
        bvrow = a.sb("bv_row", [P, D], F32)
        betac = a.sb("beta_col", [P, 1], F32)
        nhalf = a.sb("minus_half", [P, TILES], F32)

        xin = a.sb("x_in", [P, 2, TILES, D], F32)
        xres = a.sb("x_plus_bv", [P, 2, TILES, D], F32)
        z = a.sb("z", [P, TILES, D], F32)
        stat = a.sb("stat", [P, TILES, 6], F32)
        mv = a.sb("mean_var", [P, TILES, 2], F32)
        vs = a.sb("var_scaled", [P, TILES], F32)
        rstd = a.sb("rstd", [P, TILES], F32)
        nmean = a.sb("minus_mean", [P, TILES], F32)
        nmr = a.sb("minus_mean_rstd", [P, TILES], F32)
        zh = a.sb("zT_high", [P, KC, TOK], F16)
        zl = a.sb("zT_low", [P, KC, TOK], F16)
        qh = a.sb("q_high", [P, 2, KC, 2, GPS, 2, NODES], F16)
        ql = a.sb("q_low", [P, 2, KC, 2, GPS, 2, NODES], F16)
        kh = a.sb("k_high", [P, 2, KC, TOK], F16)
        kl = a.sb("k_low", [P, 2, KC, TOK], F16)
        vh = a.sb("v_high", [P, 2, TILES, HEADS, VW], F16)
        vl = a.sb("v_low", [P, 2, TILES, HEADS, VW], F16)
        adjb = a.sb("adj_in", [P, GPS * NODES], F32)
        edge = a.sb("beta_adj", [P, GPS * NODES], F32)
        neg = a.sb("mask_neg", [P, GPS * NODES], F32)
        mask = a.sb("mask_add", [P, 2, GPS * NODES], F32)
        NJ = HEADS // 2
        sc = a.sb("scores", [P, 2, NJ, P], F32)
        mx = a.sb("row_max", [P, 2, HEADS], F32)
        pth = a.sb("pT_high", [P, 2, NJ, P], F16)
        ptl = a.sb("pT_low", [P, 2, NJ, P], F16)
        rs = a.sb("row_rec", [P, 2, HEADS], F32)
        on = a.sb("out_norm", [P, 2, D], F32)
        x1b = a.sb("x1_out", [P, 2, TILES, D], F32)

        zT_ps = a.ps("zT_ps", [P, TOK])
        pr_ps = [a.ps(f"proj_ps{n}", [P, TOK]) for n in range(2)]
        s_ps = a.ps("score_ps", [P, 2 * 512])
        p_ps = a.ps("pT_ps", [P, 2 * 512])
        o_ps = a.ps("pv_ps", [P, 512])
        s3 = s_ps[:, 0:NJ * P].rearrange("p (j c) -> p j c", j=NJ)
        p3 = p_ps[:, 0:NJ * P].rearrange("p (j c) -> p j c", j=NJ)
        o3 = o_ps[:, 0:HEADS * VW].rearrange("p (h c) -> p h c", h=HEADS)

        sem = a.sem
        w_in, b_in, row_in = [sem(f"w_in{n}") for n in range(NW)], sem("b_in"), sem("row_in")
        const_set, ident_set = sem("const_set"), sem("ident_set")
        zeroed, zeroed_dve = sem("zeroed"), sem("zeroed_dve")
        tops_done, topall_done = sem("tops_done"), sem("topall_done")
        chain, scales_done = sem("chain"), sem("scales_done")
        wh_done, wl_done = sem("wh_done"), sem("wl_done")
        x_in = [sem("x_in0"), sem("x_in1")]
        adj_in = sem("adj_in")
        neg_done, mask_done = sem("neg_done"), sem("mask_done")
        bn_done, stats_done = sem("bn_done"), sem("stats_done")
        pool_chain, rstd_done, xres_done = sem("pool_chain"), sem("rstd_done"), sem("xres_done")
        z_done, zT_done, zTh_done, zTl_done = sem("z_done"), sem("zT_done"), sem("zTh_done"), sem("zTl_done")
        proj_done, projh_done, projl_done = sem("proj_done"), sem("projh_done"), sem("projl_done")
        s_done, s_evac, mx_done, sub_done, exp_done = (
            sem("s_done"), sem("s_evac"), sem("mx_done"), sem("sub_done"), sem("exp_done"))
        pT_done, pTh_done, pTl_done = sem("pT_done"), sem("pTh_done"), sem("pTl_done")
        pv_done, rs_done, o_done, x1_done = sem("pv_done"), sem("rs_done"), sem("o_done"), sem("x1_done")
        x1_out = [sem("x1_out0"), sem("x1_out1")]
        NP = 2 * KC + TILES

        FIRST, LOOP, PAIRS, LAST = -1, 2, (STEPS - 4) // 2, STEPS
        assert LOOP + 2 * PAIRS <= STEPS - 2

        block = ctx.enter_context(nc.Block())

        @block.sync
        def _(sp):
            sp.dma_start(xin[:, 0], x_v[0]).then_inc(x_in[0], 16)
            for n, w in enumerate((wq, wk, wv)):
                sp.dma_start(wst[:, n], w.rearrange("(k p) n -> p k n", p=P)).then_inc(w_in[n], 16)
            for n, b in enumerate((bq, bk)):
                sp.dma_start(bst[:, n, :], b.rearrange("(a d) -> a d", a=1)).then_inc(b_in, 16)
            sp.dma_start(bvrow[:], bv.rearrange("(a d) -> a d", a=1).to_broadcast([P, D])).then_inc(row_in, 16)
            sp.dma_start(betac[:], beta.rearrange("(a b) -> a b", a=1).to_broadcast([P, 1])).then_inc(row_in, 16)
            for n in range(2):
                sp.dma_start(adjb[n * NODES:(n + 1) * NODES, :].rearrange("q (g k) -> q g k", g=GPS),
                             adj_v[0]).then_inc(adj_in, 16)
            sp.dma_start(xin[:, 1], x_v[1]).then_inc(x_in[1], 16)

            def body(s):
                ahead, prev = s.plus(2), s.plus(-1)
                if 0 <= s.b and ahead.b < STEPS:
                    sp.wait_ge(z_done, TILES * (s.i + 1))
                    sp.wait_ge(xres_done, s.i + 1)
                    sp.dma_start(xin[:, s.par], x_v[ahead.i]).then_inc(x_in[s.par], 16)
                if ahead.b < STEPS:
                    reach(sp, mask_done, s.i + 2)
                    for n in range(2):
                        sp.dma_start(adjb[n * NODES:(n + 1) * NODES, :].rearrange("q (g k) -> q g k", g=GPS),
                                     adj_v[ahead.i]).then_inc(adj_in, 16)
                if prev.b >= 0:
                    sp.wait_ge(x1_done, TILES * (prev.i + 1))
                    sp.dma_start(x1_v[prev.i], x1b[:, prev.par]).then_inc(x1_out[prev.par], 16)

            run_steps(sp, body, FIRST, LOOP, PAIRS, LAST)
            for n in range(2):
                sp.wait_ge(x1_out[n], 16 * (STEPS // 2))

        @block.gpsimd
        def _(pool):
            g = nc.gpsimd
            g.memset(ident[:], 0.0).then_inc(zeroed, 1)
            g.memset(tops[:], 0.0).then_inc(const_set, 1)
            g.memset(scale_rows[:], Z_SCALE).then_inc(const_set, 1)
            g.memset(bias_rows[:], 0.0).then_inc(const_set, 1)
            g.memset(nhalf[:], -0.5).then_inc(const_set, 1)
            pool.wait_ge(zeroed, 1)
            g.affine_select(out=ident[:], in_=ident[:], compare_op=ALU.not_equal, fill=1.0, base=0,
                            pattern=[[-1, P]], channel_multiplier=1).then_inc(ident_set, 1)
            def ln(s):
                pool.wait_ge(stats_done, s.i + 1)
                carry(pool)
                g.tensor_scalar(nmean[:], mv[:, :, 0], -1.0, None, ALU.mult)
                g.tensor_scalar(vs[:], mv[:, :, 1], EPS, Z_SCALE ** -2, ALU.add, ALU.mult).then_inc(pool_chain, 1)
                pool.wait_ge(pool_chain, 2 * s.i + 1)
                reach(pool, z_done, TILES * s.i)
                g.tensor_tensor(rstd[:], vs[:], nhalf[:], ALU.pow).then_inc(pool_chain, 1)
                pool.wait_ge(pool_chain, 2 * s.i + 2)
                g.tensor_tensor(nmr[:], nmean[:], rstd[:], ALU.mult).then_inc(rstd_done, 1)

            def make_mask(s):
                pool.wait_ge(adj_in, 32 * (s.i + 1))
                reach(pool, mask_done, s.i)
                carry(pool)
                g.tensor_scalar(edge[:], adjb[:], betac[:, 0:1], None, ALU.mult)
                g.tensor_scalar(neg[:], adjb[:], 0.0, MASKED, ALU.is_le, ALU.mult).then_inc(neg_done, 1)
                pool.wait_ge(neg_done, s.i + 1)
                reach(pool, s_evac, TILES * (s.i - 1))
                g.tensor_tensor(mask[:, s.par], edge[:], neg[:], ALU.add).then_inc(mask_done, 1)

            def subtract(s, t):
                pool.wait_ge(mx_done, TILES * s.i + t + 1)
                sv = sc[:, t % 2].rearrange("p j (g k) -> p (j g) k", g=PER_TILE)
                g.tensor_tensor(sv, sv, mx[:, t % 2, :].unsqueeze(2).to_broadcast([P, HEADS, NODES]),
                                ALU.subtract).then_inc(sub_done, 1)

            def residual(s, t):
                pool.wait_ge(o_done, TILES * s.i + t + 1)
                if t == 0:
                    reach(pool, x1_out[s.par], 16 * s.turn)
                    pool.wait_ge(xres_done, s.i + 1)
                g.tensor_tensor(x1b[:, s.par, t, :], on[:, t % 2, :], xres[:, s.par, t, :], ALU.add).then_inc(x1_done, 1)

            def add_bv(s):
                reach(pool, x1_done, TILES * (s.i - 1))
                g.tensor_tensor(xres[:, s.par], xin[:, s.par], bvrow[:].unsqueeze(1).to_broadcast([P, TILES, D]),
                                ALU.add).then_inc(xres_done, 1)

            def body(s):
                prev, nx, ah = s.plus(-1), s.plus(1), s.plus(2)
                main, tail = 0 <= s.b < STEPS, prev.b >= 0
                if s.b < 0:
                    make_mask(nx)
                    add_bv(nx)
                if nx.b >= 1 and nx.b < STEPS:
                    make_mask(nx)
                if main:
                    subtract(s, 0)
                if tail:
                    residual(prev, 2)
                if main:
                    subtract(s, 1)
                if tail:
                    residual(prev, 3)
                if nx.b >= 1 and nx.b < STEPS:
                    add_bv(nx)
                if main:
                    subtract(s, 2)
                if ah.b < STEPS:
                    ln(ah)
                if main:
                    subtract(s, 3)
                    residual(s, 0)
                    residual(s, 1)

            g.memset(qh[:, 0], 0.0).then_inc(zeroed, 1)
            pool.wait_ge(const_set, 4)
            ln(Step(0, 0))
            pool.wait_ge(tops_done, NW + 1)
            g.partition_all_reduce(topa[:].rearrange("p a n -> p (a n)"), tops[:].rearrange("p a n -> p (a n)"),
                                   P, RMAX).then_inc(topall_done, 1)
            g.memset(ql[:, 0], 0.0).then_inc(zeroed, 1)
            pool.wait_ge(row_in, 32)
            run_steps(pool, body, FIRST, LOOP, PAIRS, LAST)

        @block.scalar
        def _(act):
            s_ = nc.scalar
            def normalise(s, t):
                if t == 0:
                    act.wait_ge(rstd_done, s.i + 1)
                    reach(act, zT_done, KC * s.i)
                s_.activation(z[:, t, :], xin[:, s.par, t, :], ACT.Identity, bias=nmr[:, t:t + 1],
                              scale=rstd[:, t:t + 1]).then_inc(z_done, 1)

            def zT_high(s, k):
                act.wait_ge(zT_done, KC * s.i + k + 1)
                s_.copy(zh[:, k, :], zT_ps[:]).then_inc(zTh_done, 1)

            def proj_high(s, n):
                act.wait_ge(proj_done, NP * s.i + n + 1)
                ps = pr_ps[n % 2]
                if n >= 2 * KC:
                    t = n - 2 * KC
                    s_.activation(vh[:, s.par, t, :, 0:HD], ps[:, 0:D].rearrange("p (h d) -> p h d", h=HEADS),
                                  ACT.Copy, scale=evac[:, 2:3]).then_inc(projh_done, 4)
                elif n % 2:
                    s_.activation(kh[:, s.par, n // 2, :], ps[:], ACT.Copy, scale=evac[:, 1:2]).then_inc(projh_done, 4)
                else:
                    for h in range(4):
                        r = slice(HD * h, HD * h + HD)
                        s_.activation(qh[r, s.par, n // 2, h // 2, :, h % 2, :],
                                      ps[r, :].rearrange("p (g q) -> p g q", g=GPS),
                                      ACT.Copy, scale=evac[r, 0:1]).then_inc(projh_done, 1)

            def exp(s, t):
                act.wait_ge(sub_done, TILES * s.i + t + 1)
                s_.activation(sc[:, t % 2], sc[:, t % 2], ACT.Exp).then_inc(exp_done, 1)

            def pT_high(s, t):
                act.wait_ge(pT_done, TILES * s.i + t + 1)
                s_.copy(pth[:, t % 2], p3).then_inc(pTh_done, 1)

            def body(s):
                prev, nx, ah = s.plus(-1), s.plus(1), s.plus(2)
                main, proj, norm, tail = 0 <= s.b < STEPS, nx.b < STEPS, ah.b < STEPS, prev.b >= 0
                turn = 0 < nx.b < STEPS
                if turn:
                    zT_high(nx, 0)
                    zT_high(nx, 1)
                if tail:
                    pT_high(prev, 3)
                if turn:
                    zT_high(nx, 2)
                if main:
                    exp(s, 0)
                if proj:
                    proj_high(nx, 0)
                    proj_high(nx, 1)
                if main:
                    pT_high(s, 0)
                    exp(s, 1)
                if proj:
                    proj_high(nx, 2)
                    proj_high(nx, 3)
                if main:
                    pT_high(s, 1)
                if proj:
                    proj_high(nx, 4)
                if norm:
                    normalise(ah, 0)
                    normalise(ah, 1)
                    normalise(ah, 2)
                if proj:
                    proj_high(nx, 5)
                if main:
                    exp(s, 2)
                if proj:
                    proj_high(nx, 6)
                if norm:
                    normalise(ah, 3)
                if proj:
                    proj_high(nx, 7)
                if main:
                    pT_high(s, 2)
                if proj:
                    proj_high(nx, 8)
                if main:
                    exp(s, 3)
                if proj:
                    proj_high(nx, 9)

            first = Step(0, 0)
            for t in range(TILES):
                normalise(first, t)
            zT_high(first, 0)
            for n in range(NW):
                if n + 1 < KC:
                    zT_high(first, n + 1)
                act.wait_ge(scales_done, 1)
                s_.activation(wh[:, n].rearrange("p k n -> p (k n)"), wst[:, n].rearrange("p k n -> p (k n)"),
                              ACT.Copy, scale=wscale[:, n:n + 1]).then_inc(wh_done, 1)
            act.wait_ge(zeroed, 3)
            act.wait_ge(zeroed_dve, 2)
            run_steps(act, body, FIRST, LOOP, PAIRS, LAST)

        @block.vector
        def _(dve):
            v = nc.vector
            def stats(s):
                dve.wait_ge(x_in[s.par], 16 * (s.turn + 1))
                for t in range(TILES):
                    last = v.bn_stats(stat[:, t, :], xin[:, s.par, t, :])
                last.then_inc(bn_done, 1)
                dve.wait_ge(bn_done, s.i + 1)
                reach(dve, rstd_done, s.i)
                carry(dve)
                for t in range(TILES):
                    last = v.bn_aggr(mv[:, t, :], stat[:, t, :])
                last.then_inc(stats_done, 1)

            def zT_low(s, k):
                dve.wait_ge(zTh_done, KC * s.i + k + 1)
                v.tensor_tensor(zl[:, k, :], zT_ps[:], zh[:, k, :], ALU.subtract).then_inc(zTl_done, 1)

            def proj_low(s, n):
                count = 4 * (NP * s.i + n)
                if n % 2 or n >= 2 * KC:
                    dve.wait_ge(projh_done, count + 4)
                ps = pr_ps[n % 2]
                if n >= 2 * KC:
                    t = n - 2 * KC
                    v.scalar_tensor_tensor(out=vl[:, s.par, t, :, 0:HD],
                                           in0=ps[:, 0:D].rearrange("p (h d) -> p h d", h=HEADS),
                                           scalar=evac[:, 2:3], in1=vh[:, s.par, t, :, 0:HD],
                                           op0=ALU.mult, op1=ALU.subtract).then_inc(projl_done, 1)
                elif n % 2:
                    v.scalar_tensor_tensor(out=kl[:, s.par, n // 2, :], in0=ps[:], scalar=evac[:, 1:2],
                                           in1=kh[:, s.par, n // 2, :],
                                           op0=ALU.mult, op1=ALU.subtract).then_inc(projl_done, 1)
                else:
                    for h in range(4):
                        dve.wait_ge(projh_done, count + h + 1)
                        r = slice(HD * h, HD * h + HD)
                        at = (r, s.par, n // 2, h // 2, slice(None), h % 2, slice(None))
                        last = v.scalar_tensor_tensor(out=ql[at], in0=ps[r, :].rearrange("p (g q) -> p g q", g=GPS),
                                                      scalar=evac[r, 0:1], in1=qh[at],
                                                      op0=ALU.mult, op1=ALU.subtract)
                    last.then_inc(projl_done, 1)

            def mask_scores(s, t):
                dve.wait_ge(s_done, TILES * s.i + t + 1)
                if t == 0:
                    dve.wait_ge(mask_done, s.i + 1)
                reach(dve, pT_done, TILES * s.i + t - 1)
                m = mask[:, s.par, P * t:P * t + P].unsqueeze(1).to_broadcast([P, NJ, P])
                v.scalar_tensor_tensor(out=sc[:, t % 2], in0=s3, scalar=sscale[:, 0:1], in1=m,
                                       op0=ALU.mult, op1=ALU.add).then_inc(s_evac, 1)
                dve.wait_ge(s_evac, TILES * s.i + t + 1)
                reach(dve, sub_done, TILES * s.i + t - 1)
                v.tensor_reduce(mx[:, t % 2, :], sc[:, t % 2].rearrange("p j (g k) -> p (j g) k", g=PER_TILE),
                                AX_X, ALU.max).then_inc(mx_done, 1)

            def pT_low(s, t):
                dve.wait_ge(pTh_done, TILES * s.i + t + 1)
                v.tensor_tensor(ptl[:, t % 2], p3, pth[:, t % 2], ALU.subtract).then_inc(pTl_done, 1)

            def divide(s, t):
                dve.wait_ge(pv_done, TILES * s.i + t + 1)
                v.reciprocal(rs[:, t % 2, :], o3[:, :, HD]).then_inc(rs_done, 1)
                dve.wait_ge(rs_done, TILES * s.i + t + 1)
                reach(dve, x1_done, TILES * s.i + t - 1)
                v.tensor_tensor(on[:, t % 2, :].rearrange("p (h d) -> p h d", h=HEADS), o3[:, :, 0:HD],
                                rs[:, t % 2, :].unsqueeze(2).to_broadcast([P, HEADS, HD]),
                                ALU.mult).then_inc(o_done, 1)

            def body(s):
                prev, nx, ah = s.plus(-1), s.plus(1), s.plus(2)
                main, proj, norm, tail = 0 <= s.b < STEPS, nx.b < STEPS, ah.b < STEPS, prev.b >= 0
                turn = 0 < nx.b < STEPS
                if turn:
                    zT_low(nx, 0)
                if main:
                    mask_scores(s, 0)
                if turn:
                    zT_low(nx, 1)
                    zT_low(nx, 2)
                if tail:
                    pT_low(prev, 3)
                    divide(prev, 2)
                if main:
                    mask_scores(s, 1)
                if tail:
                    divide(prev, 3)
                if proj:
                    proj_low(nx, 0)
                    proj_low(nx, 1)
                if main:
                    pT_low(s, 0)
                if norm:
                    stats(ah)
                if proj:
                    proj_low(nx, 2)
                if main:
                    mask_scores(s, 2)
                if proj:
                    proj_low(nx, 3)
                if main:
                    pT_low(s, 1)
                    divide(s, 0)
                if proj:
                    proj_low(nx, 4)
                    proj_low(nx, 5)
                if main:
                    mask_scores(s, 3)
                if proj:
                    proj_low(nx, 6)
                if main:
                    divide(s, 1)
                if proj:
                    proj_low(nx, 7)
                if main:
                    pT_low(s, 2)
                if proj:
                    proj_low(nx, 8)
                    proj_low(nx, 9)

            first = Step(0, 0)
            v.memset(qh[:, 1], 0.0).then_inc(zeroed_dve, 1)
            stats(first)
            dve.wait_ge(const_set, 1)
            for n in range(NW):
                dve.wait_ge(w_in[n], 16)
                v.tensor_reduce(tops[:, 0, n:n + 1], wst[:, n].rearrange("p k n -> p (k n)"), AX_X, ALU.max,
                                apply_absolute_value=True).then_inc(tops_done, 1)
            dve.wait_ge(b_in, 32)
            v.tensor_reduce(tops[0:1, 1, 0:2], bst[:], AX_X, ALU.max, apply_absolute_value=True).then_inc(tops_done, 1)
            zT_low(first, 0)
            link = Links(dve, chain).link
            dve.wait_ge(topall_done, 1)
            link(v.tensor_tensor(wmax[:], topa[:, 0, :], topa[:, 1, :], ALU.max))
            link(v.tensor_scalar(wmax[:], wmax[:], TINY, None, ALU.max))
            link(v.reciprocal(wrec[:], wmax[:]))
            v.tensor_scalar(wscale[:], wrec[:], W_TOP, None, ALU.mult).then_inc(scales_done, 1)
            zT_low(first, 1)
            link(v.scalar_tensor_tensor(out=bound[:], in0=topa[:, 0, :], scalar=Z_MAX * D, in1=topa[:, 1, :],
                                        op0=ALU.mult, op1=ALU.add))
            link(v.tensor_scalar(bound[:], bound[:], TINY, None, ALU.max))
            link(v.reciprocal(brec[:], bound[:]))
            link(v.tensor_scalar(cscale[:], brec[:], TOP, None, ALU.mult))
            link(v.scalar_tensor_tensor(out=evac[:], in0=cscale[:], scalar=1.0 / (Z_SCALE * W_TOP), in1=wmax[:],
                                        op0=ALU.mult, op1=ALU.mult))
            link(v.scalar_tensor_tensor(out=sscale[:], in0=bound[:, 0:1], scalar=RSQRT_HD / (TOP * TOP),
                                        in1=bound[:, 1:2], op0=ALU.mult, op1=ALU.mult))
            ones = vh[:, :, :, :, HD].rearrange("p a t h -> p (a t) h")
            onesl = vl[:, :, :, :, HD].rearrange("p a t h -> p (a t) h")
            cvb = cscale[:, 2:3].unsqueeze(2).to_broadcast([P, 2 * TILES, HEADS])
            link(v.tensor_copy(ones, cvb))
            link(v.tensor_tensor(onesl, cvb, ones, ALU.subtract))
            zT_low(first, 2)
            dve.wait_ge(const_set, 3)
            for n in range(2):
                link(v.tensor_scalar(bias_rows[0:1, n, :], bst[:, n, :], wscale[0:1, n:n + 1], None, ALU.mult))
                link(v.scalar_tensor_tensor(out=bias_rows[32:33, n, :], in0=bst[:, n, :],
                                            scalar=wscale[0:1, n:n + 1], in1=bias_rows[0:1, n, :],
                                            op0=ALU.mult, op1=ALU.subtract))
            for n in range(NW):
                dve.wait_ge(wh_done, n + 1)
                v.scalar_tensor_tensor(out=wl[:, n].rearrange("p k n -> p (k n)"),
                                       in0=wst[:, n].rearrange("p k n -> p (k n)"), scalar=wscale[:, n:n + 1],
                                       in1=wh[:, n].rearrange("p k n -> p (k n)"),
                                       op0=ALU.mult, op1=ALU.subtract).then_inc(wl_done, 1)
            v.memset(ql[:, 1], 0.0).then_inc(zeroed_dve, 1)
            dve.wait_ge(const_set, 4)
            dve.wait_ge(zeroed, 3)
            run_steps(dve, body, FIRST, LOOP, PAIRS, LAST)

        @block.tensor
        def _(pe):
            mm = nc.tensor.matmul
            pe.wait_ge(ident_set, 1)

            def three(out, sh, sl, mh, ml, first, last):
                mm(out, sh, mh, start=first, stop=False)
                mm(out, sl, mh, start=False, stop=False)
                return mm(out, sh, ml, start=False, stop=last)

            def zT(s, k):
                if k == 0:
                    pe.wait_ge(z_done, TILES * (s.i + 1))
                reach(pe, zTl_done, KC * s.i + k)
                for t in range(TILES):
                    last = nc.tensor.transpose(zT_ps[:, P * t:P * t + P], z[:, t, P * k:P * k + P], ident[:])
                last.then_inc(zT_done, 1)

            def proj(s, n):
                reach(pe, projl_done, NP * s.i + n - 1)
                if s.b == 0 and n in (0, 1, 2 * KC):
                    pe.wait_ge(wl_done, min(n, 2) + 1)
                ps = pr_ps[n % 2]
                if n < 2 * KC:
                    w, c = n % 2, slice(P * (n // 2), P * (n // 2) + P)
                    mm(ps[:], bias_rows[:, w, c], scale_rows[:], start=True, stop=False)
                    for k in range(KC):
                        if n == 0:
                            pe.wait_ge(zTl_done, KC * s.i + k + 1)
                        last = three(ps[:], wh[:, w, k, c], wl[:, w, k, c], zh[:, k, :], zl[:, k, :],
                                     False, k == KC - 1)
                else:
                    c = slice(P * (n - 2 * KC), P * (n - 2 * KC) + P)
                    for k in range(KC):
                        last = three(ps[:, 0:D], zh[:, k, c], zl[:, k, c], wh[:, 2, k, :], wl[:, 2, k, :],
                                     k == 0, k == KC - 1)
                last.then_inc(proj_done, 1)

            def scores(s, t):
                if t == 0:
                    pe.wait_ge(projl_done, NP * s.i + 2 * KC)
                reach(pe, s_evac, TILES * s.i + t)
                for j in range(NJ):
                    for g in range(PER_TILE):
                        gg = PER_TILE * t + g
                        at = (slice(None), s.par, j // 2, j % 2, gg)
                        st_h = qh[at].rearrange("p h q -> p (h q)")
                        st_l = ql[at].rearrange("p h q -> p (h q)")
                        c = slice(NODES * gg, NODES * gg + NODES)
                        last = three(s3[:, j, NODES * g:NODES * g + NODES], st_h, st_l,
                                     kh[:, s.par, j // 2, c], kl[:, s.par, j // 2, c], True, True)
                last.then_inc(s_done, 1)

            def pT(s, t):
                pe.wait_ge(exp_done, TILES * s.i + t + 1)
                reach(pe, pTl_done, TILES * s.i + t)
                for j in range(NJ):
                    last = nc.tensor.transpose(p3[:, j, :], sc[:, t % 2, j, :], ident[:])
                last.then_inc(pT_done, 1)

            def pv(s, t):
                pe.wait_ge(pTl_done, TILES * s.i + t + 1)
                pe.wait_ge(projl_done, NP * s.i + 2 * KC + t + 1)
                reach(pe, o_done, TILES * s.i + t)
                carry(pe)
                for h in range(HEADS):
                    for g in range(PER_TILE):
                        r = slice(NODES * g, NODES * g + NODES)
                        c = slice(NODES * (h % 2), NODES * (h % 2) + NODES)
                        last = three(o3[r, h, :], pth[r, t % 2, h // 2, c], ptl[r, t % 2, h // 2, c],
                                     vh[r, s.par, t, h, :], vl[r, s.par, t, h, :], True, True)
                last.then_inc(pv_done, 1)

            def body(s):
                prev, nx = s.plus(-1), s.plus(1)
                main, more, tail = 0 <= s.b < STEPS, nx.b < STEPS, prev.b >= 0
                turn = 0 < nx.b < STEPS
                if turn:
                    zT(nx, 0)
                if main:
                    scores(s, 0)
                if tail:
                    pT(prev, 3)
                if turn:
                    zT(nx, 1)
                if tail:
                    pv(prev, 2)
                if turn:
                    zT(nx, 2)
                if main:
                    scores(s, 1)
                if more:
                    proj(nx, 0)
                if tail:
                    pv(prev, 3)
                if more:
                    proj(nx, 1)
                if main:
                    pT(s, 0)
                    scores(s, 2)
                if more:
                    proj(nx, 2)
                    proj(nx, 3)
                if main:
                    pT(s, 1)
                    pv(s, 0)
                if more:
                    proj(nx, 4)
                if main:
                    scores(s, 3)
                if more:
                    proj(nx, 5)
                if main:
                    pv(s, 1)
                if more:
                    proj(nx, 6)
                    proj(nx, 7)
                if main:
                    pT(s, 2)
                if more:
                    proj(nx, 8)
                    proj(nx, 9)

            for k in range(KC):
                zT(Step(0, 0), k)
            run_steps(pe, body, FIRST, LOOP, PAIRS, LAST)


def mlp_phase(nc, h, x1, g2, b2, w1, bf1, w2, bf2, ident_in, out):
    with ExitStack() as ctx:
        a = Memory(nc, ctx, "mlp")
        view = lambda t: t.rearrange("(i t g) q d -> i (g q) t d", t=TILES, g=PER_TILE)
        h_v, x1_v, out_v = view(h), view(x1), view(out)
        row = lambda t: t.rearrange("(a d) -> a d", a=1)
        RING = 4
        LAG = 2
        BANKS = 3

        w1s = a.sb("w1_staging", [P, KC, F], F32)
        w2s = a.sb("w2_staging", [P, FC, D], F32)
        w1h, w1l = a.sb("w1_high", [P, KC, F], F16), a.sb("w1_low", [P, KC, F], F16)
        w2h, w2l = a.sb("w2_high", [P, FC, D], F16), a.sb("w2_low", [P, FC, D], F16)
        ident = a.sb("ident", [P, P], F32)
        WP = KC
        TOP_W1, TOP_G, TOP_B, TOP_F, TOP_W2 = range(5)
        tops, topa = a.sb("tops", [P, 5], F32), a.sb("tops_all", [P, 5], F32)
        gcol, bcol, fcol = a.sb("g2_col", [P, KC], F32), a.sb("b2_col", [P, KC], F32), a.sb("bf1_col", [P, FC], F32)
        rec5 = a.sb("rec", [P, 5], F32)
        wsc = a.sb("w_scale", [P, 2], F32)
        gsc = a.sb("g_scaled", [P, KC], F32)
        bsc = a.sb("b_scale", [P, 1], F32)
        bh, bl = a.sb("b2_high", [P, KC], F16), a.sb("b2_low", [P, KC], F16)
        ub = a.sb("u_bound", [P, 2], F32)
        ca = a.sb("act_scale", [P, 1], F32)
        us = a.sb("u_scale", [P, 1], F32)
        bs = a.sb("bias_scale", [P, 1], F32)
        os_ = a.sb("out_scale", [P, 1], F32)
        ubias = a.sb("u_bias", [P, FC], F32)
        frow = a.sb("bf2_row", [P, D], F32)
        nhalf = a.sb("minus_half", [P, TILES], F32)

        hin = a.sb("h_in", [P, 2, TILES, D], F32)
        xin = a.sb("x1_in", [P, 2, TILES, D], F32)
        base = a.sb("base", [P, TILES, D], F32)
        z = a.sb("z", [P, TILES, D], F32)
        stat = a.sb("stat", [P, TILES, 6], F32)
        mv = a.sb("mean_var", [P, TILES, 2], F32)
        vs, rstd, nmean, nmr = (a.sb(n, [P, TILES], F32) for n in ("var_eps", "rstd", "minus_mean", "minus_mean_rstd"))
        zh, zl = a.sb("zT_high", [P, 2, KC, TOK], F16), a.sb("zT_low", [P, 2, KC, TOK], F16)
        act32 = a.sb("act", [P, 2, TOK], F32)
        ah, al = a.sb("act_high", [P, RING, TOK], F16), a.sb("act_low", [P, RING, TOK], F16)
        outb = a.sb("out", [P, 2, TILES, D], F32)

        u_ps = [a.ps(f"u_ps{n}", [P, TOK]) for n in range(BANKS)]
        y_ps = [a.ps(f"y_ps{n}", [P, 512]) for n in range(TILES)]
        zT_ps = a.ps("zT_ps", [P, TOK])

        sem = a.sem
        w_in, col_in, row_in = [sem("w1_in"), sem("w2_in")], sem("col_in"), sem("row_in")
        const_set, tops_done, topall_done = sem("const_set"), sem("tops_done"), sem("topall_done")
        chain, scales_done, bsplit_done = sem("chain"), sem("scales_done"), sem("bsplit_done")
        wh_done, wl_done, bias_done, ubias_done = sem("wh_done"), sem("wl_done"), sem("bias_done"), sem("ubias_done")
        h_in, x_in = [sem("h_in0"), sem("h_in1")], [sem("x_in0"), sem("x_in1")]
        bn_done, stats_done, pool_chain, rstd_done = (
            sem("bn_done"), sem("stats_done"), sem("pool_chain"), sem("rstd_done"))
        z_done, zT_done, zTh_done, zTl_done = sem("z_done"), sem("zT_done"), sem("zTh_done"), sem("zTl_done")
        sum_done, base_done = sem("sum_done"), sem("base_done")
        u_done, gelu_done, ah_done, al_done = sem("u_done"), sem("gelu_done"), sem("ah_done"), sem("al_done")
        y_part, out_done = sem("y_part"), sem("out_done")
        out_st = [sem("out_st0"), sem("out_st1")]

        FIRST, LOOP, LOOPS, LAST = 0, 3, (STEPS - 5) // 2, STEPS
        part = lambda k: slice(FC // WP * k, FC // WP * (k + 1))
        block = ctx.enter_context(nc.Block())

        @block.sync
        def _(sp):
            sp.dma_start(hin[:, 0], h_v[0]).then_inc(h_in[0], 16)
            for to, of in ((gcol, g2), (bcol, b2), (fcol, bf1)):
                sp.dma_start(to[:], of.rearrange("(k p) -> p k", p=P), allow_slow_non_contiguous=True)\
                    .then_inc(col_in, 16)
            for k in range(WP):
                sp.dma_start(w1s[:, k, :], w1[P * k:P * k + P, :]).then_inc(w_in[0], 16)
            w2_v = w2.rearrange("(k p) n -> p k n", p=P)
            for k in range(WP):
                sp.dma_start(w2s[:, part(k), :], w2_v[:, part(k), :]).then_inc(w_in[1], 16)
            sp.dma_start(ident[:], ident_in).then_inc(row_in, 16)
            sp.dma_start(frow[:], row(bf2).to_broadcast([P, D])).then_inc(row_in, 16)
            sp.dma_start(xin[:, 0], x1_v[0]).then_inc(x_in[0], 16)
            sp.dma_start(hin[:, 1], h_v[1]).then_inc(h_in[1], 16)
            sp.dma_start(xin[:, 1], x1_v[1]).then_inc(x_in[1], 16)

            def body(s):
                if s.b >= 0 and s.b + 2 < STEPS:
                    sp.wait_ge(base_done, s.i + 1)
                    sp.dma_start(hin[:, s.par], h_v[s.i + 2]).then_inc(h_in[s.par], 16)
                    sp.dma_start(xin[:, s.par], x1_v[s.i + 2]).then_inc(x_in[s.par], 16)
                if s.b >= 1:
                    before = s.plus(-1)
                    sp.wait_ge(out_done, TILES * s.i)
                    sp.dma_start(out_v[before.i], outb[:, before.par]).then_inc(out_st[before.par], 16)

            run_steps(sp, body, FIRST, LOOP, LOOPS, LAST)
            for n in range(2):
                sp.wait_ge(out_st[n], 16 * (STEPS // 2))

        @block.gpsimd
        def _(pool):
            g = nc.gpsimd
            g.memset(nhalf[:], -0.5).then_inc(const_set, 1)

            def ln(s):
                reach(pool, stats_done, s.i + 1)
                carry(pool)
                g.tensor_scalar(nmean[:], mv[:, :, 0], -1.0, None, ALU.mult)
                g.tensor_scalar(vs[:], mv[:, :, 1], EPS, 1.0, ALU.add, ALU.mult).then_inc(pool_chain, 1)
                pool.wait_ge(pool_chain, 2 * s.i + 1)
                reach(pool, z_done, TILES * s.i)
                g.tensor_tensor(rstd[:], vs[:], nhalf[:], ALU.pow).then_inc(pool_chain, 1)
                pool.wait_ge(pool_chain, 2 * s.i + 2)
                g.tensor_tensor(nmr[:], nmean[:], rstd[:], ALU.mult).then_inc(rstd_done, 1)

            def sums(s):
                pool.wait_ge(x_in[s.par], 16 * (s.turn + 1))
                pool.wait_ge(h_in[s.par], 16 * (s.turn + 1))
                reach(pool, out_done, TILES * s.i)
                pool.wait_ge(z_done, TILES * (s.i + 1))
                g.tensor_tensor(base[:], xin[:, s.par], hin[:, s.par], ALU.add).then_inc(sum_done, 1)
                pool.wait_ge(sum_done, s.i + 1)
                g.tensor_tensor(base[:], base[:],
                                frow[:].unsqueeze(1).to_broadcast([P, TILES, D]), ALU.add).then_inc(base_done, 1)

            def body(s):
                if s.b + 1 < STEPS:
                    ln(s.plus(1))
                if 0 <= s.b < STEPS:
                    sums(s)

            pool.wait_ge(const_set, 1)
            ln(Step(0, 0))
            pool.wait_ge(tops_done, 4)
            g.partition_all_reduce(topa[:, 0:TOP_W2], tops[:, 0:TOP_W2], P, RMAX).then_inc(topall_done, 1)
            pool.wait_ge(tops_done, 5)
            g.partition_all_reduce(topa[:, TOP_W2:5], tops[:, TOP_W2:5], P, RMAX).then_inc(topall_done, 1)
            pool.wait_ge(row_in, 32)
            run_steps(pool, body, FIRST, LOOP, LOOPS, LAST)

        @block.scalar
        def _(act):
            s_ = nc.scalar
            def normalise(s, t):
                if t == 0:
                    act.wait_ge(rstd_done, s.i + 1)
                    reach(act, zT_done, KC * s.i)
                s_.activation(z[:, t, :], hin[:, s.par, t, :], ACT.Identity, bias=nmr[:, t:t + 1],
                              scale=rstd[:, t:t + 1]).then_inc(z_done, 1)

            def zT_high(s, k):
                act.wait_ge(zT_done, KC * s.i + k + 1)
                s_.activation(zh[:, s.par, k, :], zT_ps[:], ACT.Copy, scale=gsc[:, k:k + 1]).then_inc(zTh_done, 1)

            def w2_high(k):
                act.wait_ge(scales_done, 3)
                c = part(k)
                s_.activation(w2h[:, c, :], w2s[:, c, :], ACT.Copy, scale=wsc[:, 1:2]).then_inc(wh_done, 1)

            def gelu(s, c):
                act.wait_ge(u_done, FC * s.i + c + 1)
                reach(act, al_done, FC * s.i + c - 1)
                s_.activation(act32[:, c % 2, :], u_ps[c % BANKS][:], ACT.Gelu, bias=ubias[:, c:c + 1],
                              scale=us[:, 0:1]).then_inc(gelu_done, 1)

            def body(s):
                nx = s.plus(1)
                main, norm = 0 <= s.b < STEPS, nx.b < STEPS
                for c in range(FC):
                    if main:
                        gelu(s, c)
                    if s.b == 0 and c < WP:
                        w2_high(c)
                    if norm and 2 <= c < 2 + TILES:
                        normalise(nx, c - 2)
                    if norm and c in (7, 9, 11):
                        zT_high(nx, (c - 7) // 2)

            first = Step(0, 0)
            for t in range(TILES):
                normalise(first, t)
            for k in range(KC):
                act.wait_ge(scales_done, 1)
                s_.activation(w1h[:, k, :], w1s[:, k, :], ACT.Copy, scale=wsc[:, 0:1]).then_inc(wh_done, 1)
                act.wait_ge(scales_done, 2)
                zT_high(first, k)
            act.wait_ge(ubias_done, 1)
            run_steps(act, body, FIRST, LOOP, LOOPS, LAST)

        @block.vector
        def _(dve):
            v = nc.vector
            def stats(s):
                dve.wait_ge(h_in[s.par], 16 * (s.turn + 1))
                for t in range(TILES):
                    last = v.bn_stats(stat[:, t, :], hin[:, s.par, t, :])
                last.then_inc(bn_done, 1)
                reach(dve, rstd_done, s.i)
                dve.wait_ge(bn_done, s.i + 1)
                carry(dve)
                for t in range(TILES):
                    last = v.bn_aggr(mv[:, t, :], stat[:, t, :])
                last.then_inc(stats_done, 1)

            def zT_low(s, k):
                dve.wait_ge(zTh_done, KC * s.i + k + 1)
                v.scalar_tensor_tensor(out=zl[:, s.par, k, :], in0=zT_ps[:], scalar=gsc[:, k:k + 1],
                                       in1=zh[:, s.par, k, :], op0=ALU.mult, op1=ALU.subtract).then_inc(zTl_done, 1)

            def w2_low(k):
                dve.wait_ge(wh_done, KC + k + 1)
                c = part(k)
                v.scalar_tensor_tensor(out=w2l[:, c, :], in0=w2s[:, c, :], scalar=wsc[:, 1:2], in1=w2h[:, c, :],
                                       op0=ALU.mult, op1=ALU.subtract).then_inc(wl_done, 1)

            def split(s, c):
                dve.wait_ge(gelu_done, FC * s.i + c + 1)
                reach(dve, y_part, TILES * (FC * s.i + c + 1 - RING))
                v.tensor_scalar(ah[:, c % RING, :], act32[:, c % 2, :], ca[:, 0:1], None, ALU.mult).then_inc(ah_done, 1)
                dve.wait_ge(ah_done, FC * s.i + c + 1)
                v.scalar_tensor_tensor(out=al[:, c % RING, :], in0=act32[:, c % 2, :], scalar=ca[:, 0:1],
                                       in1=ah[:, c % RING, :], op0=ALU.mult, op1=ALU.subtract).then_inc(al_done, 1)

            def finish(s, t):
                dve.wait_ge(y_part, TILES * (FC * s.i + FC - 1) + t + 1)
                if t == 0:
                    dve.wait_ge(base_done, s.i + 1)
                    reach(dve, out_st[s.par], 16 * s.turn)
                v.scalar_tensor_tensor(out=outb[:, s.par, t, :], in0=y_ps[t][:, 0:D], scalar=os_[:, 0:1],
                                       in1=base[:, t, :], op0=ALU.mult, op1=ALU.add).then_inc(out_done, 1)

            def body(s):
                nx = s.plus(1)
                main, norm = 0 <= s.b < STEPS, nx.b < STEPS
                for c in range(FC):
                    if main:
                        split(s, c)
                    if s.b == 0 and c < WP:
                        w2_low(c)
                    if c == 1 and s.b >= 1:
                        for t in range(TILES):
                            finish(s.plus(-1), t)
                    if c == 1 and main and norm:
                        stats(nx)
                    if norm and c in (7, 9, 11):
                        zT_low(nx, (c - 7) // 2)

            first = Step(0, 0)
            stats(first)
            dve.wait_ge(w_in[0], 16 * WP)
            v.tensor_reduce(tops[:, 0:1], w1s[:].rearrange("p k n -> p (k n)"), AX_X, ALU.max,
                            apply_absolute_value=True).then_inc(tops_done, 1)
            dve.wait_ge(col_in, 48)
            for n, c in enumerate((gcol, bcol, fcol)):
                v.tensor_reduce(tops[:, TOP_G + n:TOP_G + n + 1], c[:], AX_X, ALU.max, apply_absolute_value=True)\
                    .then_inc(tops_done, 1)
            link = Links(dve, chain).link
            col = lambda n: topa[:, n:n + 1]
            dve.wait_ge(topall_done, 1)
            link(v.tensor_scalar(topa[:, 0:TOP_W2], topa[:, 0:TOP_W2], TINY, None, ALU.max))
            link(v.reciprocal(rec5[:, 0:TOP_W2], topa[:, 0:TOP_W2]))
            v.tensor_scalar(wsc[:, 0:1], rec5[:, TOP_W1:TOP_W1 + 1], W_TOP, None, ALU.mult).then_inc(scales_done, 1)
            v.tensor_scalar(gsc[:], gcol[:], rec5[:, TOP_G:TOP_G + 1], TOP / Z_MAX, ALU.mult, ALU.mult)\
                .then_inc(scales_done, 1)
            v.tensor_scalar(us[:], col(TOP_W1), col(TOP_G), Z_MAX / (TOP * W_TOP), ALU.mult, ALU.mult)
            v.tensor_scalar(bs[:], col(TOP_W1), col(TOP_B), 1.0 / (TOP * W_TOP), ALU.mult, ALU.mult)
            v.tensor_scalar(bsc[:], rec5[:, TOP_B:TOP_B + 1], TOP, None, ALU.mult)
            link(v.scalar_tensor_tensor(out=ub[:, 0:1], in0=col(TOP_G), scalar=Z_MAX, in1=col(TOP_B),
                                        op0=ALU.mult, op1=ALU.add))
            v.tensor_scalar(bh[:], bcol[:], bsc[:, 0:1], None, ALU.mult)
            link(v.tensor_scalar(ub[:, 0:1], ub[:, 0:1], col(TOP_W1), float(D), ALU.mult, ALU.mult))
            v.scalar_tensor_tensor(out=bl[:], in0=bcol[:], scalar=bsc[:, 0:1], in1=bh[:],
                                   op0=ALU.mult, op1=ALU.subtract).then_inc(bsplit_done, 1)
            link(v.tensor_tensor(ub[:, 0:1], ub[:, 0:1], col(TOP_F), ALU.add))
            link(v.reciprocal(ub[:, 1:2], ub[:, 0:1]))
            link(v.tensor_scalar(ca[:], ub[:, 1:2], TOP, None, ALU.mult))
            dve.wait_ge(scales_done, 2)
            for k in range(KC):
                dve.wait_ge(wh_done, k + 1)
                v.scalar_tensor_tensor(out=w1l[:, k, :], in0=w1s[:, k, :], scalar=wsc[:, 0:1], in1=w1h[:, k, :],
                                       op0=ALU.mult, op1=ALU.subtract).then_inc(wl_done, 1)
                zT_low(first, k)
            dve.wait_ge(w_in[1], 16 * WP)
            v.tensor_reduce(tops[:, TOP_W2:5], w2s[:].rearrange("p k n -> p (k n)"), AX_X, ALU.max,
                            apply_absolute_value=True).then_inc(tops_done, 1)
            dve.wait_ge(bias_done, 1)
            v.scalar_tensor_tensor(out=ubias[:], in0=y_ps[0][:, 0:FC], scalar=bs[:, 0:1], in1=fcol[:],
                                   op0=ALU.mult, op1=ALU.add).then_inc(ubias_done, 1)
            dve.wait_ge(topall_done, 2)
            link(v.tensor_scalar(col(TOP_W2), col(TOP_W2), TINY, None, ALU.max))
            link(v.reciprocal(rec5[:, TOP_W2:5], col(TOP_W2)))
            v.tensor_scalar(wsc[:, 1:2], rec5[:, TOP_W2:5], W_TOP, None, ALU.mult).then_inc(scales_done, 1)
            dve.wait_ge(scales_done, 3)
            link(v.tensor_scalar(os_[:], ub[:, 0:1], col(TOP_W2), 1.0 / (TOP * W_TOP), ALU.mult, ALU.mult))
            run_steps(dve, body, FIRST, LOOP, LOOPS, LAST)

        @block.tensor
        def _(pe):
            mm = nc.tensor.matmul
            def zT(s, k):
                if k == 0:
                    pe.wait_ge(z_done, TILES * (s.i + 1))
                reach(pe, zTl_done, KC * s.i + k)
                for t in range(TILES):
                    last = nc.tensor.transpose(zT_ps[:, P * t:P * t + P], z[:, t, P * k:P * k + P], ident[:])
                last.then_inc(zT_done, 1)

            def first(s, c):
                if c == 0:
                    pe.wait_ge(zTl_done, KC * (s.i + 1))
                reach(pe, gelu_done, FC * s.i + c + 1 - BANKS)
                ps, f = u_ps[c % BANKS], slice(P * c, P * c + P)
                for k in range(KC):
                    mm(ps[:], w1h[:, k, f], zh[:, s.par, k, :], start=k == 0, stop=False)
                    mm(ps[:], w1h[:, k, f], zl[:, s.par, k, :], start=False, stop=False)
                    last = mm(ps[:], w1l[:, k, f], zh[:, s.par, k, :], start=False, stop=k == KC - 1)
                last.then_inc(u_done, 1)

            def second(s, c):
                pe.wait_ge(al_done, FC * s.i + c + 1)
                if s.b == 0 and c == 0:
                    pe.wait_ge(ubias_done, 1)
                if s.b == 0 and c % (FC // WP) == 0:
                    pe.wait_ge(wl_done, KC + c // (FC // WP) + 1)
                for t in range(TILES):
                    if c == 0:
                        reach(pe, out_done, TILES * (s.i - 1) + t + 1)
                    y, tk = y_ps[t][:, 0:D], slice(P * t, P * t + P)
                    mm(y, ah[:, c % RING, tk], w2h[:, c, :], start=c == 0, stop=False)
                    mm(y, ah[:, c % RING, tk], w2l[:, c, :], start=False, stop=False)
                    last = mm(y, al[:, c % RING, tk], w2h[:, c, :], start=False, stop=c == FC - 1)
                    last.then_inc(y_part, 1)

            def body(s):
                nx, before = s.plus(1), s.plus(-1)
                main, norm = 0 <= s.b < STEPS, nx.b < STEPS
                for c in range(FC):
                    if main:
                        first(s, c)
                    if norm and c in (6, 8, 10):
                        zT(nx, (c - 6) // 2)
                    if c >= LAG and main:
                        second(s, c - LAG)
                    elif c < LAG and s.b >= 1:
                        second(before, FC - LAG + c)

            pe.wait_ge(row_in, 32)
            for k in range(KC):
                zT(Step(0, 0), k)
            pe.wait_ge(bsplit_done, 1)
            pe.wait_ge(wl_done, KC)
            for c in range(FC):
                f = slice(P * c, P * c + P)
                for k in range(KC):
                    mm(y_ps[0][:, c:c + 1], w1h[:, k, f], bh[:, k:k + 1], start=k == 0, stop=False)
                    mm(y_ps[0][:, c:c + 1], w1l[:, k, f], bh[:, k:k + 1], start=False, stop=False)
                    last = mm(y_ps[0][:, c:c + 1], w1h[:, k, f], bl[:, k:k + 1], start=False, stop=k == KC - 1)
            last.then_inc(bias_done, 1)
            run_steps(pe, body, FIRST, LOOP, LOOPS, LAST)


C_ID, C_ONE, C_SAME, C_LESS, C_IOTA, C_GRAPH, C_ATT, C_BIAS, C_ALL = 0, 128, 256, 384, 512, 532, 534, 535, 536
SLOT = 32
SPARE = PER_TILE * PICK
LOGIT_TOP = 16.635532
LOGIT_LOW = -88.7228


def constants():
    import numpy as np

    c = np.zeros((P, C_ALL), np.float32)
    p, q = np.arange(P)[:, None], np.arange(P)[None, :]
    c[:, C_ID:C_ID + P] = p == q
    c[:, C_ONE:C_ONE + P] = 1
    c[:, C_SAME:C_SAME + P] = p // NODES == q // NODES
    c[:, C_LESS:C_LESS + P] = (p // NODES == q // NODES) & (q < p)
    r = np.arange(SPARE)[None, :]
    c[:, C_IOTA:C_IOTA + SPARE] = np.where(r // PICK == p // NODES, r % PICK, -1)
    c[:, C_GRAPH:C_GRAPH + PER_TILE] = p // NODES == np.arange(PER_TILE)[None, :]
    c[:, C_ATT] = np.arange(P) % SLOT < SPARE
    c[:, C_BIAS] = np.arange(P) % SLOT == SPARE + PER_TILE
    return c


def mix_phase(nc, x1, g1, b1, wr, br, wq, bq, wk, bk, wv, bv, wo, bo, wm, bm, const_in, h):
    with ExitStack() as ctx:
        a = Memory(nc, ctx, "mix")
        view = lambda t: t.rearrange("(i t g) q d -> i (g q) t d", t=TILES, g=PER_TILE)
        x1_v, h_v = view(x1), view(h)
        row = lambda t: t.rearrange("(a d) -> a d", a=1)
        NW = 5
        Q, K, V, O, M = range(NW)
        SPLIT_ORDER = (K, V, Q, O, M)
        U = 3
        G4 = GPS

        wraw = a.sb("w_staging", [P, NW * KC * D], F32)
        wst = wraw[:].rearrange("p (w k n) -> p w k n", w=NW, k=KC)
        wh, wl = a.sb("w_high", [P, NW, KC, D], F16), a.sb("w_low", [P, NW, KC, D], F16)
        cst = a.sb("constants", [P, C_ALL], F32)
        id16 = a.sb("ident16", [P, P], F16)
        bst = a.sb("b_staging", [1, NW, D], F32)
        bias_rows, scale_rows = a.sb("bias_rows", [P, 2, D], F16), a.sb("scale_rows", [P, TOK], F16)
        tops, topa = a.sb("tops", [P, 2 * NW], F32), a.sb("tops_all", [P, 2 * NW], F32)
        tgb = a.sb("top_gb", [P, 2], F32)
        nb, nr = a.sb("n_bound", [P, 1], F32), a.sb("n_rec", [P, 1], F32)
        nscale = a.sb("n_scale", [P, 1], F32)
        wmax, wrec, wscale = (a.sb(n, [P, NW], F32) for n in ("w_max", "w_rec", "w_scale"))
        brow = a.sb("b_row_scale", [P, 2], F32)
        bound, brec, cscale, evac = (a.sb(n, [P, 3], F32) for n in ("bound", "bound_rec", "out_scale", "evac_scale"))
        sscale = a.sb("score_scale", [P, 1], F32)
        tb = a.sb("t_bound", [P, 3], F32)
        tr = a.sb("t_rec", [P, 1], F32)
        ct = a.sb("t_scale", [P, 1], F32)
        tdown = a.sb("t_down", [P, 1], F32)
        d1 = a.sb("mix_down", [P, 1], F32)
        es = a.sb("e_scale", [P, 3], F32)
        sel2 = a.sb("bias_scale", [P, 2], F32)
        biasm = a.sb("e_bias", [P, D], F32)
        grow, b1row, wrow = (a.sb(n, [P, D], F32) for n in ("g1_row", "b1_row", "wr_row"))
        borow, bmrow = a.sb("bo_row", [P, D], F32), a.sb("bm_row", [P, D], F32)
        bvcol, brcol = a.sb("bv_col", [P, KC], F32), a.sb("br_col", [P, 1], F32)
        nhalf = a.sb("minus_half", [P, TILES], F32)

        xin = a.sb("x1_in", [P, TILES, D], F32)
        h0 = a.sb("h0", [P, U, TILES, D], F32)
        n32 = a.sb("normed", [P, TILES, D], F32)
        nh, nl = a.sb("n_high", [P, U, TILES, D], F16), a.sb("n_low", [P, U, TILES, D], F16)
        nT = a.sb("nT", [P, U, KC, 2, TOK], F16)
        KEYS = U * KC * TOK // 2
        kh, kl = (wraw[:, KEYS * n:KEYS * (n + 1)].bitcast(F16).rearrange("p (u k c) -> p u k c", u=U, k=KC)
                  for n in range(2))
        vh, vl = a.sb("v_high", [P, U, TILES, D], F16), a.sb("v_low", [P, U, TILES, D], F16)
        stat = a.sb("stat", [P, TILES, 6], F32)
        mv = a.sb("mean_var", [P, TILES, 2], F32)
        vs, rstd, nmean, nmr = (a.sb(n, [P, TILES], F32) for n in ("var_eps", "rstd", "minus_mean", "minus_mean_rstd"))
        dots = a.sb("dots", [P, D], F32)
        lg = a.sb("logit", [P, TILES], F32)
        lgb = a.sb("logit_br", [P, TILES], F32)
        lgc = a.sb("logit_clamped", [P, U, TILES], F32)
        ex = a.sb("exp_logit", [P, TILES], F32)
        sg = a.sb("score", [P, U, TILES], F32)
        diag = a.sb("logit_diag", [P, TILES, P], F32)
        cmp_ = a.sb("compared", [P, TILES, 2, P], F32)
        rank, keep, sk = (a.sb(n, [P, TILES], F32) for n in ("rank", "keep", "kept_score"))
        acol = a.sb("mix_scale", [P, U, TILES], F32)
        den, rden, wc = (a.sb(n, [P, TILES], F32) for n in ("pool_den", "pool_den_rec", "pool_weight"))
        wg, sgk = a.sb("weight_by_graph", [P, TILES, 2], F32), a.sb("kept_by_graph", [P, TILES, 2], F32)
        gh, gl = a.sb("gather_high", [P, TILES, SLOT], F16), a.sb("gather_low", [P, TILES, SLOT], F16)
        ch, cl = a.sb("scatter_high", [P, TILES * (P + SLOT)], F16), a.sb("scatter_low", [P, TILES * (P + SLOT)], F16)
        cT = a.sb("scatterT", [P, 2, TOK], F16)
        nsh, nsl = a.sb("picked_high", [P, KC, P], F16), a.sb("picked_low", [P, KC, P], F16)
        plh, pll = a.sb("pooled_high", [P, KC, TILES, SLOT], F16), a.sb("pooled_low", [P, KC, TILES, SLOT], F16)
        qh, ql = a.sb("q_high", [P, KC, G4, P], F16), a.sb("q_low", [P, KC, G4, P], F16)
        sx = a.sb("scores", [P, G4, NODES], F32)
        smx, ssm, srec = (a.sb(n, [P, G4], F32) for n in ("row_max", "row_sum", "row_rec"))
        pth, ptl = a.sb("pT_high", [P, TILES, P], F16), a.sb("pT_low", [P, TILES, P], F16)
        c32 = a.sb("ctx", [P, KC, TILES, SLOT], F32)
        cxh, cxl = a.sb("ctx_high", [P, KC, P], F16), a.sb("ctx_low", [P, KC, P], F16)
        e32 = a.sb("rows", [P, D], F32)
        eh, el = a.sb("rows_high", [P, D], F16), a.sb("rows_low", [P, D], F16)
        tT = a.sb("scattered", [P, 2, D], F32)
        mg = a.sb("merged", [P, 2, D], F32)
        hb = a.sb("h_out", [P, TILES, D], F32)

        A = a.ps("turn_ps", [P, 2, TOK], F16)
        ring = [a.ps(f"proj_ps{n}", [P, TOK]) for n in range(2)]
        XY = a.ps("chain_ps", [P, 2, TOK])
        X, Y = XY[:, 0, :], XY[:, 1, :]
        T = a.ps("scatter_ps", [P, TOK])
        MX = [a.ps(f"mix_ps{n}", [P, TOK]) for n in range(2)]

        ident = cst[:, C_ID:C_ID + P]
        ones = cst[:, C_ONE:C_ONE + P]
        same, less = cst[:, C_SAME:C_SAME + P], cst[:, C_LESS:C_LESS + P]
        iota = cst[:, C_IOTA:C_IOTA + SPARE]
        graph = cst[:, C_GRAPH:C_GRAPH + PER_TILE]
        slots = lambda t: t[:, 0:TILES * (P + SLOT)].rearrange("p (t c) -> p t c", c=P + SLOT)
        ch4, cl4 = slots(ch), slots(cl)

        W4 = 4 * PICK

        def own_block(r, n, c):
            blocks = XY[r, :, 0:TILES * KC * W4].rearrange("p y (t c w) -> p t c y w", t=TILES, c=KC)
            to = c32[r, c, :, 0:SPARE].rearrange("p t (g w) -> p t g w", g=PER_TILE)
            return to, blocks[:, :, c, :, PICK * n:PICK * n + PICK]

        sem = a.sem
        qk_in, vom_in = sem("qk_in"), sem("vom_in")
        b_in, gb_in, row_in, col_in, cst_in = (sem(n) for n in ("b_in", "gb_in", "row_in", "col_in", "cst_in"))
        gb_done = sem("gb_done")
        const_set, zeroed = sem("const_set"), sem("zeroed")
        tops_done, topall_done, chain, scales_done, rows_done = (
            sem(n) for n in ("tops_done", "topall_done", "chain", "scales_done", "rows_done"))
        wh_done, wl_done = sem("wh_done"), sem("wl_done")
        x_in = sem("x_in")
        h_st = sem("h_st")
        bn_done, stats_done, pool_chain, rstd_done = (
            sem(n) for n in ("bn_done", "stats_done", "pool_chain", "rstd_done"))
        h0_done, z_done, zg_done, n_done, nh_done, nl_done = (
            sem(n) for n in ("h0_done", "z_done", "zg_done", "n_done", "nh_done", "nl_done"))
        dot_done, score_chain, lgb_done, sexp_done, diag_done = (
            sem(n) for n in ("dot_done", "score_chain", "lgb_done", "sexp_done", "diag_done"))
        nT_done, nTe_done = sem("nT_done"), sem("nTe_done")
        kv_done, kvh_done, kvl_done = sem("kv_done"), sem("kvh_done"), sem("kvl_done")
        r_done, cmp_done, rank_chain, rank_done = (
            sem(n) for n in ("r_done", "cmp_done", "rank_chain", "rank_done"))
        cT_done, cTe_done = sem("cT_done"), sem("cTe_done")
        ns_done, nsh_done, nsl_done = sem("ns_done"), sem("nsh_done"), sem("nsl_done")
        q_done, qh_done, ql_done = sem("q_done"), sem("qh_done"), sem("ql_done")
        s_done, smx_done, ssub_done, exp_done, ssum_done, srec_done, p_done = (
            sem(n) for n in ("s_done", "smx_done", "ssub_done", "exp_done", "ssum_done", "srec_done", "p_done"))
        pt_done, pth_done, ptl_done = sem("pt_done"), sem("pth_done"), sem("ptl_done")
        pv_done, ctx_done, ctx_act_done, cxh_done, cx_done = (
            sem(n) for n in ("pv_done", "ctx_done", "ctx_act_done", "cxh_done", "cx_done"))
        e_done, e32_done, eh_done, el_done = sem("e_done"), sem("e32_done"), sem("eh_done"), sem("el_done")
        m_done, t_done, te_done, mg_done, h_done = (
            sem(n) for n in ("m_done", "t_done", "te_done", "mg_done", "h_done"))
        NKV = KC + TILES

        FIRST, LOOP, LOOPS, LAST = -1, 2, (STEPS - 5) // U, STEPS
        flags = lambda s: (s.b >= 1, 0 <= s.b < STEPS, 0 <= s.b + 1 < STEPS, s.b + 2 < STEPS)

        block = ctx.enter_context(nc.Block())

        @block.sync
        def _(sp):
            for t, r in ((grow, g1), (b1row, b1)):
                sp.dma_start(t[:], row(r).to_broadcast([P, D])).then_inc(gb_in, 16)
            sp.dma_start(xin[:], x1_v[0]).then_inc(x_in, 16)
            for n, w in enumerate((wq, wk, wv, wo, wm)):
                sp.dma_start(wst[:, n], w.rearrange("(k p) n -> p k n", p=P)).then_inc(qk_in if n < 2 else vom_in, 16)
            for n, b in enumerate((bq, bk, bv, bo, bm)):
                sp.dma_start(bst[:, n, :], row(b)).then_inc(b_in, 16)
            sp.dma_start(cst[:], const_in).then_inc(cst_in, 16)
            for t, r in ((wrow, wr), (borow, bo), (bmrow, bm)):
                sp.dma_start(t[:], row(r).to_broadcast([P, D])).then_inc(row_in, 16)
            sp.dma_start(bvcol[:], bv.rearrange("(k p) -> p k", p=P), allow_slow_non_contiguous=True)\
                .then_inc(col_in, 16)
            sp.dma_start(brcol[:], row(br).to_broadcast([P, 1])).then_inc(col_in, 16)

            def body(s):
                if s.b >= 1:
                    sp.wait_ge(h_done, TILES * s.i)
                    sp.dma_start(h_v[s.plus(-1).i], hb[:]).then_inc(h_st, 16)
                if s.b + 3 < STEPS:
                    sp.wait_ge(h0_done, TILES * (s.i + 3))
                    sp.dma_start(xin[:], x1_v[s.i + 3]).then_inc(x_in, 16)

            sp.wait_ge(h0_done, TILES)
            sp.dma_start(xin[:], x1_v[1]).then_inc(x_in, 16)
            run_steps(sp, body, FIRST, LOOP, LOOPS, LAST, U)
            sp.wait_ge(h_st, 16 * STEPS)

        @block.gpsimd
        def _(pool):
            g = nc.gpsimd
            g.memset(tops[:], 0.0).then_inc(const_set, 1)
            g.memset(nhalf[:], -0.5).then_inc(const_set, 1)
            g.memset(scale_rows[:], TOP).then_inc(const_set, 1)
            for t in (bias_rows, qh, ql):
                g.memset(t[:], 0.0).then_inc(zeroed, 1)

            def rstd_of(s, nth):
                n = 2 * s.i + nth
                reach(pool, stats_done, n + 1)
                carry(pool)
                g.tensor_scalar(nmean[:], mv[:, :, 0], -1.0, None, ALU.mult)
                g.tensor_scalar(vs[:], mv[:, :, 1], EPS, 1.0, ALU.add, ALU.mult).then_inc(pool_chain, 1)
                pool.wait_ge(pool_chain, 2 * n + 1)
                if nth:
                    pool.wait_ge(h0_done, TILES * (s.i + 1))
                else:
                    reach(pool, z_done, TILES * s.i)
                g.tensor_tensor(rstd[:], vs[:], nhalf[:], ALU.pow).then_inc(pool_chain, 1)
                pool.wait_ge(pool_chain, 2 * n + 2)
                g.tensor_tensor(nmr[:], nmean[:], rstd[:], ALU.mult).then_inc(rstd_done, 1)

            def times_g1(s):
                for t in range(TILES):
                    pool.wait_ge(z_done, TILES * s.i + t + 1)
                    g.tensor_tensor(n32[:, t, :], n32[:, t, :], grow[:], ALU.mult).then_inc(zg_done, 1)

            def plus_b1(s):
                for t in range(TILES):
                    pool.wait_ge(zg_done, TILES * s.i + t + 1)
                    g.tensor_tensor(n32[:, t, :], n32[:, t, :], b1row[:], ALU.add).then_inc(n_done, 1)

            def low(s):
                for t in range(TILES):
                    pool.wait_ge(nh_done, TILES * s.i + t + 1)
                    g.tensor_tensor(nl[:, s.par, t, :], n32[:, t, :], nh[:, s.par, t, :], ALU.subtract)\
                        .then_inc(nl_done, 1)

            def residual(s, t):
                pool.wait_ge(mg_done, TILES * s.i + t + 1)
                if t == 0:
                    reach(pool, h_st, 16 * s.i)
                g.tensor_tensor(hb[:, t, :], mg[:, t % 2, :], h0[:, s.par, t, :], ALU.add).then_inc(h_done, 1)

            def body(s):
                tail, main, proj, norm = flags(s)
                prev, ah = s.plus(-1), s.plus(2)
                if tail:
                    residual(prev, 0)
                if norm:
                    rstd_of(ah, 0)
                if tail:
                    for t in range(1, TILES):
                        residual(prev, t)
                if norm:
                    rstd_of(ah, 1)
                    times_g1(ah)
                    plus_b1(ah)
                    low(ah)

            first = Step(0, 0, U)
            pool.wait_ge(const_set, 3)
            rstd_of(first, 0)
            for t in (gh, gl, ch, cl, plh, pll, c32):
                g.memset(t[:], 0.0).then_inc(zeroed, 1)
            rstd_of(first, 1)
            pool.wait_ge(gb_done, 1)
            times_g1(first)
            pool.wait_ge(tops_done, NW + 1)
            g.partition_all_reduce(topa[:], tops[:], P, RMAX).then_inc(topall_done, 1)
            plus_b1(first)
            low(first)
            run_steps(pool, body, FIRST, LOOP, LOOPS, LAST, U)

        @block.scalar
        def _(act):
            s_ = nc.scalar
            def first_norm(s, t):
                if t == 0:
                    act.wait_ge(rstd_done, 2 * s.i + 1)
                    reach(act, h_done, TILES * (s.i - 2))
                s_.activation(h0[:, s.par, t, :], xin[:, t, :], ACT.Identity, bias=nmr[:, t:t + 1],
                              scale=rstd[:, t:t + 1]).then_inc(h0_done, 1)

            def second_norm(s, t):
                if t == 0:
                    act.wait_ge(rstd_done, 2 * s.i + 2)
                    reach(act, nl_done, TILES * s.i)
                    reach(act, dot_done, TILES * s.i)
                s_.activation(n32[:, t, :], h0[:, s.par, t, :], ACT.Identity, bias=nmr[:, t:t + 1],
                              scale=rstd[:, t:t + 1]).then_inc(z_done, 1)

            def n_high(s, t):
                act.wait_ge(n_done, TILES * s.i + t + 1)
                s_.copy(nh[:, s.par, t, :], n32[:, t, :]).then_inc(nh_done, 1)

            def score_exp(s):
                act.wait_ge(lgb_done, s.i + 1)
                s_.activation(ex[:], lgb[:], ACT.Exp, scale=-1.0).then_inc(sexp_done, 1)

            def nT_out(s, k):
                act.wait_ge(nT_done, KC * s.i + k + 1)
                s_.copy(nT[:, s.par, k], A[:]).then_inc(nTe_done, 1)

            def kv_high(s, n):
                act.wait_ge(kv_done, NKV * s.i + n + 1)
                ps = ring[n % 2]
                if n < KC:
                    s_.activation(kh[:, s.par, n, :], ps[:], ACT.Copy, scale=evac[:, K:K + 1]).then_inc(kvh_done, 1)
                else:
                    s_.activation(vh[:, s.par, n - KC, :], ps[:, 0:D], ACT.Copy, scale=evac[:, V:V + 1])\
                        .then_inc(kvh_done, 1)

            def picked_high(s):
                act.wait_ge(ns_done, s.i + 1)
                s_.copy(nsh[:].rearrange("p k c -> p (k c)"), X[:, 0:KC * P]).then_inc(nsh_done, 1)

            def scatter_out(s):
                act.wait_ge(cT_done, s.i + 1)
                s_.copy(cT[:], A[:]).then_inc(cTe_done, 1)

            def q_high(s):
                act.wait_ge(q_done, s.i + 1)
                for c in range(KC):
                    for n in range(4):
                        r, hd = slice(HD * n, HD * n + HD), PICK * (4 * c + n)
                        src = Y[r, P * c:P * c + P].rearrange("p (t c) -> p t c", c=SLOT)[:, :, 0:SPARE]\
                            .rearrange("p t (g c) -> p t g c", g=PER_TILE)
                        dst = qh[r, c, :, hd:hd + PICK].rearrange("p (t g) c -> p t g c", g=PER_TILE)
                        last = s_.activation(dst, src, ACT.Copy, scale=evac[r, Q:Q + 1])
                last.then_inc(qh_done, 1)

            def exp(s):
                act.wait_ge(ssub_done, s.i + 1)
                s_.activation(sx[:], sx[:], ACT.Exp, scale=sscale[:, 0:1]).then_inc(exp_done, 1)

            def pT_high(s):
                act.wait_ge(pt_done, s.i + 1)
                s_.copy(pth[:].rearrange("p t c -> p (t c)"), X).then_inc(pth_done, 1)

            def context_rows(s):
                act.wait_ge(pv_done, s.i + 1)
                reach(act, cx_done, s.i)
                for n in (2, 3):
                    r = slice(HD * n, HD * n + HD)
                    for c in range(KC):
                        last = s_.activation(*own_block(r, n, c), ACT.Identity, bias=bvcol[r, c:c + 1])
                last.then_inc(ctx_act_done, 1)

            def scattered(s, t):
                act.wait_ge(t_done, TILES * s.i + t + 1)
                reach(act, mg_done, TILES * s.i + t - 1)
                s_.activation(tT[:, t % 2, :], T[:, 0:D], ACT.Copy, scale=tdown[:, 0:1]).then_inc(te_done, 1)

            def body(s):
                tail, main, proj, norm = flags(s)
                prev, nx, ah = s.plus(-1), s.plus(1), s.plus(2)
                if tail:
                    scattered(prev, 0)
                if proj:
                    nT_out(nx, 0)
                if main:
                    picked_high(s)
                if tail:
                    scattered(prev, 1)
                if proj:
                    nT_out(nx, 1)
                if main:
                    q_high(s)
                if proj:
                    nT_out(nx, 2)
                if tail:
                    scattered(prev, 2)
                if proj:
                    score_exp(nx)
                    kv_high(nx, 0)
                if tail:
                    scattered(prev, 3)
                if proj:
                    kv_high(nx, 1)
                if norm:
                    for t in range(TILES):
                        first_norm(ah, t)
                if proj:
                    kv_high(nx, 2)
                if main:
                    exp(s)
                if proj:
                    kv_high(nx, 3)
                if main:
                    scatter_out(s)
                if norm:
                    second_norm(ah, 0)
                    second_norm(ah, 1)
                if main:
                    pT_high(s)
                if proj:
                    kv_high(nx, 4)
                if norm:
                    second_norm(ah, 2)
                if proj:
                    kv_high(nx, 5)
                if norm:
                    second_norm(ah, 3)
                if main:
                    context_rows(s)
                if norm:
                    for t in range(TILES):
                        n_high(ah, t)
                if proj:
                    kv_high(nx, 6)

            first = Step(0, 0, U)
            for t in range(TILES):
                first_norm(first, t)
            for t in range(TILES):
                second_norm(first, t)
            act.wait_ge(scales_done, 1)
            for n in SPLIT_ORDER:
                if n == SPLIT_ORDER[2]:
                    for t in range(TILES):
                        n_high(first, t)
                s_.activation(wh[:, n].rearrange("p k n -> p (k n)"), wst[:, n].rearrange("p k n -> p (k n)"),
                              ACT.Copy, scale=wscale[:, n:n + 1]).then_inc(wh_done, 1)
            act.wait_ge(zeroed, 10)
            act.wait_ge(rows_done, 1)
            run_steps(act, body, FIRST, LOOP, LOOPS, LAST, U)

        @block.vector
        def _(dve):
            v = nc.vector
            def stats(s, nth):
                n = 2 * s.i + nth
                if nth:
                    dve.wait_ge(h0_done, TILES * (s.i + 1))
                else:
                    dve.wait_ge(x_in, 16 * (s.i + 1))
                reach(dve, stats_done, n)
                for t in range(TILES):
                    last = v.bn_stats(stat[:, t, :], h0[:, s.par, t, :] if nth else xin[:, t, :])
                last.then_inc(bn_done, 1)
                reach(dve, rstd_done, n)
                dve.wait_ge(bn_done, n + 1)
                carry(dve)
                for t in range(TILES):
                    last = v.bn_aggr(mv[:, t, :], stat[:, t, :])
                last.then_inc(stats_done, 1)

            def dot(s):
                for t in range(TILES):
                    dve.wait_ge(n_done, TILES * s.i + t + 1)
                    reach(dve, dot_done, TILES * s.i + t)
                    v.tensor_tensor_reduce(out=dots[:], in0=n32[:, t, :], in1=wrow[:], scale=1.0, scalar=0.0,
                                           op0=ALU.mult, op1=ALU.add, accum_out=lg[:, t:t + 1]).then_inc(dot_done, 1)
                dve.wait_ge(dot_done, TILES * (s.i + 1))
                v.tensor_scalar(lgb[:], lg[:], brcol[:, 0:1], None, ALU.add).then_inc(lgb_done, 1)
                dve.wait_ge(lgb_done, s.i + 1)
                links = Links(dve, score_chain)
                links.start(3 * s.i)
                links.link(v.tensor_scalar(lgc[:, s.par, :], lgb[:], LOGIT_TOP, LOGIT_LOW, ALU.min, ALU.max))
                reach(dve, r_done, s.i)
                v.tensor_tensor(diag[:], ident.unsqueeze(1).to_broadcast([P, TILES, P]),
                                lgc[:, s.par, :].unsqueeze(2).to_broadcast([P, TILES, P]), ALU.mult)\
                    .then_inc(diag_done, 1)
                dve.wait_ge(sexp_done, s.i + 1)
                links.link(v.tensor_scalar(ex[:], ex[:], 1.0, None, ALU.add))
                links.link(v.reciprocal(sg[:, s.par, :], ex[:]))

            def kv_low(s, n):
                dve.wait_ge(kvh_done, NKV * s.i + n + 1)
                ps = ring[n % 2]
                if n < KC:
                    v.scalar_tensor_tensor(out=kl[:, s.par, n, :], in0=ps[:], scalar=evac[:, K:K + 1],
                                           in1=kh[:, s.par, n, :], op0=ALU.mult, op1=ALU.subtract)\
                        .then_inc(kvl_done, 1)
                else:
                    v.scalar_tensor_tensor(out=vl[:, s.par, n - KC, :], in0=ps[:, 0:D], scalar=evac[:, V:V + 1],
                                           in1=vh[:, s.par, n - KC, :], op0=ALU.mult, op1=ALU.subtract)\
                        .then_inc(kvl_done, 1)

            def picked_low(s):
                dve.wait_ge(nsh_done, s.i + 1)
                v.tensor_tensor(nsl[:].rearrange("p k c -> p (k c)"), X[:, 0:KC * P],
                                nsh[:].rearrange("p k c -> p (k c)"), ALU.subtract).then_inc(nsl_done, 1)
                dve.wait_ge(nsl_done, 2 * s.i + 1)
                for to, of in ((plh, nsh), (pll, nsl)):
                    last = v.tensor_copy(to[:, :, :, SPARE:SPARE + PER_TILE],
                                         of[:].rearrange("p k (t c) -> p k t c", c=SLOT)[:, :, :, SPARE:SPARE + PER_TILE])
                last.then_inc(nsl_done, 1)

            def q_low(s):
                dve.wait_ge(qh_done, s.i + 1)
                for c in range(KC):
                    for n in range(4):
                        r, hd = slice(HD * n, HD * n + HD), PICK * (4 * c + n)
                        src = Y[r, P * c:P * c + P].rearrange("p (t c) -> p t c", c=SLOT)[:, :, 0:SPARE]\
                            .rearrange("p t (g c) -> p t g c", g=PER_TILE)
                        at = lambda t: t[r, c, :, hd:hd + PICK].rearrange("p (t g) c -> p t g c", g=PER_TILE)
                        last = v.scalar_tensor_tensor(out=at(ql), in0=src, scalar=evac[r, Q:Q + 1], in1=at(qh),
                                                      op0=ALU.mult, op1=ALU.subtract)
                last.then_inc(ql_done, 1)

            def score_max(s):
                dve.wait_ge(s_done, s.i + 1)
                x3 = X.rearrange("p (g k) -> p g k", g=G4)
                v.tensor_reduce(smx[:], x3, AX_X, ALU.max).then_inc(smx_done, 1)
                dve.wait_ge(smx_done, s.i + 1)
                reach(dve, pt_done, s.i)
                v.tensor_tensor(sx[:], x3, smx[:].unsqueeze(2).to_broadcast([P, G4, NODES]), ALU.subtract)\
                    .then_inc(ssub_done, 1)

            def score_norm(s):
                dve.wait_ge(exp_done, s.i + 1)
                v.tensor_reduce(ssm[:], sx[:], AX_X, ALU.add).then_inc(ssum_done, 1)
                dve.wait_ge(ssum_done, s.i + 1)
                v.reciprocal(srec[:], ssm[:]).then_inc(srec_done, 1)
                dve.wait_ge(srec_done, s.i + 1)
                v.tensor_tensor(sx[:], sx[:], srec[:].unsqueeze(2).to_broadcast([P, G4, NODES]), ALU.mult)\
                    .then_inc(p_done, 1)

            def compare(s):
                dve.wait_ge(r_done, s.i + 1)
                for t in range(TILES):
                    rt = Y[:, P * t:P * t + P]
                    v.scalar_tensor_tensor(out=cmp_[:, t, 0, :], in0=rt, scalar=lgc[:, s.par, t:t + 1], in1=same,
                                           op0=ALU.is_lt, op1=ALU.mult)
                    last = v.scalar_tensor_tensor(out=cmp_[:, t, 1, :], in0=rt, scalar=lgc[:, s.par, t:t + 1],
                                                  in1=less, op0=ALU.is_equal, op1=ALU.mult)
                last.then_inc(cmp_done, 1)

            def lists(s):
                dve.wait_ge(cmp_done, s.i + 1)
                links = Links(dve, rank_chain)
                links.start(5 * s.i)
                ln = links.link
                v.tensor_scalar(den[:], T[:, 0:TILES], 1e-6, None, ALU.add)
                ln(v.tensor_reduce(rank[:], cmp_[:].rearrange("p t a c -> p t (a c)"), AX_X, ALU.add))
                reach(dve, ns_done, s.i)
                reach(dve, cT_done, s.i)
                v.tensor_tensor(gh[:, :, 0:SPARE], iota.unsqueeze(1).to_broadcast([P, TILES, SPARE]),
                                rank[:].unsqueeze(2).to_broadcast([P, TILES, SPARE]), ALU.is_equal)
                v.reciprocal(rden[:], den[:])
                ln(v.tensor_scalar(keep[:], rank[:], float(PICK), None, ALU.is_ge))
                v.tensor_copy(ch4[:, :, 0:SPARE], gh[:, :, 0:SPARE])
                v.tensor_copy(ch4[:, :, SPARE + 2:SPARE + 3], keep[:].unsqueeze(2))
                v.tensor_scalar(acol[:, s.par, :], keep[:], d1[:, 0:1], None, ALU.mult)
                v.tensor_tensor(sk[:], sg[:, s.par, :], keep[:], ALU.mult)
                ln(v.tensor_tensor(wc[:], sg[:, s.par, :], rden[:], ALU.mult))
                g2_ = graph.unsqueeze(1).to_broadcast([P, TILES, PER_TILE])
                two = lambda c: c.unsqueeze(2).to_broadcast([P, TILES, PER_TILE])
                v.tensor_tensor(wg[:], two(wc[:]), g2_, ALU.mult)
                ln(v.tensor_tensor(sgk[:], two(sk[:]), g2_, ALU.mult))
                v.tensor_copy(gh[:, :, SPARE:SPARE + 2], wg[:])
                ln(v.tensor_copy(ch4[:, :, SPARE:SPARE + 2], sgk[:]))
                v.tensor_tensor(gl[:, :, SPARE:SPARE + 2], wg[:], gh[:, :, SPARE:SPARE + 2], ALU.subtract)
                v.tensor_tensor(cl4[:, :, SPARE:SPARE + 2], sgk[:], ch4[:, :, SPARE:SPARE + 2], ALU.subtract)\
                    .then_inc(rank_done, 1)

            def pT_low(s):
                dve.wait_ge(pth_done, s.i + 1)
                v.tensor_tensor(ptl[:].rearrange("p t c -> p (t c)"), X, pth[:].rearrange("p t c -> p (t c)"),
                                ALU.subtract).then_inc(ptl_done, 1)

            def context(s):
                dve.wait_ge(pv_done, s.i + 1)
                for n in (0, 1):
                    r = slice(HD * n, HD * n + HD)
                    for c in range(KC):
                        to, of = own_block(r, n, c)
                        last = v.tensor_scalar(to, of, bvcol[r, c:c + 1], None, ALU.add)
                last.then_inc(ctx_done, 1)
                dve.wait_ge(ctx_done, s.i + 1)
                dve.wait_ge(ctx_act_done, s.i + 1)
                f = c32[:].rearrange("p k t c -> p (k t c)")
                v.tensor_copy(cxh[:].rearrange("p k c -> p (k c)"), f).then_inc(cxh_done, 1)
                dve.wait_ge(cxh_done, s.i + 1)
                v.tensor_tensor(cxl[:].rearrange("p k c -> p (k c)"), f, cxh[:].rearrange("p k c -> p (k c)"),
                                ALU.subtract).then_inc(cx_done, 1)

            def rows(s):
                dve.wait_ge(e_done, s.i + 1)
                v.scalar_tensor_tensor(out=e32[:], in0=X[:, 0:D], scalar=es[:, 2:3], in1=biasm[:],
                                       op0=ALU.mult, op1=ALU.add).then_inc(e32_done, 1)
                dve.wait_ge(e32_done, s.i + 1)
                v.tensor_copy(eh[:], e32[:]).then_inc(eh_done, 1)
                dve.wait_ge(eh_done, s.i + 1)
                v.tensor_tensor(el[:], e32[:], eh[:], ALU.subtract).then_inc(el_done, 1)

            def merge(s, t):
                dve.wait_ge(m_done, TILES * s.i + t + 1)
                dve.wait_ge(te_done, TILES * s.i + t + 1)
                reach(dve, h_done, TILES * s.i + t - 1)
                v.scalar_tensor_tensor(out=mg[:, t % 2, :], in0=MX[t % 2][:, 0:D], scalar=acol[:, s.par, t:t + 1],
                                       in1=tT[:, t % 2, :], op0=ALU.mult, op1=ALU.add).then_inc(mg_done, 1)

            def body(s):
                tail, main, proj, norm = flags(s)
                prev, nx, ah = s.plus(-1), s.plus(1), s.plus(2)
                if tail:
                    merge(prev, 0)
                if main:
                    picked_low(s)
                if tail:
                    merge(prev, 1)
                if norm:
                    stats(ah, 0)
                if proj:
                    dot(nx)
                if main:
                    q_low(s)
                if tail:
                    merge(prev, 2)
                if proj:
                    kv_low(nx, 0)
                if tail:
                    merge(prev, 3)
                if proj:
                    kv_low(nx, 1)
                    compare(nx)
                if main:
                    score_max(s)
                if norm:
                    stats(ah, 1)
                if proj:
                    kv_low(nx, 2)
                if main:
                    score_norm(s)
                if proj:
                    kv_low(nx, 3)
                if main:
                    pT_low(s)
                if proj:
                    kv_low(nx, 4)
                    kv_low(nx, 5)
                if main:
                    context(s)
                if proj:
                    lists(nx)
                if main:
                    rows(s)
                if proj:
                    kv_low(nx, 6)

            link = Links(dve, chain).link
            dve.wait_ge(gb_in, 32)
            v.tensor_reduce(tgb[:, 0:1], grow[:], AX_X, ALU.max, apply_absolute_value=True)
            link(v.tensor_reduce(tgb[:, 1:2], b1row[:], AX_X, ALU.max, apply_absolute_value=True))
            link(v.scalar_tensor_tensor(out=nb[:], in0=tgb[:, 0:1], scalar=Z_MAX, in1=tgb[:, 1:2],
                                        op0=ALU.mult, op1=ALU.add))
            link(v.tensor_scalar(nb[:], nb[:], TINY, None, ALU.max))
            link(v.reciprocal(nr[:], nb[:]))
            link(v.tensor_scalar(nscale[:], nr[:], TOP, None, ALU.mult))
            v.tensor_scalar(grow[:], grow[:], nscale[:, 0:1], None, ALU.mult)
            v.tensor_scalar(b1row[:], b1row[:], nscale[:, 0:1], None, ALU.mult).then_inc(gb_done, 1)
            first = Step(0, 0, U)
            stats(first, 0)
            dve.wait_ge(const_set, 1)
            for n in range(NW):
                if n == 0:
                    dve.wait_ge(qk_in, 32)
                if n == 2:
                    stats(first, 1)
                    dve.wait_ge(vom_in, 48)
                v.tensor_reduce(tops[:, n:n + 1], wst[:, n].rearrange("p k n -> p (k n)"), AX_X, ALU.max,
                                apply_absolute_value=True).then_inc(tops_done, 1)
            dve.wait_ge(b_in, 16 * NW)
            v.tensor_reduce(tops[0:1, NW:2 * NW], bst[:], AX_X, ALU.max, apply_absolute_value=True)\
                .then_inc(tops_done, 1)
            dve.wait_ge(topall_done, 1)
            tw, tbias = topa[:, 0:NW], topa[:, NW:2 * NW]
            v.tensor_copy(wmax[:, 2:NW], tw[:, 2:NW])
            link(v.scalar_tensor_tensor(out=wmax[:, 0:2], in0=tbias[:, 0:2], scalar=nr[:, 0:1], in1=tw[:, 0:2],
                                        op0=ALU.mult, op1=ALU.max))
            link(v.tensor_scalar(wmax[:], wmax[:], TINY, None, ALU.max))
            link(v.reciprocal(wrec[:], wmax[:]))
            v.tensor_scalar(wscale[:], wrec[:], W_TOP, None, ALU.mult).then_inc(scales_done, 1)
            dve.wait_ge(cst_in, 16)
            dve.wait_ge(row_in, 48)
            dve.wait_ge(col_in, 32)
            dve.wait_ge(zeroed, 10)
            v.tensor_copy(id16[:], ident)
            v.tensor_copy(ssm[:], cst[:, 0:G4])
            v.tensor_scalar(wrow[:], wrow[:], nb[:, 0:1], 1.0 / TOP, ALU.mult, ALU.mult)
            v.tensor_scalar(brow[:], wrec[:, 0:2], nr[:, 0:1], W_TOP, ALU.mult, ALU.mult)
            v.tensor_scalar(d1[:], nb[:], wmax[:, M:M + 1], 1.0 / (TOP * W_TOP), ALU.mult, ALU.mult)
            v.tensor_scalar(tb[:, 1:2], tw[:, M:M + 1], nb[:, 0:1], float(D), ALU.mult, ALU.mult)
            v.tensor_tensor(tb[:, 2:3], tbias[:, O:O + 1], tbias[:, M:M + 1], ALU.add)
            link(v.tensor_scalar(bound[:], tw[:, 0:3], nb[:, 0:1], float(D), ALU.mult, ALU.mult))
            for n in range(2):
                v.tensor_scalar(bias_rows[0:1, n, :], bst[:, n, :], brow[0:1, n:n + 1], None, ALU.mult)
            link(v.tensor_tensor(bound[:], bound[:], tbias[:, 0:3], ALU.add))
            for n in range(2):
                v.scalar_tensor_tensor(out=bias_rows[32:33, n, :], in0=bst[:, n, :], scalar=brow[0:1, n:n + 1],
                                       in1=bias_rows[0:1, n, :], op0=ALU.mult, op1=ALU.subtract)
            link(v.tensor_scalar(bound[:], bound[:], TINY, None, ALU.max))
            v.reciprocal(brec[:], bound[:])
            v.tensor_scalar(tb[:, 0:1], tw[:, O:O + 1], bound[:, V:V + 1], float(D), ALU.mult, ALU.mult)
            v.scalar_tensor_tensor(out=sscale[:], in0=bound[:, Q:Q + 1], scalar=RSQRT_HD / (TOP * TOP),
                                   in1=bound[:, K:K + 1], op0=ALU.mult, op1=ALU.mult)
            link(v.tensor_scalar(es[:, 0:1], bound[:, V:V + 1], wmax[:, O:O + 1], 1.0 / (TOP * W_TOP),
                                 ALU.mult, ALU.mult))
            v.tensor_scalar(cscale[:], brec[:], TOP, None, ALU.mult)
            v.tensor_scalar(evac[:], brec[:], nb[:, 0:1], 1.0 / W_TOP, ALU.mult, ALU.mult)
            v.tensor_tensor(tb[:, 2:3], tb[:, 2:3], tb[:, 0:1], ALU.add)
            link(v.tensor_tensor(es[:, 0:1], es[:, 0:1], d1[:], ALU.subtract))
            v.tensor_tensor(evac[:], evac[:], wmax[:, 0:3], ALU.mult)
            v.tensor_tensor(tb[:, 2:3], tb[:, 2:3], tb[:, 1:2], ALU.add)
            v.tensor_scalar(bvcol[:], bvcol[:], cscale[:, V:V + 1], None, ALU.mult)
            link(v.scalar_tensor_tensor(out=es[:, 1:2], in0=es[:, 0:1], scalar=cst[:, C_ATT:C_ATT + 1], in1=d1[:],
                                        op0=ALU.mult, op1=ALU.add))
            link(v.tensor_scalar(tb[:, 2:3], tb[:, 2:3], TINY, None, ALU.max))
            v.tensor_scalar(tdown[:], tb[:, 2:3], 1.0 / TOP, None, ALU.mult)
            link(v.reciprocal(tr[:], tb[:, 2:3]))
            link(v.tensor_scalar(ct[:], tr[:], TOP, None, ALU.mult))
            v.tensor_tensor(es[:, 2:3], es[:, 1:2], ct[:], ALU.mult)
            link(v.tensor_scalar(sel2[:], cst[:, C_ATT:C_ATT + 2], ct[:, 0:1], None, ALU.mult))
            link(v.tensor_scalar(biasm[:], borow[:], sel2[:, 0:1], None, ALU.mult))
            v.scalar_tensor_tensor(out=biasm[:], in0=bmrow[:], scalar=sel2[:, 1:2], in1=biasm[:],
                                   op0=ALU.mult, op1=ALU.add).then_inc(rows_done, 1)
            for n in SPLIT_ORDER:
                dve.wait_ge(wh_done, SPLIT_ORDER.index(n) + 1)
                v.scalar_tensor_tensor(out=wl[:, n].rearrange("p k n -> p (k n)"),
                                       in0=wst[:, n].rearrange("p k n -> p (k n)"), scalar=wscale[:, n:n + 1],
                                       in1=wh[:, n].rearrange("p k n -> p (k n)"),
                                       op0=ALU.mult, op1=ALU.subtract).then_inc(wl_done, 1)
            dve.wait_ge(const_set, 3)
            run_steps(dve, body, FIRST, LOOP, LOOPS, LAST, U)

        @block.tensor
        def _(pe):
            mm = nc.tensor.matmul
            pe.wait_ge(rows_done, 1)

            def three(out, sh, sl, mh, ml, first, last):
                mm(out, sh, mh, start=first, stop=False)
                mm(out, sl, mh, start=False, stop=False)
                return mm(out, sh, ml, start=False, stop=last)

            def picked(s):
                pe.wait_ge(rank_done, s.i + 1)
                reach(pe, e32_done, s.i)
                for t in range(TILES):
                    for k in range(KC):
                        f = slice(P * k, P * k + P)
                        out = X[:, P * k + SLOT * t:P * k + SLOT * t + SLOT]
                        last = three(out, nh[:, s.par, t, f], nl[:, s.par, t, f], gh[:, t, :], gl[:, t, :], True, True)
                last.then_inc(ns_done, 1)

            def turn_scatter(s):
                reach(pe, nTe_done, KC * (s.i + 2 if s.b + 1 < STEPS else s.i + 1))
                for n, c in enumerate((ch, cl)):
                    for t in range(TILES):
                        last = nc.tensor.transpose(A[:, n, P * t:P * t + P], c[:, P * t:P * t + P], id16[:])
                last.then_inc(cT_done, 1)

            def nT_of(s, k):
                if k == 0:
                    pe.wait_ge(nl_done, TILES * (s.i + 1))
                    reach(pe, cTe_done, s.i - 1)
                reach(pe, nTe_done, KC * s.i + k)
                for n, c in enumerate((nh, nl)):
                    for t in range(TILES):
                        last = nc.tensor.transpose(A[:, n, P * t:P * t + P], c[:, s.par, t, P * k:P * k + P], id16[:])
                last.then_inc(nT_done, 1)

            def kv(s, n):
                if s.b == 0 and n in (0, KC):
                    pe.wait_ge(wl_done, 1 if n == 0 else 2)
                reach(pe, kvl_done, NKV * s.i + max(n - 1, 0))
                ps = ring[n % 2]
                if n < KC:
                    c = slice(P * n, P * n + P)
                    mm(ps[:], bias_rows[:, K, c], scale_rows[:], start=True, stop=False)
                    for k in range(KC):
                        if n == 0:
                            pe.wait_ge(nTe_done, KC * s.i + k + 1)
                        last = three(ps[:], wh[:, K, k, c], wl[:, K, k, c], nT[:, s.par, k, 0, :],
                                     nT[:, s.par, k, 1, :], False, k == KC - 1)
                else:
                    c = slice(P * (n - KC), P * (n - KC) + P)
                    for k in range(KC):
                        last = three(ps[:, 0:D], nT[:, s.par, k, 0, c], nT[:, s.par, k, 1, c], wh[:, V, k, :],
                                     wl[:, V, k, :], k == 0, k == KC - 1)
                last.then_inc(kv_done, 1)

            def queries(s):
                if s.b == 0:
                    pe.wait_ge(wl_done, NW)
                pe.wait_ge(nsl_done, 2 * s.i + 1)
                reach(pe, ctx_done, s.i)
                reach(pe, ctx_act_done, s.i)
                for n in range(KC):
                    c = slice(P * n, P * n + P)
                    mm(Y[:, c], bias_rows[:, Q, c], scale_rows[:, 0:P], start=True, stop=False)
                    for k in range(KC):
                        last = three(Y[:, c], wh[:, Q, k, c], wl[:, Q, k, c], nsh[:, k, :], nsl[:, k, :],
                                     False, k == KC - 1)
                last.then_inc(q_done, 1)

            def scores(s):
                pe.wait_ge(ql_done, s.i + 1)
                pe.wait_ge(nsl_done, 2 * s.i + 2)
                pe.wait_ge(kvl_done, NKV * (s.i + 1))
                for g in range(G4):
                    c = slice(NODES * g, NODES * g + NODES)
                    for k in range(KC):
                        last = three(X[:, c], qh[:, k, g, :], ql[:, k, g, :], kh[:, s.par, k, c], kl[:, s.par, k, c],
                                     k == 0, k == KC - 1)
                last.then_inc(s_done, 1)

            def spread(s):
                pe.wait_ge(diag_done, s.i + 1)
                pe.wait_ge(score_chain, 3 * (s.i + 1))
                reach(pe, ql_done, s.i)
                reach(pe, te_done, TILES * (s.i - 1))
                mm(T[:, 0:TILES], same, sg[:, s.par, :], start=True, stop=True)
                mm(Y, ones, diag[:].rearrange("p t c -> p (t c)"), start=True, stop=True).then_inc(r_done, 1)

            def turn_p(s):
                pe.wait_ge(p_done, s.i + 1)
                f = sx[:].rearrange("p g k -> p (g k)")
                for t in range(TILES):
                    last = nc.tensor.transpose(X[:, P * t:P * t + P], f[:, P * t:P * t + P], ident)
                last.then_inc(pt_done, 1)

            def attend(s):
                pe.wait_ge(ptl_done, s.i + 1)
                if s.b + 1 < STEPS:
                    pe.wait_ge(cmp_done, s.i + 2)
                for g in range(G4):
                    t, r = g // PER_TILE, slice(NODES * (g % PER_TILE), NODES * (g % PER_TILE) + NODES)
                    for c in range(KC):
                        at = W4 * (KC * t + c)
                        out = XY[:, g % PER_TILE, at:at + W4]
                        f = slice(P * c, P * c + P)
                        q = slice(W4 * c, W4 * c + W4)
                        last = three(out, vh[r, s.par, t, f], vl[r, s.par, t, f], pth[r, t, q], ptl[r, t, q], True, True)
                last.then_inc(pv_done, 1)

            def make_rows(s):
                pe.wait_ge(cx_done, s.i + 1)
                pl = lambda t, k: t[:, k].rearrange("p t c -> p (t c)")
                for k in range(KC):
                    three(X[:, 0:D], cxh[:, k, :], cxl[:, k, :], wh[:, O, k, :], wl[:, O, k, :], k == 0, False)
                for k in range(KC):
                    last = three(X[:, 0:D], pl(plh, k), pl(pll, k), wh[:, M, k, :], wl[:, M, k, :],
                                 False, k == KC - 1)
                last.then_inc(e_done, 1)

            def mix(s, t):
                reach(pe, mg_done, TILES * s.i + t - 1)
                c = slice(P * t, P * t + P)
                for k in range(KC):
                    last = three(MX[t % 2][:, 0:D], nT[:, s.par, k, 0, c], nT[:, s.par, k, 1, c], wh[:, M, k, :],
                                 wl[:, M, k, :], k == 0, k == KC - 1)
                last.then_inc(m_done, 1)

            def scatter(s, t):
                if t == 0:
                    pe.wait_ge(el_done, s.i + 1)
                    pe.wait_ge(cTe_done, s.i + 1)
                    if s.b + 1 < STEPS:
                        pe.wait_ge(rank_done, s.i + 2)
                reach(pe, te_done, TILES * s.i + t)
                c = slice(P * t, P * t + P)
                three(T[:, 0:D], cT[:, 0, c], cT[:, 1, c], eh[:], el[:], True, True).then_inc(t_done, 1)

            def body(s):
                tail, main, proj, norm = flags(s)
                prev, nx = s.plus(-1), s.plus(1)
                if tail:
                    scatter(prev, 0)
                if proj:
                    nT_of(nx, 0)
                if main:
                    picked(s)
                if tail:
                    scatter(prev, 1)
                if proj:
                    nT_of(nx, 1)
                if main:
                    queries(s)
                if proj:
                    nT_of(nx, 2)
                if tail:
                    scatter(prev, 2)
                    mix(prev, 2)
                if proj:
                    kv(nx, 0)
                if tail:
                    scatter(prev, 3)
                    mix(prev, 3)
                if proj:
                    kv(nx, 1)
                    spread(nx)
                if main:
                    scores(s)
                if proj:
                    kv(nx, 2)
                if main:
                    turn_scatter(s)
                if proj:
                    kv(nx, 3)
                    kv(nx, 4)
                if main:
                    turn_p(s)
                if proj:
                    kv(nx, 5)
                if main:
                    attend(s)
                if proj:
                    kv(nx, 6)
                if main:
                    mix(s, 0)
                    make_rows(s)
                    mix(s, 1)

            run_steps(pe, body, FIRST, LOOP, LOOPS, LAST, U)


def build(nc, x, adj, gnn, attention, mlp, const_in, out):
    x1 = nc.dram_tensor("x1_dram", (GRAPHS, NODES, D), F32, kind="Internal").ap()
    h = nc.dram_tensor("h_dram", (GRAPHS, NODES, D), F32, kind="Internal").ap()
    gnn_phase(nc, x, adj, *gnn, x1)
    mix_phase(nc, x1, *attention, const_in, h)
    mlp_phase(nc, h, x1, *mlp, const_in[:, C_ID:C_ID + P], out)


GNN_INS = ["Wq", "bq", "Wk", "bk", "Wv", "bv", "beta"]
ATTENTION_INS = ["g1", "b1", "Wr", "br", "Wq", "bq", "Wk", "bk", "Wv", "bv", "Wo", "bo", "Wm", "bm"]
MLP_INS = ["g2", "b2", "W1", "bf1", "W2", "bf2"]


def kernel(**inputs):
    import numpy as np
    import concourse.bacc as bacc
    from concourse.bass_utils import run_bass_kernel_spmd

    nc = bacc.Bacc("TRN2", target_bir_lowering=False, num_devices=1)
    arrays = {}

    def take(name, array):
        array = np.ascontiguousarray(np.atleast_1d(array))
        arrays[f"in_{name}_dram"] = array
        return nc.dram_tensor(f"in_{name}_dram", array.shape, mybir.dt.from_np(array.dtype),
                              kind="ExternalInput").ap()

    x, adj = take("x", inputs["x"]), take("adj", inputs["adj"])
    gnn = [take(f"L0_gnn_{n}", inputs[f"L0_gnn_{n}"]) for n in GNN_INS]
    attention, mlp = ([take(f"L0_ffn_{n}", inputs[f"L0_ffn_{n}"]) for n in names] for names in (ATTENTION_INS, MLP_INS))
    const_in = take("constants", constants())
    out = nc.dram_tensor("out_0_dram", (GRAPHS, NODES, D), F32, kind="ExternalOutput").ap()
    build(nc, x, adj, gnn, attention, mlp, const_in, out)
    result = run_bass_kernel_spmd(nc, [arrays], core_ids=[0])
    return result.results[0]["out_0_dram"]
```
